# Optimizing a Trainium2 kernel written in Bass

```python
import numpy as np
import jax
import jax.numpy as jnp

def _softmax(x, axis=-1):
    return jax.nn.softmax(x, axis=axis)

def _gelu(x):
    return jax.nn.gelu(x, approximate=True)

def _silu(x):
    return jax.nn.silu(x)

def _sigmoid(x):
    return jax.nn.sigmoid(x)

def _layernorm(x, axis=-1, eps=1e-05):
    m = jnp.mean(x, axis=axis, keepdims=True)
    v = jnp.var(x, axis=axis, keepdims=True)
    return (x - m) / jnp.sqrt(v + eps)

def _scatter_add(tgt, idx, src, axis=0):
    return tgt.at[idx].add(src)

def _segment_sum(src, seg, n):
    return jax.ops.segment_sum(src, seg, n)
kernel_name = 'mk_adj_preln_d4_adj_r2_a55848'

def setup_inputs(seed: int=0):
    np.random.seed(seed)
    _w = jnp.asarray

    def _rec_inputs():
        import jax
        import jax.numpy as jnp
        _gk = jax.random.key(seed)
        x = -0.000929 + 1 * jax.random.normal(jax.random.fold_in(_gk, 1), (8, 1024, 64), jnp.float32)
        _w = (1.0 + jnp.arange(1024, dtype=jnp.float32)) ** (-0.5)
        _w = _w / _w.mean()
        _pij = jnp.clip(0.00390625 * _w[:, None] * _w[None, :], 0.0, 1.0)
        _a = jax.random.uniform(jax.random.fold_in(_gk, 2), (1024, 1024)) < _pij
        _a = jnp.logical_or(_a, jnp.eye(1024, dtype=bool))
        _af = _a.astype(jnp.float32)
        adj = _af
        return (x, adj)
    x, adj = _rec_inputs()

    def _L0_gnn_setup():
        import jax, jax.numpy as jnp
        import numpy as np
        NEG = -1000000000.0
        key = jax.random.key(seed)
        ks = jax.random.split(key, 14)
        B, N, E, NF, NH = (8, 1024, 64, 64, 64)
        x = jax.random.normal(ks[0], (B, N, NF), dtype=jnp.float32)
        base = jax.nn.one_hot(jax.random.randint(ks[1], (N,), 0, E), E, dtype=jnp.float32)
        extra = (jax.random.uniform(ks[2], (N, E)) < 0.03).astype(jnp.float32)
        H = jnp.clip(base + extra, 0.0, 1.0)
        adj = (jax.random.uniform(ks[3], (N, N)) < 0.01).astype(jnp.float32)
        adj = jnp.clip(adj + jnp.eye(N, dtype=jnp.float32), 0.0, 1.0)
        s_in = 1.0 / np.sqrt(NF)
        s_h = 1.0 / np.sqrt(NH)
        W = jax.random.normal(ks[4], (NF, NH), dtype=jnp.float32) * s_in
        W_ind = jax.random.normal(ks[5], (NF, NH), dtype=jnp.float32) * s_in
        a_node = jax.random.normal(ks[6], (NH,), dtype=jnp.float32) * s_h
        a_gn = jax.random.normal(ks[7], (NH,), dtype=jnp.float32) * s_h
        a_ge = jax.random.normal(ks[8], (NH,), dtype=jnp.float32) * s_h
        fcW = jax.random.normal(ks[9], (NH, 2 * NH), dtype=jnp.float32) * s_h
        fcb = jnp.zeros((2 * NH,), dtype=jnp.float32)
        av = jax.random.normal(ks[10], (2 * NH,), dtype=jnp.float32) / np.sqrt(2 * NH)
        return {'x': x, 'H': H, 'adj': adj, 'nhid': NH, 'W': W, 'W_ind': W_ind, 'a_node': a_node, 'a_gn': a_gn, 'a_ge': a_ge, 'fcW': fcW, 'fcb': fcb, 'av': av}
    _L0_gnn_all = _L0_gnn_setup()
    _L0_gnn_in = {k: v for k, v in _L0_gnn_all.items() if k in ('H', 'W', 'W_ind', 'a_node', 'a_gn', 'a_ge', 'fcW', 'fcb', 'av')}
    del _L0_gnn_all

    def _L1_gnn_setup():
        import jax, jax.numpy as jnp
        import numpy as np
        NEG_INF = -1e+16

        def gat_layer(x, graph, W, b):
            h = x @ W
            s = jnp.einsum('bnd,bmd->bnm', h, h) * graph
            s = jnp.where(s == 0.0, NEG_INF, s)
            a = jax.nn.softmax(s, axis=2)
            return jnp.einsum('bnm,bmd->bnd', a, h) + b
        key = jax.random.key(seed)
        k1, k2, k3, k4, k5, k6 = jax.random.split(key, 6)
        B, N, C_IN, HID, HEADS, C_OUT = (16, 512, 64, 128, 8, 64)
        flow_x = jax.random.normal(k1, (B, N, C_IN), dtype=jnp.float32)
        graph = jax.random.randint(k2, (N, N), 0, 2).astype(jnp.float32)
        Wh = jax.random.normal(k3, (HEADS, C_IN, HID), dtype=jnp.float32)
        bh = jax.random.normal(k4, (HEADS, HID), dtype=jnp.float32)
        W_out = jax.random.normal(k5, (HID * HEADS, C_OUT), dtype=jnp.float32)
        b_out = jax.random.normal(k6, (C_OUT,), dtype=jnp.float32)
        return {'flow_x': flow_x, 'graph': graph, 'Wh': Wh, 'bh': bh, 'W_out': W_out, 'b_out': b_out}
    _L1_gnn_all = _L1_gnn_setup()
    _L1_gnn_in = {k: v for k, v in _L1_gnn_all.items() if k in ('Wh', 'bh', 'W_out', 'b_out')}
    del _L1_gnn_all

    def _L2_gnn_setup():
        import jax, jax.numpy as jnp
        import numpy as np
        ALPHA = 0.2
        key = jax.random.key(seed)
        k1, k2, k3, k4 = jax.random.split(key, 4)
        B, N, Din, Dout = (8, 1024, 64, 64)
        x = jax.random.normal(k1, (B, N, Din), dtype=jnp.float32)
        adj = (jax.random.uniform(k2, (N, N)) < 0.05).astype(jnp.float32)
        lim_w = float(np.sqrt(6.0 / (Din + Dout)))
        weight = jax.random.uniform(k3, (Din, Dout), dtype=jnp.float32, minval=-lim_w, maxval=lim_w)
        lim_a = float(np.sqrt(6.0 / (2 * Dout + 1)))
        a = jax.random.uniform(k4, (2 * Dout, 1), dtype=jnp.float32, minval=-lim_a, maxval=lim_a)
        bias = jnp.zeros((Dout,), dtype=jnp.float32)
        return {'x': x, 'adj': adj, 'weight': weight, 'a': a, 'bias': bias}
    _L2_gnn_all = _L2_gnn_setup()
    _L2_gnn_in = {k: v for k, v in _L2_gnn_all.items() if k in ('weight', 'a', 'bias')}
    del _L2_gnn_all

    def _L3_gnn_setup():
        import jax, jax.numpy as jnp
        import numpy as np
        B, N, F_IN, F_OUT = (8, 1024, 64, 64)
        ALPHA = 0.2
        NEG = -9000000000000000.0
        key = jax.random.key(seed)
        k1, k2, k3, k4 = jax.random.split(key, 4)
        h = jax.random.normal(k1, (B, N, F_IN), dtype=jnp.float32)
        adj = jax.random.randint(k2, (N, N), 0, 2).astype(jnp.float32)
        W = jax.random.normal(k3, (F_OUT, F_IN), dtype=jnp.float32) * 0.05
        a = jax.random.normal(k4, (2 * F_OUT,), dtype=jnp.float32) * 0.05
        return {'h': h, 'adj': adj, 'W': W, 'a': a}
    _L3_gnn_all = _L3_gnn_setup()
    _L3_gnn_in = {k: v for k, v in _L3_gnn_all.items() if k in ('W', 'a')}
    del _L3_gnn_all
    return {'x': x, 'adj': adj, 'L0_gnn_H': _L0_gnn_in['H'], 'L0_gnn_W': _L0_gnn_in['W'], 'L0_gnn_W_ind': _L0_gnn_in['W_ind'], 'L0_gnn_a_node': _L0_gnn_in['a_node'], 'L0_gnn_a_gn': _L0_gnn_in['a_gn'], 'L0_gnn_a_ge': _L0_gnn_in['a_ge'], 'L0_gnn_fcW': _L0_gnn_in['fcW'], 'L0_gnn_fcb': _L0_gnn_in['fcb'], 'L0_gnn_av': _L0_gnn_in['av'], 'L1_gnn_Wh': _L1_gnn_in['Wh'], 'L1_gnn_bh': _L1_gnn_in['bh'], 'L1_gnn_W_out': _L1_gnn_in['W_out'], 'L1_gnn_b_out': _L1_gnn_in['b_out'], 'L2_gnn_weight': _L2_gnn_in['weight'], 'L2_gnn_a': _L2_gnn_in['a'], 'L2_gnn_bias': _L2_gnn_in['bias'], 'L3_gnn_W': _L3_gnn_in['W'], 'L3_gnn_a': _L3_gnn_in['a']}

def reference(x, adj, L0_gnn_H, L0_gnn_W, L0_gnn_W_ind, L0_gnn_a_node, L0_gnn_a_gn, L0_gnn_a_ge, L0_gnn_fcW, L0_gnn_fcb, L0_gnn_av, L1_gnn_Wh, L1_gnn_bh, L1_gnn_W_out, L1_gnn_b_out, L2_gnn_weight, L2_gnn_a, L2_gnn_bias, L3_gnn_W, L3_gnn_a):
    import jax
    import jax.numpy as jnp

    def _L0_gnn_ref(x, H, adj, nhid, W, W_ind, a_node, a_gn, a_ge, fcW, fcb, av):
        import jax, jax.numpy as jnp
        import numpy as np
        NEG = -1000000000.0
        h = x @ W
        maskEN = H.T
        s = jax.nn.leaky_relu(h @ a_node, 0.2)
        logits = jnp.where(maskEN[None, :, :] > 0, s[:, None, :], NEG)
        alpha = jax.nn.softmax(logits, axis=-1)
        agg = jnp.einsum('ben,bnf->bef', alpha, h)
        beta = jax.nn.sigmoid((h @ a_gn)[:, None, :] + (agg @ a_ge)[:, :, None])
        all_he = beta[..., None] * h[:, None, :, :] + (1.0 - beta[..., None]) * agg[:, :, None, :]
        deg = jnp.maximum(adj.sum(-1), 1.0)[:, None]
        industry = jnp.einsum('nm,bmf->bnf', adj / deg, x @ W_ind)
        all_he = jax.nn.elu(all_he)
        he = jax.nn.elu(agg)

        def attn_scores(f):
            return jnp.tanh(f @ fcW + fcb) @ av
        se = attn_scores(he)
        logits2 = jnp.where(H[None, :, :] > 0, se[:, None, :], NEG)
        coefs1 = jax.nn.softmax(logits2, axis=-1)
        g = jnp.einsum('bne,benf->bnf', coefs1, all_he)
        pair = jnp.stack([industry, g], axis=2)
        coefs2 = jax.nn.softmax(attn_scores(pair), axis=-1)
        out = jnp.einsum('bnk,bnkf->bnf', coefs2, pair)
        return out

    def _L1_gnn_ref(flow_x, graph, Wh, bh, W_out, b_out):
        import jax, jax.numpy as jnp
        import numpy as np
        NEG_INF = -1e+16

        def gat_layer(x, graph, W, b):
            h = x @ W
            s = jnp.einsum('bnd,bmd->bnm', h, h) * graph
            s = jnp.where(s == 0.0, NEG_INF, s)
            a = jax.nn.softmax(s, axis=2)
            return jnp.einsum('bnm,bmd->bnd', a, h) + b
        heads = jax.vmap(lambda W, b: gat_layer(flow_x, graph, W, b))(Wh, bh)
        H, B, N, D = heads.shape
        cat = jnp.moveaxis(heads, 0, 2).reshape(B, N, H * D)
        x = jax.nn.leaky_relu(cat, negative_slope=0.01)
        out = gat_layer(x, graph, W_out, b_out)
        return jax.nn.leaky_relu(out, negative_slope=0.01)

    def _L2_gnn_ref(x, adj, weight, a, bias):
        import jax, jax.numpy as jnp
        import numpy as np
        ALPHA = 0.2
        N = adj.shape[0]
        adj = adj.at[jnp.diag_indices(N)].set(1.0)
        h = jnp.einsum('bni,io->bno', x, weight)
        D = h.shape[-1]
        e_src = h @ a[:D, 0]
        e_dst = h @ a[D:, 0]
        e = jax.nn.leaky_relu(e_src[:, :, None] + e_dst[:, None, :], negative_slope=ALPHA)
        e = adj[None, :, :] * e
        attention = jax.nn.softmax(e, axis=-1)
        h_prime = jnp.einsum('bij,bjd->bid', attention, h)
        return h_prime + bias

    def _L3_gnn_ref(h, adj, W, a):
        import jax, jax.numpy as jnp
        import numpy as np
        B, N, F_IN, F_OUT = (8, 1024, 64, 64)
        ALPHA = 0.2
        NEG = -9000000000000000.0
        Wh = jnp.einsum('bnf,of->bno', h, W)
        e1 = Wh @ a[:F_OUT]
        e2 = Wh @ a[F_OUT:]
        e = jax.nn.leaky_relu(e1[:, :, None] + e2[:, None, :], negative_slope=ALPHA)
        att = jnp.where(adj[None, :, :] > 0, e, NEG)
        att = jax.nn.softmax(att, axis=-1)
        h_prime = jnp.einsum('bij,bjo->bio', att, Wh)
        return jax.nn.elu(h_prime)
    h = jnp.maximum(_layernorm(x, axis=-1), 0.0)
    x = x + _L0_gnn_ref(h, L0_gnn_H, adj, 64, L0_gnn_W, L0_gnn_W_ind, L0_gnn_a_node, L0_gnn_a_gn, L0_gnn_a_ge, L0_gnn_fcW, L0_gnn_fcb, L0_gnn_av)
    h = jnp.maximum(_layernorm(x, axis=-1), 0.0)
    x = x + _L1_gnn_ref(h, adj, L1_gnn_Wh, L1_gnn_bh, L1_gnn_W_out, L1_gnn_b_out)
    h = jnp.maximum(_layernorm(x, axis=-1), 0.0)
    x = x + _L2_gnn_ref(h, adj, L2_gnn_weight, L2_gnn_a, L2_gnn_bias)
    h = jnp.maximum(_layernorm(x, axis=-1), 0.0)
    x = x + _L3_gnn_ref(h, adj, L3_gnn_W, L3_gnn_a)
    return x

_drawn_inputs = setup_inputs


def setup_inputs(seed=0):
    import zlib

    import numpy as np

    out = dict(_drawn_inputs(seed))
    spreads = {'L0_gnn_fcb': (0.0, 2.0), 'L2_gnn_bias': (0.0, 2.0)}
    factors = {'L0_gnn_H': 3.639,
     'L0_gnn_a_node': 3.989,
     'L1_gnn_b_out': 6.54,
     'L2_gnn_weight': 8.0,
     'L2_gnn_a': 8.0,
     'L3_gnn_W': 25.022,
     'L3_gnn_a': 64.0}
    for name, (base, spread) in spreads.items():
        noise = np.random.default_rng([zlib.crc32(name.encode()), seed]).standard_normal(out[name].shape)
        drawn = base * np.exp(spread * noise) if base else spread * noise
        out[name] = jnp.asarray(drawn.astype(out[name].dtype))
    for name, factor in factors.items():
        out[name] = (out[name] * factor).astype(out[name].dtype)
    return out
```

```python
from contextlib import ExitStack

import concourse.bass as bass
from concourse import mybir

ALU = mybir.AluOpType
ACT = mybir.ActivationFunctionType
AX = mybir.AxisListType
F32 = mybir.dt.float32
F32R = mybir.dt.float32r
BF16 = mybir.dt.bfloat16

P = 128
N = 1024
F = 64
NT = N // P
HALF = 512
TPH = HALF // P
HEADS = 8
HID = 128
MASKED = -1.0e16
EPS = 1e-5


def layer_norm_relu(nc, ctx, B, x, hx, name):
    rows = B * NT
    stat = ctx.enter_context(nc.sbuf_tensor(f"{name}_stat", [P, 4, rows], F32))
    sq = ctx.enter_context(nc.sbuf_tensor(f"{name}_sq", [P, rows, F], F32))
    total, mean, var, rstd = (stat[:, i, :] for i in range(4))
    step = nc.alloc_semaphore(f"{name}_dve_step")
    squared = nc.alloc_semaphore(f"{name}_squared")
    rooted = nc.alloc_semaphore(f"{name}_rooted")

    def over_features(col):
        return col.unsqueeze(2).broadcast_to([P, rows, F])

    with nc.Block() as block:
        @block.vector
        def _(dve):
            nc.vector.tensor_reduce(total, x[:], AX.X, ALU.add).then_inc(step, 1)
            dve.wait_ge(step, 1)
            nc.vector.tensor_scalar(mean, total, 1.0 / F, None, ALU.mult).then_inc(step, 1)
            dve.wait_ge(step, 2)
            nc.vector.tensor_tensor(hx[:], x[:], over_features(mean), ALU.subtract).then_inc(step, 1)
            dve.wait_ge(squared, 1)
            nc.vector.tensor_reduce(total, sq[:], AX.X, ALU.add).then_inc(step, 1)
            dve.wait_ge(step, 4)
            nc.vector.tensor_scalar(var, total, 1.0 / F, EPS, ALU.mult, ALU.add).then_inc(step, 1)
            dve.wait_ge(rooted, 1)
            nc.vector.reciprocal(rstd, mean).then_inc(step, 1)
            dve.wait_ge(step, 6)
            nc.vector.scalar_tensor_tensor(out=hx[:], in0=hx[:], scalar=0.0, in1=over_features(rstd),
                                           op0=ALU.max, op1=ALU.mult).then_inc(step, 1)

        @block.scalar
        def _(act):
            act.wait_ge(step, 3)
            nc.scalar.activation(sq[:], hx[:], ACT.Square).then_inc(squared, 1)
            act.wait_ge(step, 5)
            nc.scalar.activation(mean, var, ACT.Sqrt).then_inc(rooted, 1)


def layer0(nc, ctx, B, x, hx, ident, fold, adj, H, W, W_ind, a_node, a_gn, a_ge, fcW, fcb, av):
    sb = lambda n, s, d=F32: ctx.enter_context(nc.sbuf_tensor(f"l0_{n}", s, d))
    sem = lambda n: nc.alloc_semaphore(f"l0_{n}")
    E = H.shape[1]
    PAIRS = E // 2
    ps_a, ps_b, ps_c, ps_d = (ctx.enter_context(nc.psum_tensor(f"l0_ps_{n}", [P, N], F32)) for n in "abcd")
    halves = [slice(q * HALF, (q + 1) * HALF) for q in range(2)]

    adj_t = sb("adj_t", [P, NT, N])
    mask_rows = sb("mask_rows", [P, NT, E])
    mask_cols = sb("mask_cols", [E, N])
    w_st = sb("w_st", [P, P], F32R)
    wi_st = sb("wi_st", [P, P], F32R)
    v_st = sb("v_st", [P, 2, P], F32R)
    fcw, fcb_col, age_col = sb("fcw", [F, P]), sb("fcb_col", [P, 1]), sb("age_col", [F, 1])
    av_rep, av_neg = sb("av_rep", [P, P]), sb("av_neg", [P, P])
    ones = sb("ones", [P, P])
    fold2 = sb("fold2", [P, 2, F])

    with ExitStack() as own:
        mine = lambda n, s, d=F32: own.enter_context(nc.sbuf_tensor(f"l0_{n}", s, d))
        rows = mine("rows", [P, NT, N])
        h_rows = mine("h_rows", [P, NT, E])
        w_in, wi_in = mine("w_in", [P, 2, F]), mine("wi_in", [P, 2, F])
        w_t = mine("w_t", [F, P])
        cols = mine("cols", [F, 2])
        a_rep = mine("a_rep", [F, 2, P])
        av_col = mine("av_col", [P, 1])
        deg = mine("deg", [P, NT, 3])
        names = ("loaded adj_in summed floored inverted scaled hmask spread w_turned w_copied v_ready v_hi w_hi "
                 "w_lo turned untied hm_turned hm_copied const")
        S = {n: nc.alloc_semaphore(f"l0s_{n}") for n in names.split()}
        SMALL = 15 * 16
        with nc.Block() as block:
            @block.sync
            def _(sp):
                sp.dma_start(rows[:], adj.rearrange("(k p) m -> p k m", p=P)).then_inc(S["adj_in"], 16)
                sp.dma_start(h_rows[:], H.rearrange("(k p) e -> p k e", p=P)).then_inc(S["loaded"], 16)
                for to, src in ((w_in, W), (wi_in, W_ind)):
                    for r in range(2):
                        for c in range(2):
                            sp.dma_start(to[r * F:(r + 1) * F, c, :], src).then_inc(S["loaded"], 16)
                sp.dma_start(fcw[:], fcW).then_inc(S["loaded"], 16)
                with nc.allow_non_contiguous_dma(reason="a few hundred numbers"):
                    col = lambda v: v.rearrange("(f o) -> f o", o=1)
                    for to, src in ((fcb_col[:], fcb), (age_col[:], a_ge), (cols[:, 0:1], a_node),
                                    (cols[:, 1:2], a_gn), (av_col[:], av)):
                        sp.dma_start(to, col(src)).then_inc(S["loaded"], 16)
                sp.wait_ge(S["loaded"], SMALL)
                sp.wait_ge(S["adj_in"], 16)

            @block.gpsimd
            def _(pool):
                nc.gpsimd.memset(ones[:], 1.0).then_inc(S["const"], 1)
                nc.gpsimd.tensor_copy(fold2[:], fold[:].unsqueeze(1).broadcast_to([P, 2, F])).then_inc(S["const"], 1)

            @block.vector
            def _(dve):
                dve.wait_ge(S["loaded"], SMALL)
                nc.vector.tensor_copy(a_rep[:], cols[:].unsqueeze(2).broadcast_to([F, 2, P])).then_inc(S["spread"], 1)
                nc.vector.tensor_copy(av_rep[:], av_col[:].broadcast_to([P, P])).then_inc(S["spread"], 1)
                nc.vector.tensor_scalar(av_neg[:], av_col[:].broadcast_to([P, P]), -1.0, None,
                                        ALU.mult).then_inc(S["spread"], 1)
                nc.vector.tensor_scalar(mask_rows[:], h_rows[:], 0.0, MASKED, ALU.is_le, ALU.mult)\
                    .then_inc(S["hmask"], 1)
                dve.wait_ge(S["w_turned"], 1)
                nc.vector.tensor_copy(w_t[:], ps_a[0:F, 0:P]).then_inc(S["w_copied"], 1)
                dve.wait_ge(S["w_hi"], 2)
                for k, (to, src) in enumerate(((w_st, w_in), (wi_st, wi_in))):
                    nc.vector.tensor_tensor(to[F:P, :], src[F:P].rearrange("p c f -> p (c f)"),
                                            to[F:P, :].bitcast(F32), ALU.subtract).then_inc(S["w_lo"], 1)
                dve.wait_ge(S["v_hi"], 1)
                nc.vector.tensor_tensor(v_st[F:P], ps_b[F:P, 0:2 * P].rearrange("p (c n) -> p c n", n=P),
                                        v_st[F:P].bitcast(F32), ALU.subtract).then_inc(S["w_lo"], 1)
                dve.wait_ge(S["hm_turned"], 1)
                nc.vector.tensor_copy(mask_cols[:], ps_d[0:E, :]).then_inc(S["hm_copied"], 1)
                dve.wait_ge(S["adj_in"], 16)
                nc.vector.tensor_reduce(deg[:, :, 0], rows[:], AX.X, ALU.add).then_inc(S["summed"], 1)
                dve.wait_ge(S["summed"], 1)
                nc.vector.tensor_scalar(deg[:, :, 1], deg[:, :, 0], 1.0, None, ALU.max).then_inc(S["floored"], 1)
                dve.wait_ge(S["floored"], 1)
                nc.vector.reciprocal(deg[:, :, 2], deg[:, :, 1]).then_inc(S["inverted"], 1)
                dve.wait_ge(S["inverted"], 1)
                for k in range(NT):
                    nc.vector.tensor_scalar(rows[:, k, :], rows[:, k, :], deg[:, k, 2:3], None, ALU.mult)\
                        .then_inc(S["scaled"], 1)
                for m in range(NT):
                    if m % 2 == 0:
                        dve.wait_ge(S["turned"], m + 1)
                        nc.vector.tensor_copy(adj_t[:, m, :], ps_a[:]).then_inc(S["untied"], 1)

            @block.scalar
            def _(act):
                act.wait_ge(S["loaded"], SMALL)
                for to, src in ((w_st, w_in), (wi_st, wi_in)):
                    nc.scalar.activation(to[:], src[:].rearrange("p c f -> p (c f)"), ACT.Copy).then_inc(S["w_hi"], 1)
                act.wait_ge(S["v_ready"], 1)
                nc.scalar.activation(v_st[:], ps_b[:, 0:2 * P].rearrange("p (c n) -> p c n", n=P), ACT.Copy)\
                    .then_inc(S["v_hi"], 1)
                for m in range(1, NT, 2):
                    act.wait_ge(S["turned"], m + 1)
                    nc.scalar.activation(adj_t[:, m, :], ps_c[:], ACT.Copy).then_inc(S["v_hi"], 1)

            @block.tensor
            def _(pe):
                pe.wait_ge(S["loaded"], SMALL)
                nc.tensor.transpose(ps_a[0:F, 0:P], w_in[:, 0, :], ident[:]).then_inc(S["w_turned"], 1)
                pe.wait_ge(S["hmask"], 1)
                for k in range(NT):
                    last = nc.tensor.transpose(ps_d[0:E, k * P:(k + 1) * P], mask_rows[:, k, :], ident[:])
                last.then_inc(S["hm_turned"], 1)
                pe.wait_ge(S["w_copied"], 1)
                pe.wait_ge(S["spread"], 1)
                nc.tensor.matmul(ps_b[:, 0:2 * P], w_t[:], a_rep[:].rearrange("p c n -> p (c n)"),
                                 start=True, stop=True).then_inc(S["v_ready"], 1)
                pe.wait_ge(S["scaled"], NT)
                for m in range(NT):
                    bank = ps_a if m % 2 == 0 else ps_c
                    if m >= 2:
                        pe.wait_ge(S["untied"] if m % 2 == 0 else S["v_hi"], m // 2 + m % 2)
                    for k in range(NT):
                        last = nc.tensor.transpose(bank[:, k * P:(k + 1) * P], rows[:, k, m * P:(m + 1) * P], ident[:])
                    last.then_inc(S["turned"], 1)

    pair = sb("pair", [P, NT, 2, F])
    xhh, xll = sb("xhh", [P, N], F32R), sb("xll", [P, N], F32R)
    h_t = sb("h_t", [P, N])
    h_n = sb("h_n", [P, NT, P])
    al = sb("al", [E, N])
    al_t = sb("al_t", [P, NT, E])
    al_stat = sb("al_stat", [E, 3])
    agg2, nagg2 = sb("agg2", [P, PAIRS]), sb("nagg2", [P, PAIRS])
    agg_td = sb("agg_td", [F, 2, E])
    agg_e = sb("agg_e", [E, P])
    he_e, he = sb("he_e", [F, E]), sb("he", [F, E])
    u_t = sb("u_t", [P, E])
    age = sb("age", [P, 1])
    beta = sb("beta", [P, N])
    bhl, chl = sb("bhl", [P, N], F32R), sb("chl", [P, N], F32R)
    lc = sb("lc", [P, NT, E])
    lc_stat = sb("lc_stat", [P, 3, NT])
    c_n = sb("c_n", [P, NT, 2, E])
    m1, c1 = sb("m1", [E, N]), sb("c1", [E, N])
    hlin = sb("hlin", [P, N])
    zc = [sb(f"zc{i}", [P, N]) for i in range(2)]
    r = [sb(f"r{i}", [P, N]) for i in range(4)]
    ex = [sb(f"ex{i}", [P, N]) for i in range(2)]
    u = [sb(f"u{i}", [P, N]) for i in range(2)]
    sel_b, sel_c = ([sb(f"sel_{n}{i}", [P, 2, F], F32R) for i in range(2)] for n in "bc")
    g_t, ind = beta, h_t
    xw = h_n
    tg, ti = zc[0], zc[1]
    mix = r[0]
    res = r[1]

    names = ("paired xt hh ll ht ht_out v hg hn hn_out v02 lean peak alex alinv alnorm al_turned al_out agg "
             "agg_out he_ex he_min he_done age ut ut_out se age_out tanh_b beta bhi blo lc mx lcs lce lcsum lcinv c_n "
             "c_turned chi m1 c1 clo lin bsum hlin g xw xw_out ind ind_out sg sg_out si si_out diff wt wt2 d dw "
             "res res_t added passed pe_passed")
    S = {n: sem(n) for n in names.split()}
    names = "selb selc b_in zc_done r_done ex_done t_done c_in u_done folded"
    T = {n: sem(n) for n in names.split()}
    LAG = 3

    with nc.Block() as block:
        def pairs_of(loop, step):
            ends = lambda s: lambda k: 0 <= s - k < PAIRS
            for s in range(4):
                step(s, s % 4, ends(s))
            with loop(4, PAIRS - 4, 4) as s0:
                for j in range(4):
                    step(s0 + j, j, lambda k: True)
            for s in range(PAIRS - 4, PAIRS + LAG + 1):
                step(s, s % 4, ends(s))

        @block.gpsimd
        def _(pool):
            with pool.Fori(0, B) as b:
                nc.gpsimd.tensor_copy(pair[:], hx[:, bass.ds(b * NT, NT), :].unsqueeze(2)
                                      .broadcast_to([P, NT, 2, F])).then_inc(S["paired"], 1)

                def select(to, k, done):
                    src = fold[:].rearrange("p (c k) -> p c k", k=PAIRS)[:, :, bass.ds(k, 1)]
                    nc.gpsimd.tensor_copy(to[:], src.broadcast_to([P, 2, F])).then_inc(done, 1)

                def step(s, j, has):
                    n = PAIRS * b + s
                    if has(-1):
                        if has(1):
                            pool.wait_ge(T["b_in"], n)
                            pool.sem_inc(S["passed"], 1)
                        select(sel_b[(j + 1) % 2], s + 1, T["selb"])
                    if has(2):
                        if has(4):
                            pool.wait_ge(T["c_in"], n - 3)
                            pool.sem_inc(S["passed"], 1)
                        select(sel_c[j % 2], s - 2, T["selc"])
                    if has(1):
                        pool.wait_ge(T["ex_done"], n)
                        nc.gpsimd.tensor_tensor(r[(j - 1) % 4][:], r[(j - 1) % 4][:], ex[(j - 1) % 2][:], ALU.add)\
                            .then_inc(T["t_done"], 1)

                select(sel_b[0], 0, T["selb"])
                pairs_of(pool.Fori, step)

        @block.tensor
        def _(pe):
            with pe.Fori(0, B) as b:
                after = lambda name: pe.wait_ge(S[name], b + 1)

                def product(out, lhs_t, parts):
                    for c in halves:
                        for part in parts:
                            last = nc.tensor.matmul(out[:, c], lhs_t, part[:, c], start=(part is parts[0]),
                                                    stop=(part is parts[-1]))
                    return last

                def rows_of(out, weights):
                    for k in range(NT):
                        c = slice(k * P, (k + 1) * P)
                        for part in (xhh, xll):
                            last = nc.tensor.matmul(out[:, c], part[:, c], weights[:], start=(part is xhh),
                                                    stop=(part is xll))
                    return last

                after("paired")
                for k in range(NT):
                    last = nc.tensor.transpose(ps_a[:, k * P:(k + 1) * P],
                                               pair[:, k].rearrange("p c f -> p (c f)"), ident[:])
                last.then_inc(S["xt"], 1)
                after("ll")
                product(ps_a, v_st[:, 0], (xhh, xll)).then_inc(S["v"], 1)
                rows_of(ps_d, w_st).then_inc(S["hn"], 1)
                product(ps_b, w_st[:], (xhh, xll)).then_inc(S["ht"], 1)
                product(ps_c, v_st[:, 1], (xhh, xll)).then_inc(S["hg"], 1)
                after("alnorm")
                pe.sem_inc(S["pe_passed"], 1)
                for k in range(NT):
                    last = nc.tensor.transpose(ps_a[:, k * E:(k + 1) * E], al[:, k * P:(k + 1) * P], ident[0:E, 0:E])
                last.then_inc(S["al_turned"], 1)
                after("al_out")
                after("hn_out")
                after("ht_out")
                for k in range(NT):
                    nc.tensor.matmul(ps_b[:, 0:E], h_n[:, k, :], al_t[:, k, :], start=(k == 0), stop=(k == NT - 1))
                for k in range(NT):
                    last = nc.tensor.matmul(ps_b[0:E, HALF:HALF + P], al_t[:, k, :], h_n[:, k, :],
                                            start=(k == 0), stop=(k == NT - 1))
                last.then_inc(S["agg"], 1)
                after("agg_out")
                nc.tensor.matmul(ps_a[:, 0:1], agg_td[:].rearrange("p c e -> p (c e)"), age_col[:],
                                 start=True, stop=True).then_inc(S["age"], 1)
                after("he_done")
                nc.tensor.matmul(ps_a[:, HALF:HALF + E], fcw[:], he[:], start=True, stop=True).then_inc(S["ut"], 1)
                after("ut_out")
                after("age_out")
                nc.tensor.matmul(ps_a[:, 0:E], av_rep[:], u_t[:], start=True, stop=True).then_inc(S["se"], 1)
                after("c_n")
                for k in range(NT):
                    last = nc.tensor.transpose(ps_d[:, k * P:(k + 1) * P],
                                               c_n[:, k].rearrange("p c e -> p (c e)"), ident[:])
                last.then_inc(S["c_turned"], 1)
                after("m1")
                product(ps_a, ones[0:E, :], (m1,)).then_inc(S["bsum"], 1)
                after("c1")
                after("tanh_b")
                for c in halves:
                    last = nc.tensor.matmul(ps_c[:, c], agg_e[:], c1[:, c], start=True, stop=False)
                last.then_inc(S["lin"], 1)
                after("hlin")
                after("blo")
                after("clo")

                def step(s, j, has):
                    n = PAIRS * b + s
                    if has(0):
                        pe.wait_ge(T["selb"], n + 1)
                        if has(2):
                            pe.wait_ge(T["zc_done"], n - 1)
                        product((ps_a, ps_b)[j % 2], sel_b[j % 2][:].rearrange("p c f -> p (c f)"), (bhl,))\
                            .then_inc(T["b_in"], 1)
                    if has(3):
                        pe.wait_ge(T["selc"], n - 2)
                        if has(4):
                            pe.wait_ge(T["u_done"], n - 3)
                        product(ps_d, sel_c[(j - 3) % 2][:].rearrange("p c f -> p (c f)"), (chl,))\
                            .then_inc(T["c_in"], 1)
                    if has(4):
                        pe.wait_ge(T["u_done"], n - 3)
                        final = isinstance(s, int) and s == PAIRS + LAG
                        for c in halves:
                            last = nc.tensor.matmul(ps_c[:, c], fold2[:].rearrange("p c f -> p (c f)"),
                                                    u[(j - 4) % 2][:, c], start=False, stop=final)
                        last.then_inc(T["folded"], 1)

                pairs_of(pe.Fori, step)
                pe.wait_ge(T["zc_done"], PAIRS * b + PAIRS)
                rows_of(ps_a, wi_st).then_inc(S["xw"], 1)
                after("xw_out")
                for c in halves:
                    for m in range(NT):
                        last = nc.tensor.matmul(ps_b[:, c], xw[:, m, :], adj_t[:, m, c], start=(m == 0),
                                                stop=(m == NT - 1))
                last.then_inc(S["ind"], 1)
                after("g")
                product(ps_a, fcw[:], (g_t[0:F, :],)).then_inc(S["sg"], 1)
                after("ind_out")
                product(ps_d, fcw[:], (ind[0:F, :],)).then_inc(S["si"], 1)
                after("sg_out")
                after("si_out")
                for c in halves:
                    nc.tensor.matmul(ps_c[:, c], av_rep[:], tg[:, c], start=True, stop=False)
                    last = nc.tensor.matmul(ps_c[:, c], av_neg[:], ti[:, c], start=False, stop=True)
                last.then_inc(S["diff"], 1)
                after("res")
                pe.sem_inc(S["pe_passed"], 1)
                for k in range(NT):
                    last = nc.tensor.transpose(ps_b[:, k * F:(k + 1) * F], res[0:F, k * P:(k + 1) * P], ident[0:F, 0:F])
                last.then_inc(S["res_t"], 1)

        @block.vector
        def _(dve):
            with dve.Fori(0, B) as b:
                after = lambda name: dve.wait_ge(S[name], b + 1)
                tt, ts, stt = nc.vector.tensor_tensor, nc.vector.tensor_scalar, nc.vector.scalar_tensor_tensor
                after("hh")
                tt(xll[:], ps_a[:], xhh[:].bitcast(F32), ALU.subtract).then_inc(S["ll"], 1)
                after("v02")
                stt(out=al[:], in0=ps_a[0:E, :], scalar=1.0, in1=m1[:], op0=ALU.mult, op1=ALU.max)\
                    .then_inc(S["lean"], 1)
                after("lean")
                dve.sem_inc(S["passed"], 1)
                nc.vector.tensor_tensor_reduce(out=al[:], in0=al[:], in1=mask_cols[:], scale=-1.0, scalar=3.0e38,
                                               op0=ALU.add, op1=ALU.min, accum_out=al_stat[:, 0:1])\
                    .then_inc(S["peak"], 1)
                after("alex")
                nc.vector.reciprocal(al_stat[:, 2:3], al_stat[:, 1:2]).then_inc(S["alinv"], 1)
                after("alinv")
                ts(al[:], al[:], al_stat[:, 2:3], None, ALU.mult).then_inc(S["alnorm"], 1)
                after("al_turned")
                nc.vector.tensor_copy(al_t[:].rearrange("p k e -> p (k e)"), ps_a[:, 0:NT * E]).then_inc(S["al_out"], 1)
                after("agg")
                for c in range(2):
                    part = ps_b[c * F:(c + 1) * F, c * PAIRS:(c + 1) * PAIRS]
                    nc.vector.tensor_copy(agg2[c * F:(c + 1) * F, :], part)
                    ts(nagg2[c * F:(c + 1) * F, :], part, -1.0, None, ALU.mult)
                    nc.vector.tensor_copy(agg_td[:, c, :], ps_b[0:F, 0:E])
                nc.vector.tensor_copy(agg_e[:], ps_b[0:E, HALF:HALF + P]).then_inc(S["agg_out"], 1)
                after("he_ex")
                ts(he_e[:], he_e[:], 1.0, -1.0, ALU.min, ALU.add).then_inc(S["he_min"], 1)
                after("he_min")
                stt(out=he[:], in0=agg_td[:, 0, :], scalar=0.0, in1=he_e[:], op0=ALU.max, op1=ALU.add)\
                    .then_inc(S["he_done"], 1)
                after("tanh_b")
                ts(beta[:], beta[:], 0.5, 0.5, ALU.mult, ALU.add).then_inc(S["beta"], 1)
                after("bhi")
                tt(bhl[F:P, :], beta[F:P, :], bhl[F:P, :].bitcast(F32), ALU.subtract).then_inc(S["blo"], 1)
                wide = [P, NT, E]
                over_e = lambda i: lc_stat[:, i, :].unsqueeze(2).broadcast_to(wide)
                after("se")
                tt(lc[:], mask_rows[:], ps_a[:, 0:E].unsqueeze(1).broadcast_to(wide), ALU.add).then_inc(S["lc"], 1)
                after("lc")
                nc.vector.tensor_reduce(lc_stat[:, 0, :], lc[:], AX.X, ALU.max).then_inc(S["mx"], 1)
                after("mx")
                tt(lc[:], lc[:], over_e(0), ALU.subtract).then_inc(S["lcs"], 1)
                after("lce")
                nc.vector.tensor_reduce(lc_stat[:, 1, :], lc[:], AX.X, ALU.add).then_inc(S["lcsum"], 1)
                after("lcsum")
                nc.vector.reciprocal(lc_stat[:, 2, :], lc_stat[:, 1, :]).then_inc(S["lcinv"], 1)
                after("lcinv")
                for c in range(2):
                    last = tt(c_n[:, :, c, :], lc[:], over_e(2), ALU.mult)
                last.then_inc(S["c_n"], 1)
                after("c_turned")
                after("chi")
                tt(m1[:], ps_d[0:E, :], beta[0:E, :], ALU.mult).then_inc(S["m1"], 1)
                after("m1")
                tt(c1[:], ps_d[0:E, :], m1[:], ALU.subtract).then_inc(S["c1"], 1)
                tt(chl[F:P, :], ps_d[F:P, :], chl[F:P, :].bitcast(F32), ALU.subtract).then_inc(S["clo"], 1)
                after("bsum")
                tt(hlin[:], h_t[:], ps_a[:], ALU.mult).then_inc(S["hlin"], 1)

                def step(s, j, has):
                    n = PAIRS * b + s
                    if has(0):
                        if has(2):
                            dve.wait_ge(T["r_done"], n - 1)
                        dve.wait_ge(T["b_in"], n + 1)
                        stt(out=zc[j % 2][:], in0=h_t[:], scalar=agg2[:, bass.ds(s, 1)], in1=(ps_a, ps_b)[j % 2][:],
                            op0=ALU.subtract, op1=ALU.mult).then_inc(T["zc_done"], 1)
                    if has(3):
                        dve.wait_ge(T["t_done"], n - 2)
                        if has(5):
                            dve.wait_ge(T["folded"], n - 4)
                        dve.wait_ge(T["c_in"], n - 2)
                        tt(u[(j - 3) % 2][:], r[(j - 3) % 4][:], ps_d[:], ALU.mult).then_inc(T["u_done"], 1)

                pairs_of(dve.Fori, step)
                dve.wait_ge(T["folded"], PAIRS * b + PAIRS)
                stt(out=g_t[:], in0=ps_c[:], scalar=-1.0, in1=hlin[:], op0=ALU.add, op1=ALU.add).then_inc(S["g"], 1)
                after("ind_out")
                after("g")
                tt(res[:], g_t[:], ind[:], ALU.subtract).then_inc(S["d"], 1)
                after("wt")
                ts(mix[:], mix[:], 0.5, 0.5, ALU.mult, ALU.add).then_inc(S["wt2"], 1)
                after("wt2")
                tt(res[:], res[:], mix[:], ALU.mult).then_inc(S["dw"], 1)
                after("dw")
                tt(res[:], res[:], ind[:], ALU.add).then_inc(S["res"], 1)
                after("res_t")
                rows = x[:, bass.ds(b * NT, NT), :]
                tt(rows, rows, ps_b[:, 0:NT * F].rearrange("p (k f) -> p k f", f=F), ALU.add).then_inc(S["added"], 1)

        @block.scalar
        def _(act):
            with act.Fori(0, B) as b:
                after = lambda name: act.wait_ge(S[name], b + 1)
                fn = nc.scalar.activation
                after("xt")
                fn(xhh[:], ps_a[:], ACT.Copy).then_inc(S["hh"], 1)
                after("v")
                fn(m1[:], ps_a[0:E, :], ACT.Copy, scale=0.2).then_inc(S["v02"], 1)
                after("hn")
                fn(h_n[:].rearrange("p k c -> p (k c)"), ps_d[:], ACT.Copy).then_inc(S["hn_out"], 1)
                after("ht")
                fn(h_t[:], ps_b[:], ACT.Copy).then_inc(S["ht_out"], 1)
                after("peak")
                fn(al[:], al[:], ACT.Exp, bias=al_stat[:, 0:1], scale=-1.0, accum_out=al_stat[:, 1:2])\
                    .then_inc(S["alex"], 1)
                after("agg_out")
                fn(he_e[:], agg_td[:, 0, :], ACT.Exp).then_inc(S["he_ex"], 1)
                after("age")
                fn(age[:], ps_a[:, 0:1], ACT.Copy, scale=0.5).then_inc(S["age_out"], 1)
                after("ut")
                fn(u_t[:], ps_a[:, HALF:HALF + E], ACT.Tanh, bias=fcb_col[:, 0:1]).then_inc(S["ut_out"], 1)
                after("hg")
                after("age_out")
                fn(beta[:], ps_c[:], ACT.Tanh, bias=age[:, 0:1], scale=0.5).then_inc(S["tanh_b"], 1)
                after("beta")
                fn(bhl[:], beta[:], ACT.Copy).then_inc(S["bhi"], 1)
                after("lcs")
                fn(lc[:], lc[:], ACT.Exp).then_inc(S["lce"], 1)
                after("c_turned")
                fn(chl[:], ps_d[:], ACT.Copy).then_inc(S["chi"], 1)

                def step(s, j, has):
                    n = PAIRS * b + s
                    if has(0):
                        if has(4):
                            act.wait_ge(T["u_done"], n - 3)
                        act.wait_ge(T["zc_done"], n + 1)
                        act.sem_inc(S["passed"], 1)
                        fn(r[j % 4][:], zc[j % 2][:], ACT.Relu, bias=nagg2[:, bass.ds(s, 1)], scale=-1.0)\
                            .then_inc(T["r_done"], 1)
                    if has(1):
                        if has(3):
                            act.wait_ge(T["t_done"], n - 2)
                        act.wait_ge(T["r_done"], n)
                        fn(ex[(j - 1) % 2][:], r[(j - 1) % 4][:], ACT.Exp, scale=-1.0).then_inc(T["ex_done"], 1)

                pairs_of(act.Fori, step)
                after("xw")
                fn(xw[:].rearrange("p k c -> p (k c)"), ps_a[:], ACT.Copy).then_inc(S["xw_out"], 1)
                after("ind")
                fn(ind[:], ps_b[:], ACT.Copy).then_inc(S["ind_out"], 1)
                after("sg")
                fn(tg[:], ps_a[:], ACT.Tanh, bias=fcb_col[:, 0:1]).then_inc(S["sg_out"], 1)
                after("si")
                fn(ti[:], ps_d[:], ACT.Tanh, bias=fcb_col[:, 0:1]).then_inc(S["si_out"], 1)
                after("diff")
                fn(mix[:], ps_c[:], ACT.Tanh, scale=0.5).then_inc(S["wt"], 1)


class Attention:

    def __init__(self, nc, ctx, name):
        sb = lambda n, s, d=F32: ctx.enter_context(nc.sbuf_tensor(f"{name}_{n}", s, d))
        sem = lambda n: nc.alloc_semaphore(f"{name}_{n}")
        ps = lambda n, s: ctx.enter_context(nc.psum_tensor(f"{name}_{n}", s, F32))
        sem = lambda n: nc.alloc_semaphore(f"{name}_{n}")
        self.nc = nc
        self.pair = sb("pair", [P, NT, 2, F])
        self.paired = sem("paired")
        self.prob = [sb(f"prob{i}", [P, N]) for i in range(4)]
        self.negmax = sb("negmax", [P, 4])
        self.rowsum = sb("rowsum", [P, 4])
        self.rowinv = sb("rowinv", [P, 4])
        self.pt_hi = [sb(f"pt_hi{i}", [P, NT, HALF], F32R) for i in range(2)]
        self.pt_lo = [sb(f"pt_lo{i}", [P, NT, HALF], F32R) for i in range(2)]
        self.z = [sb(f"z{i}", [P, HALF]) for i in range(2)]
        self.ps_score = [ps(f"ps_score{i}", [P, N]) for i in range(2)]
        self.ps_turn = [ps(f"ps_turn{i}", [P, HALF]) for i in range(2)]
        self.ps_z = ps("ps_z", [P, HALF])
        self.ps_post = ps("ps_post", [P, HALF])
        self.xhh = sb("xhh", [P, N], F32R)
        self.xll = sb("xll", [P, N], F32R)
        self.xhl = sb("xhl", [P, N], F32R)
        self.xm = sb("xm", [P, NT, P], F32R)
        self.scored = sem("scored")
        self.masked = sem("masked")
        self.exped = sem("exped")
        self.dve_passed, self.pool_passed = sem("dve_passed"), sem("pool_passed")
        self.inverted = sem("inverted")
        self.normed = sem("normed")
        self.turned = sem("turned")
        self.high = sem("high")
        self.low = sem("low")
        self.summed = sem("summed")
        self.copied = sem("copied")
        self.posted = sem("posted")
        self.finished = sem("finished")
        self.xt_ready = sem("xt_ready")
        self.hh_ready = sem("hh_ready")
        self.ll_ready = sem("ll_ready")
        self.hl_ready = sem("hl_ready")
        self.xm_turned = sem("xm_turned")
        self.xm_ready = sem("xm_ready")

    def dve_credits(self, dve):
        dve.sem_inc(self.masked, 2)
        dve.sem_inc(self.low, 2)
        dve.sem_inc(self.copied, 1)

    def pe_credits(self, pe):
        pe.sem_inc(self.turned, 8)
        pe.sem_inc(self.summed, 2)
        pe.sem_inc(self.posted, 2)

    def pe_score_free(self, pe, u, i):
        pe.wait_ge(self.masked, 8 * u + i + 1)

    def dve_mask_add(self, dve, u, i, mask):
        dve.wait_ge(self.turned, 16 * u + 2 * i + 2)
        dve.wait_ge(self.scored, 8 * u + i + 1)
        dve.sem_inc(self.dve_passed, 1)
        self.nc.vector.tensor_tensor_reduce(
            out=self.prob[i % 4][:], in0=self.ps_score[i % 2][:], in1=mask, scale=-1.0, scalar=3.0e38,
            op0=ALU.add, op1=ALU.min, accum_out=self.negmax[:, i % 4:i % 4 + 1]).then_inc(self.masked, 1)

    def act_exp(self, act, u, i):
        act.wait_ge(self.masked, 8 * u + i + 3)
        c = slice(i % 4, i % 4 + 1)
        self.nc.scalar.activation(self.prob[i % 4][:], self.prob[i % 4][:], ACT.Exp, bias=self.negmax[:, c],
                                  scale=-1.0, accum_out=self.rowsum[:, c]).then_inc(self.exped, 1)

    def dve_invert(self, dve, u, i):
        dve.wait_ge(self.exped, 8 * u + i + 1)
        c = slice(i % 4, i % 4 + 1)
        self.nc.vector.reciprocal(self.rowinv[:, c], self.rowsum[:, c]).then_inc(self.inverted, 1)

    def pool_norm(self, pool, u, i):
        pool.wait_ge(self.inverted, 8 * u + i + 1)
        pool.sem_inc(self.pool_passed, 1)
        self.nc.gpsimd.tensor_scalar(self.prob[i % 4][:], self.prob[i % 4][:], self.rowinv[:, i % 4:i % 4 + 1],
                                     1.0, ALU.mult, ALU.mult).then_inc(self.normed, 1)

    def pe_turn(self, pe, u, i, ident):
        pe.wait_ge(self.normed, 8 * u + i + 1)
        for j in range(2):
            pe.wait_ge(self.low, 16 * u + 2 * i + j + 1)
            for k in range(TPH):
                m = TPH * j + k
                last = self.nc.tensor.transpose(self.ps_turn[j][:, k * P:(k + 1) * P],
                                                self.prob[i % 4][:, m * P:(m + 1) * P], ident[:])
            last.then_inc(self.turned, 1)

    def part(self, parts, i, j):
        return parts[i // TPH][:, TPH * j:TPH * (j + 1), (i % TPH) * P:(i % TPH + 1) * P]

    def act_high(self, act, u, i, j):
        act.wait_ge(self.turned, 16 * u + 2 * i + j + 9)
        if i % TPH == 0 and j == 0:
            act.wait_ge(self.summed, 2 * u + i // TPH + 1)
        self.nc.scalar.activation(self.part(self.pt_hi, i, j),
                                  self.ps_turn[j][:].rearrange("p (k n) -> p k n", n=P),
                                  ACT.Copy).then_inc(self.high, 1)

    def dve_low(self, dve, u, i, j):
        dve.wait_ge(self.high, 16 * u + 2 * i + j + 1)
        if i % TPH == 0 and j == 0:
            dve.wait_ge(self.summed, 2 * u + i // TPH + 1)
        self.nc.vector.tensor_tensor(self.part(self.pt_lo, i, j),
                                     self.ps_turn[j][:].rearrange("p (k n) -> p k n", n=P),
                                     self.part(self.pt_hi, i, j).bitcast(F32), ALU.subtract).then_inc(self.low, 1)

    def pe_sum(self, pe, u, q):
        pe.wait_ge(self.low, 16 * u + 8 * (q + 1) + 2)
        pe.wait_ge(self.copied, 2 * u + q + 1)
        for part in (self.pt_hi, self.pt_lo):
            for m in range(NT):
                last = self.nc.tensor.matmul(self.ps_z[:], self.xm[:, m, :], part[q][:, m, :],
                                             start=(part is self.pt_hi and m == 0),
                                             stop=(part is self.pt_lo and m == NT - 1))
        last.then_inc(self.summed, 1)

    def dve_copy(self, dve, u, q):
        dve.wait_ge(self.summed, 2 * u + q + 3)
        dve.wait_ge(self.posted, 2 * u + q + 1)
        self.nc.vector.tensor_copy(self.z[q][:], self.ps_z[:]).then_inc(self.copied, 1)

    def act_xhh(self, act, n):
        act.wait_ge(self.xt_ready, n + 1)
        self.nc.scalar.activation(self.xhh[:], self.ps_score[0][:], ACT.Copy).then_inc(self.hh_ready, 1)

    def dve_xll(self, dve, n):
        dve.wait_ge(self.hh_ready, n + 1)
        self.nc.vector.tensor_tensor(self.xll[:], self.ps_score[0][:], self.xhh[:].bitcast(F32),
                                     ALU.subtract).then_inc(self.ll_ready, 1)

    def act_xhl(self, act, n):
        act.wait_ge(self.ll_ready, n + 1)
        for rows, part in ((slice(0, F), self.xhh), (slice(F, P), self.xll)):
            self.nc.scalar.activation(self.xhl[rows, :], part[rows, :].bitcast(F32), ACT.Copy)\
                .then_inc(self.hl_ready, 1)

    def pe_xm_turn(self, pe, n, ident):
        pe.wait_ge(self.hl_ready, 2 * n + 2)
        for k in range(NT):
            last = self.nc.tensor.transpose(self.ps_score[1][:, k * P:(k + 1) * P],
                                            self.xhl[:, k * P:(k + 1) * P].bitcast(F32), ident[:])
        last.then_inc(self.xm_turned, 1)

    def dve_xm(self, dve, n):
        dve.wait_ge(self.xm_turned, n + 1)
        self.nc.vector.tensor_copy(self.xm[:].rearrange("p k c -> p (k c)"), self.ps_score[1][:])\
            .then_inc(self.xm_ready, 1)

    def pool_pair(self, pool, b, hx):
        self.nc.gpsimd.tensor_copy(
            self.pair[:], hx[:, bass.ds(b * NT, NT), :].unsqueeze(2).broadcast_to([P, NT, 2, F]))\
            .then_inc(self.paired, 1)

    def pe_x_turn(self, pe, b, ident):
        pe.wait_ge(self.paired, b + 1)
        for k in range(NT):
            last = self.nc.tensor.transpose(self.ps_score[0][:, k * P:(k + 1) * P],
                                            self.pair[:, k].rearrange("p c f -> p (c f)"), ident[:])
        last.then_inc(self.xt_ready, 1)


def layer1(nc, ctx, B, x, hx, mask, ident, fold, Wh, bh, W_out, b_out):
    sb = lambda n, s, d=F32: ctx.enter_context(nc.sbuf_tensor(n, s, d))
    sem = lambda n: nc.alloc_semaphore(n)
    UNITS = HEADS + 1
    ww = sb("ww", [P, HEADS, HID])
    g = sb("g", [P, HEADS, P], F32R)
    bcol = sb("bcol", [P, HEADS])
    wo = sb("wo", [P, HEADS, 2, F])
    bout = sb("bout", [P, F])
    at = Attention(nc, ctx, "l1")
    loaded, wt_ready, wt_done, g_ready, g_hi, g_lo = (
        sem(f"l1_{n}") for n in ("loaded", "wt_ready", "wt_done", "g_ready", "g_hi", "g_lo"))
    LOADS = 6 * 16
    wt = at.prob[0]

    with nc.Block() as block:
        @block.sync
        def _(sp):
            sp.dma_start(ww[0:F], Wh.rearrange("h c d -> c h d")).then_inc(loaded, 16)
            sp.dma_start(ww[F:P], Wh.rearrange("h c d -> c h d")).then_inc(loaded, 16)
            with nc.allow_non_contiguous_dma(reason="a small transposed load"):
                sp.dma_start(bcol[:], bh.rearrange("h d -> d h")).then_inc(loaded, 16)
            for c in range(2):
                sp.dma_start(wo[:, :, c, :], W_out.rearrange("(h d) f -> d h f", d=HID)).then_inc(loaded, 16)
            sp.dma_start(bout[:], b_out.rearrange("(o f) -> o f", o=1).broadcast_to([P, F])).then_inc(loaded, 16)
            sp.wait_ge(loaded, LOADS)

        @block.tensor
        def _(pe):
            pe.wait_ge(loaded, LOADS)
            for h in range(HEADS):
                last = nc.tensor.transpose(at.ps_score[0][:, h * P:(h + 1) * P], ww[:, h, :], ident[:])
            last.then_inc(wt_ready, 1)
            pe.wait_ge(wt_done, 1)
            for h in range(HEADS):
                w = wt[:, h * P:(h + 1) * P]
                last = nc.tensor.matmul(at.ps_score[1][:, h * P:(h + 1) * P], w, w, start=True, stop=True)
            last.then_inc(g_ready, 1)

        @block.vector
        def _(dve):
            dve.wait_ge(wt_ready, 1)
            nc.vector.tensor_copy(wt[:], at.ps_score[0][:]).then_inc(wt_done, 1)
            dve.wait_ge(g_hi, 1)
            nc.vector.tensor_tensor(g[F:P], at.ps_score[1][F:P, :].rearrange("p (h c) -> p h c", c=P),
                                    g[F:P].bitcast(F32), ALU.subtract).then_inc(g_lo, 1)

        @block.scalar
        def _(act):
            act.wait_ge(g_ready, 1)
            nc.scalar.activation(g[:], at.ps_score[1][:].rearrange("p (h c) -> p h c", c=P),
                                 ACT.Copy).then_inc(g_hi, 1)

    cat = sb("cat", [P, HEADS, N])
    y = [sb(f"y{i}", [P, N], F32R) for i in range(2)]
    gs = [sb(f"gs{i}", [P, P], F32R) for i in range(2)]
    ws = [sb(f"ws{i}", [P, HID]) for i in range(2)]
    bs = [sb(f"bs{i}", [P, 1]) for i in range(2)]
    biased = at.pair[:].rearrange("p k c f -> p (k c f)")[:, 0:HALF]
    last_act = cat[:, 0, 0:TPH * F].rearrange("p (i f) -> p i f", f=F)
    staged = sem("l1_staged")
    projected = sem("l1_projected")
    y_hi, y_lo = sem("l1_y_hi"), sem("l1_y_lo")
    cat_biased = sem("l1_cat_biased")
    cat_done = sem("l1_cat_done")
    out_sum = sem("l1_out_sum")

    with nc.Block() as block:

        def heads_of(loop, unit):
            unit(0, 0, False, True)
            unit(1, 1, True, True)
            with loop(2, HEADS - 2, 2) as h:
                unit(h, 0, True, True)
                unit(h + 1, 1, True, True)
            unit(HEADS - 2, 0, True, True)
            unit(HEADS - 1, 1, True, False)

        @block.tensor
        def _(pe):
            at.pe_credits(pe)
            with pe.Fori(0, B) as b:
                u0, n0 = b * UNITS, b * (2 * HEADS)

                def project(h, par, q):
                    if q == 0:
                        pe.wait_ge(staged, 3 * HEADS * b + 3 * h + 3)
                    else:
                        pe.wait_ge(y_lo, n0 + 2 * h + 1)
                    c = slice(q * HALF, (q + 1) * HALF)
                    nc.tensor.matmul(at.ps_post[:], gs[par][:], at.xhh[:, c], start=True, stop=False)
                    nc.tensor.matmul(at.ps_post[:], gs[par][:], at.xll[:, c], start=False, stop=True)\
                        .then_inc(projected, 1)

                def score(u, i, operand):
                    at.pe_score_free(pe, u, i)
                    for q in range(2):
                        c = slice(q * HALF, (q + 1) * HALF)
                        for part in (at.xhh, at.xll):
                            last = nc.tensor.matmul(at.ps_score[i % 2][:, c], operand[:, i * P:(i + 1) * P],
                                                    part[:, c], start=(part is at.xhh), stop=(part is at.xll))
                    last.then_inc(at.scored, 1)

                def post(h, par, q):
                    pe.wait_ge(at.copied, 2 * u0 + 2 * h + q + 2)
                    nc.tensor.matmul(at.ps_post[:], ws[par][:], at.z[q][:], start=True, stop=True)\
                        .then_inc(at.posted, 1)

                def unit(h, par, prev, following):
                    u = u0 + h
                    pe.wait_ge(y_lo, n0 + 2 * h + 2)
                    for i in range(NT):
                        score(u, i, y[par])
                        if i >= 2:
                            at.pe_turn(pe, u, i - 2, ident)
                        elif prev:
                            at.pe_turn(pe, u - 1, i + 6, ident)
                        if i == 1 and prev:
                            at.pe_sum(pe, u - 1, 1)
                        if i == 3 and prev:
                            pe.wait_ge(cat_biased, n0 + 2 * h - 1)
                            post(h - 1, 1 - par, 1)
                        if i == 4 and following:
                            if prev:
                                pe.wait_ge(cat_biased, n0 + 2 * h)
                            project(h + 1, 1 - par, 0)
                        if i == 5:
                            if following:
                                project(h + 1, 1 - par, 1)
                            at.pe_sum(pe, u, 0)
                        if i == 7:
                            if following:
                                pe.wait_ge(y_lo, n0 + 2 * h + 4)
                            else:
                                pe.wait_ge(cat_biased, n0 + 2 * h)
                            post(h, par, 0)

                at.pe_x_turn(pe, b, ident)
                at.pe_xm_turn(pe, 2 * b, ident)
                project(0, 0, 0)
                project(0, 0, 1)
                pe.wait_ge(at.xm_ready, 2 * b + 1)
                heads_of(pe.Fori, unit)
                u = u0 + (HEADS - 1)
                at.pe_turn(pe, u, 6, ident)
                at.pe_turn(pe, u, 7, ident)
                at.pe_sum(pe, u, 1)
                pe.wait_ge(cat_biased, n0 + 2 * HEADS - 1)
                post(HEADS - 1, 1, 1)
                for q in range(2):
                    pe.wait_ge(cat_done, n0 + 2 * HEADS - 1 + q + 1)
                    for h in range(HEADS):
                        last = nc.tensor.matmul(at.ps_score[0][:, q * HALF:(q + 1) * HALF],
                                                wo[:, h].rearrange("p c f -> p (c f)"),
                                                cat[:, h, q * HALF:(q + 1) * HALF],
                                                start=(h == 0), stop=(h == HEADS - 1))
                last.then_inc(at.xt_ready, 1)
                at.pe_xm_turn(pe, 2 * b + 1, ident)
                pe.wait_ge(at.xm_ready, 2 * b + 2)
                u = u0 + HEADS
                for i in range(NT + 2):
                    if i < NT:
                        score(u, i, at.xhl)
                    if i >= 2:
                        at.pe_turn(pe, u, i - 2, ident)
                    if i == 5:
                        at.pe_sum(pe, u, 0)
                at.pe_sum(pe, u, 1)
                for q in range(2):
                    pe.wait_ge(at.copied, 2 * u + q + 2)
                    if q == 0:
                        pe.wait_ge(cat_biased, n0 + 2 * HEADS)
                    else:
                        pe.wait_ge(out_sum, 6 * b + 1)
                    for i in range(TPH):
                        last = nc.tensor.matmul(at.ps_post[:, i * F:(i + 1) * F],
                                                at.z[q][:, i * P:(i + 1) * P], fold[:], start=True, stop=True)
                    last.then_inc(at.posted, 1)

        @block.vector
        def _(dve):
            at.dve_credits(dve)
            dve.sem_inc(cat_done, 1)
            with dve.Fori(0, B) as b:
                u0, n0 = b * UNITS, b * (2 * HEADS)

                def tile(u, i, prev):
                    at.dve_mask_add(dve, u, i, mask[:, i, :])
                    if i >= 1:
                        at.dve_invert(dve, u, i - 1)
                    elif prev:
                        at.dve_invert(dve, u - 1, NT - 1)
                    for j in range(2):
                        if i >= 2:
                            at.dve_low(dve, u, i - 2, j)
                        elif prev:
                            at.dve_low(dve, u - 1, i + 6, j)

                def split_y(h, par, q):
                    dve.wait_ge(y_hi, n0 + 2 * h + q + 1)
                    c = slice(q * HALF, (q + 1) * HALF)
                    nc.vector.tensor_tensor(y[par][F:P, c], at.ps_post[F:P, :], y[par][F:P, c].bitcast(F32),
                                            ALU.subtract).then_inc(y_lo, 1)

                def leaky(h, q):
                    dve.wait_ge(cat_biased, n0 + 2 * h + q + 1)
                    nc.vector.scalar_tensor_tensor(
                        out=cat[:, bass.ds(h, 1), q * HALF:(q + 1) * HALF].rearrange("p o n -> p (o n)"),
                        in0=biased, scalar=0.01, in1=biased, op0=ALU.mult, op1=ALU.max)\
                        .then_inc(cat_done, 1)

                def unit(h, par, prev, following):
                    u = u0 + h
                    for i in range(NT):
                        tile(u, i, prev)
                        if i == 1 and prev:
                            at.dve_copy(dve, u - 1, 1)
                        if i == 3 and prev:
                            leaky(h - 1, 1)
                        if i == 4 and following:
                            split_y(h + 1, 1 - par, 0)
                        if i == 5:
                            if following:
                                split_y(h + 1, 1 - par, 1)
                            at.dve_copy(dve, u, 0)
                        if i == 7:
                            leaky(h, 0)

                at.dve_xll(dve, 2 * b)
                at.dve_xm(dve, 2 * b)
                split_y(0, 0, 0)
                split_y(0, 0, 1)
                heads_of(dve.Fori, unit)

                def tail(u):
                    at.dve_invert(dve, u, NT - 1)
                    for i in (6, 7):
                        for j in range(2):
                            at.dve_low(dve, u, i, j)
                    at.dve_copy(dve, u, 1)

                tail(u0 + (HEADS - 1))
                leaky(HEADS - 1, 1)
                at.dve_xll(dve, 2 * b + 1)
                at.dve_xm(dve, 2 * b + 1)
                u = u0 + HEADS
                for i in range(NT):
                    tile(u, i, False)
                    if i == 5:
                        at.dve_copy(dve, u, 0)
                tail(u)
                for q in range(2):
                    dve.wait_ge(at.posted, 2 * u + q + 3)
                    nc.vector.tensor_tensor(last_act, at.ps_post[:, 0:TPH * F].rearrange("p (i f) -> p i f", f=F),
                                            bout[:].unsqueeze(1).broadcast_to([P, TPH, F]), ALU.add)\
                        .then_inc(out_sum, 1)
                    dve.wait_ge(out_sum, 6 * b + 3 * q + 1)
                    nc.vector.scalar_tensor_tensor(out=last_act, in0=last_act, scalar=0.01,
                                                   in1=last_act, op0=ALU.mult, op1=ALU.max)\
                        .then_inc(out_sum, 1)
                    dve.wait_ge(out_sum, 6 * b + 3 * q + 2)
                    rows = x[:, bass.ds(b * NT + q * TPH, TPH), :]
                    nc.vector.tensor_tensor(rows, rows, last_act, ALU.add).then_inc(out_sum, 1)
                    dve.wait_ge(out_sum, 6 * b + 3 * q + 3)

        @block.scalar
        def _(act):
            with act.Fori(0, B) as b:
                u0, n0 = b * UNITS, b * (2 * HEADS)

                def tile(u, i, prev):
                    at.act_exp(act, u, i)
                    for j in range(2):
                        if i >= 2:
                            at.act_high(act, u, i - 2, j)
                        elif prev:
                            at.act_high(act, u - 1, i + 6, j)

                def high_y(h, par, q):
                    act.wait_ge(projected, n0 + 2 * h + q + 1)
                    nc.scalar.activation(y[par][:, q * HALF:(q + 1) * HALF], at.ps_post[:], ACT.Copy)\
                        .then_inc(y_hi, 1)

                def bias(h, par, q):
                    act.wait_ge(at.posted, 2 * u0 + 2 * h + q + 3)
                    act.wait_ge(cat_done, n0 + 2 * h + q + 1)
                    nc.scalar.activation(biased, at.ps_post[:], ACT.Identity, bias=bs[par][:, 0:1])\
                        .then_inc(cat_biased, 1)

                def unit(h, par, prev, following):
                    u = u0 + h
                    for i in range(NT):
                        tile(u, i, prev)
                        if i == 3 and prev:
                            bias(h - 1, 1 - par, 1)
                        if i == 4 and following:
                            high_y(h + 1, 1 - par, 0)
                        if i == 5 and following:
                            high_y(h + 1, 1 - par, 1)
                        if i == 7:
                            bias(h, par, 0)

                at.act_xhh(act, 2 * b)
                at.act_xhl(act, 2 * b)
                high_y(0, 0, 0)
                high_y(0, 0, 1)
                heads_of(act.Fori, unit)

                def tail(u):
                    for i in (6, 7):
                        for j in range(2):
                            at.act_high(act, u, i, j)

                tail(u0 + (HEADS - 1))
                bias(HEADS - 1, 1, 1)
                at.act_xhh(act, 2 * b + 1)
                at.act_xhl(act, 2 * b + 1)
                u = u0 + HEADS
                for i in range(NT):
                    tile(u, i, False)
                tail(u)

        @block.gpsimd
        def _(pool):
            with pool.Fori(0, B) as b:
                u0, n0 = b * UNITS, b * (2 * HEADS)

                def stage(h, par):
                    for out, src in ((gs[par][:], g[:, bass.ds(h, 1), :].bitcast(F32).rearrange("p o c -> p (o c)")),
                                     (ws[par][:], ww[:, bass.ds(h, 1), :].rearrange("p o c -> p (o c)")),
                                     (bs[par][:], bcol[:, bass.ds(h, 1)])):
                        nc.gpsimd.tensor_copy(out, src).then_inc(staged, 1)

                def unit(h, par, prev, following):
                    u = u0 + h
                    for i in range(NT):
                        at.pool_norm(pool, u, i)
                        if i == 2 and following:
                            if prev:
                                pool.wait_ge(cat_biased, n0 + 2 * h)
                                pool.sem_inc(at.pool_passed, 1)
                            stage(h + 1, 1 - par)

                at.pool_pair(pool, b, hx)
                stage(0, 0)
                heads_of(pool.Fori, unit)
                for i in range(NT):
                    at.pool_norm(pool, u0 + HEADS, i)


def edge_layer(nc, ctx, B, x, hx, pairs, ident, name, W, a, bias):
    sb = lambda n, s, d=F32: ctx.enter_context(nc.sbuf_tensor(f"{name}_{n}", s, d))
    sem = lambda n: nc.alloc_semaphore(f"{name}_{n}")
    weighted = bias is not None
    SLOPE = 0.2
    at = Attention(nc, ctx, name)
    given = sb("given", [P, P])
    other = sb("other", [P, P])
    acol = sb("acol", [F, 2])
    arep = sb("arep", [F, 2, P])
    dst = sb("dst", [P, P], F32R)
    src_hi, src_lo = sb("src_hi", [P, P], F32R), sb("src_lo", [P, P], F32R)
    brow = sb("brow", [P, F])
    loaded, spread, turned, copied, mixed, split = (
        sem(n) for n in ("loaded", "spread", "w_turned", "w_copied", "mixed", "split"))
    loads = 5 if weighted else 4
    a_flat = a.rearrange("(c f) o -> f (c o)", f=F) if weighted else a.rearrange("(c f) -> f c", f=F)

    with nc.Block() as block:
        @block.sync
        def _(sp):
            for c in range(2):
                to = given[c * F:(c + 1) * F, 0:F] if weighted else given[0:F, c * F:(c + 1) * F]
                sp.dma_start(to, W).then_inc(loaded, 16)
            with nc.allow_non_contiguous_dma(reason="128 numbers"):
                for c in range(2):
                    sp.dma_start(acol[:, c:c + 1], a_flat[:, c:c + 1]).then_inc(loaded, 16)
            if weighted:
                sp.dma_start(brow[:], bias.rearrange("(o f) -> o f", o=1).broadcast_to([P, F])).then_inc(loaded, 16)
            sp.wait_ge(loaded, 16 * loads)

        @block.tensor
        def _(pe):
            pe.wait_ge(loaded, 16 * loads)
            if weighted:
                nc.tensor.transpose(at.ps_post[0:F, 0:P], given[:, 0:F], ident[:]).then_inc(turned, 1)
            else:
                nc.tensor.transpose(at.ps_post[:, 0:F], given[0:F, :], ident[0:F, 0:F]).then_inc(turned, 1)
            pe.wait_ge(copied, 1)
            pe.wait_ge(spread, 1)
            lhs = other[0:F, :] if weighted else given[0:F, :]
            nc.tensor.matmul(at.ps_z[:, 0:2 * P], lhs, arep[:].rearrange("p c n -> p (c n)"),
                             start=True, stop=True).then_inc(mixed, 1)

        @block.vector
        def _(dve):
            dve.wait_ge(loaded, 16 * loads)
            nc.vector.tensor_copy(arep[:], acol[:].unsqueeze(2).broadcast_to([F, 2, P])).then_inc(spread, 1)
            dve.wait_ge(turned, 1)
            if weighted:
                nc.vector.tensor_copy(other[0:F, :], at.ps_post[0:F, 0:P]).then_inc(copied, 1)
            else:
                nc.vector.tensor_copy(other[:, 0:F], at.ps_post[:, 0:F]).then_inc(copied, 1)
            dve.wait_ge(split, 2)
            nc.vector.tensor_tensor(src_lo[:], at.ps_z[:, 0:P], src_hi[:].bitcast(F32), ALU.subtract).then_inc(split, 1)
            nc.vector.tensor_tensor(dst[F:P, :], at.ps_z[F:P, P:2 * P], dst[F:P, :].bitcast(F32),
                                    ALU.subtract).then_inc(split, 1)

        @block.scalar
        def _(act):
            act.wait_ge(mixed, 1)
            nc.scalar.activation(src_hi[:], at.ps_z[:, 0:P], ACT.Copy).then_inc(split, 1)
            nc.scalar.activation(dst[:], at.ps_z[:, P:2 * P], ACT.Copy).then_inc(split, 1)

    wst = given[:, 0:F] if weighted else other[:, 0:F]
    d1, d02 = sb("d1", [P, N]), sb("d02", [P, N])
    s08, s02 = sb("s08", [P, NT, 2]), sb("s02", [P, NT, 2])
    e, new = sb("e", [P, TPH, F]), sb("new", [P, TPH, F])
    projected, termed, leaned, shifted, peaked, exped_out, out_step = (
        sem(n) for n in ("projected", "termed", "leaned", "shifted", "peaked", "exped_out", "out_step"))
    OUT = 2 if weighted else 3

    with nc.Block() as block:
        @block.tensor
        def _(pe):
            at.pe_credits(pe)
            with pe.Fori(0, B) as b:
                at.pe_x_turn(pe, b, ident)
                at.pe_xm_turn(pe, b, ident)
                for q in range(2):
                    c = slice(q * HALF, (q + 1) * HALF)
                    nc.tensor.matmul(at.ps_score[0][:, c], dst[:], at.xhh[:, c], start=True, stop=False)
                    nc.tensor.matmul(at.ps_score[0][:, c], dst[:], at.xll[:, c], start=False, stop=True)\
                        .then_inc(projected, 1)
                for i in range(NT):
                    for part in (src_hi, src_lo):
                        last = nc.tensor.matmul(at.ps_post[:, 2 * i:2 * i + 2], at.xhl[:, i * P:(i + 1) * P],
                                                part[:, 0:2], start=(part is src_hi), stop=(part is src_lo))
                last.then_inc(projected, 1)
                pe.wait_ge(at.xm_ready, b + 1)
                for i in range(NT):
                    at.pe_turn(pe, b, i, ident)
                    if i == 5:
                        at.pe_sum(pe, b, 0)
                at.pe_sum(pe, b, 1)
                for q in range(2):
                    pe.wait_ge(at.copied, 2 * b + q + 2)
                    if q == 1:
                        pe.wait_ge(out_step, 2 * OUT * b + OUT)
                    for i in range(TPH):
                        last = nc.tensor.matmul(at.ps_post[:, i * F:(i + 1) * F],
                                                at.z[q][:, i * P:(i + 1) * P], wst, start=True, stop=True)
                    last.then_inc(at.posted, 1)

        @block.vector
        def _(dve):
            at.dve_credits(dve)
            with dve.Fori(0, B) as b:
                def lean(i):
                    dve.wait_ge(at.turned, 16 * b + 2 * i + 2)
                    nc.vector.scalar_tensor_tensor(out=at.prob[i % 4][:], in0=d1[:], scalar=s08[:, i, 0:1],
                                                   in1=d02[:], op0=ALU.add, op1=ALU.max).then_inc(leaned, 1)

                def peak(i):
                    p, c = at.prob[i % 4][:], slice(i % 4, i % 4 + 1)
                    if weighted:
                        dve.wait_ge(shifted, 8 * b + i + 1)
                        dve.sem_inc(at.dve_passed, 1)
                        nc.vector.tensor_tensor_reduce(out=p, in0=p, in1=pairs[:, i, :], scale=1.0, scalar=-3.0e38,
                                                       op0=ALU.mult, op1=ALU.max,
                                                       accum_out=at.negmax[:, c]).then_inc(peaked, 1)
                        dve.wait_ge(peaked, 8 * b + i + 1)
                        nc.vector.tensor_scalar(at.negmax[:, c], at.negmax[:, c], -1.0, None,
                                                ALU.mult).then_inc(at.masked, 1)
                    else:
                        dve.wait_ge(leaned, 8 * b + i + 1)
                        dve.sem_inc(at.dve_passed, 1)
                        nc.vector.tensor_tensor_reduce(out=p, in0=p, in1=pairs[:, i, :], scale=-1.0, scalar=3.0e38,
                                                       op0=ALU.add, op1=ALU.min,
                                                       accum_out=at.negmax[:, c]).then_inc(at.masked, 1)

                at.dve_xll(dve, b)
                at.dve_xm(dve, b)
                dve.wait_ge(termed, 4 * b + 4)
                lean(0)
                for i in range(NT + 3):
                    if i + 1 < NT:
                        lean(i + 1)
                    if i < NT:
                        peak(i)
                    if i >= 1 and i <= NT:
                        at.dve_invert(dve, b, i - 1)
                    if i >= 3:
                        for j in range(2):
                            at.dve_low(dve, b, i - 3, j)
                    if i == 7:
                        at.dve_copy(dve, b, 0)
                at.dve_copy(dve, b, 1)
                for q in range(2):
                    step = 2 * OUT * b + OUT * q
                    v = at.ps_post[:, 0:TPH * F].rearrange("p (i f) -> p i f", f=F)
                    if weighted:
                        dve.wait_ge(at.posted, 2 * b + q + 3)
                        nc.vector.tensor_tensor(new[:], v, brow[:].unsqueeze(1).broadcast_to([P, TPH, F]),
                                                ALU.add).then_inc(out_step, 1)
                    else:
                        dve.wait_ge(exped_out, 2 * b + q + 1)
                        nc.vector.tensor_scalar(e[:], e[:], 1.0, -1.0, ALU.min, ALU.add).then_inc(out_step, 1)
                        dve.wait_ge(out_step, step + 1)
                        nc.vector.scalar_tensor_tensor(out=new[:].rearrange("p i f -> p (i f)"), in0=at.ps_post[:, 0:TPH * F], scalar=0.0,
                                                       in1=e[:].rearrange("p i f -> p (i f)"),
                                                       op0=ALU.max, op1=ALU.add).then_inc(out_step, 1)
                    dve.wait_ge(out_step, step + OUT - 1)
                    rows = x[:, bass.ds(b * NT + q * TPH, TPH), :]
                    nc.vector.tensor_tensor(rows, rows, new[:], ALU.add).then_inc(out_step, 1)
                    dve.wait_ge(out_step, step + OUT)

        @block.scalar
        def _(act):
            with act.Fori(0, B) as b:
                def exp(i):
                    act.wait_ge(at.masked, 8 * b + i + 3)
                    c = slice(i % 4, i % 4 + 1)
                    nc.scalar.activation(at.prob[i % 4][:], at.prob[i % 4][:], ACT.Exp, bias=at.negmax[:, c],
                                         scale=1.0 if weighted else -1.0,
                                         accum_out=at.rowsum[:, c]).then_inc(at.exped, 1)

                def shift(i):
                    act.wait_ge(leaned, 8 * b + i + 1)
                    nc.scalar.activation(at.prob[i % 4][:], at.prob[i % 4][:], ACT.Identity,
                                         bias=s02[:, i, 0:1]).then_inc(shifted, 1)

                at.act_xhh(act, b)
                at.act_xhl(act, b)
                act.wait_ge(projected, 3 * b + 3)
                nc.scalar.activation(d1[:], at.ps_score[0][:], ACT.Copy).then_inc(termed, 1)
                nc.scalar.activation(d02[:], at.ps_score[0][:], ACT.Copy, scale=SLOPE).then_inc(termed, 1)
                src = at.ps_post[:, 0:2 * NT].rearrange("p (i c) -> p i c", c=2)
                nc.scalar.activation(s08[:], src, ACT.Copy, scale=1.0 - SLOPE).then_inc(termed, 1)
                nc.scalar.activation(s02[:], src, ACT.Copy, scale=SLOPE).then_inc(termed, 1)
                if weighted:
                    act.wait_ge(termed, 4 * b + 4)
                    shift(0)
                for i in range(NT + 2):
                    if weighted and i + 1 < NT:
                        shift(i + 1)
                    if i < NT:
                        exp(i)
                    if i >= 2:
                        for j in range(2):
                            at.act_high(act, b, i - 2, j)
                if not weighted:
                    for q in range(2):
                        act.wait_ge(at.posted, 2 * b + q + 3)
                        if q == 1:
                            act.wait_ge(out_step, 2 * OUT * b + OUT)
                        nc.scalar.activation(e[:], at.ps_post[:, 0:TPH * F].rearrange("p (i f) -> p i f", f=F),
                                             ACT.Exp).then_inc(exped_out, 1)

        @block.gpsimd
        def _(pool):
            with pool.Fori(0, B) as b:
                at.pool_pair(pool, b, hx)
                for i in range(NT):
                    at.pool_norm(pool, b, i)


def load_adjacency(nc, adj, pairs):
    loaded, set_ones = nc.alloc_semaphore("adj_loaded"), nc.alloc_semaphore("adj_ones")
    with nc.Block() as block:
        @block.sync
        def _(sp):
            sp.dma_start(pairs[:], adj.rearrange("(k p) m -> p k m", p=P)).then_inc(loaded, 16)
            sp.wait_ge(loaded, 16)

        @block.gpsimd
        def _(pool):
            pool.wait_ge(loaded, 16)
            nc.gpsimd.affine_select(out=pairs[:], in_=pairs[:], compare_op=ALU.not_equal, fill=1.0, base=0,
                                    pattern=[[P, NT], [-1, N]], channel_multiplier=1).then_inc(set_ones, 1)


def build(nc, B, layers, x_in, adj, L0, L1, L2, L3, out):
    with ExitStack() as ctx:
        sb = lambda n, s, d=F32: ctx.enter_context(nc.sbuf_tensor(n, s, d))
        sem = lambda n: ctx.enter_context(nc.semaphore(n))
        x = sb("x", [P, B * NT, F])
        hx = sb("hx", [P, B * NT, F])
        mask = sb("mask", [P, NT, N], BF16)
        ident = sb("ident", [P, P])
        fold = sb("fold", [P, F])
        loaded, made, masked, stored = sem("loaded"), sem("made"), sem("mask_made"), sem("stored")
        with ExitStack() as own:
            adj_rows = own.enter_context(nc.sbuf_tensor("adj_rows", [P, NT, N], F32))
            with nc.Block() as block:
                @block.sync
                def _(sp):
                    sp.dma_start(x[:], x_in.rearrange("b (k p) f -> p (b k) f", p=P)).then_inc(loaded, 16)
                    sp.dma_start(adj_rows[:], adj.rearrange("(k p) m -> p k m", p=P)).then_inc(loaded, 16)
                    sp.wait_ge(loaded, 32)

                @block.gpsimd
                def _(pool):
                    nc.gpsimd.memset(ident[:], 0.0).then_inc(made, 1)
                    nc.gpsimd.memset(fold[:], 0.0).then_inc(made, 1)
                    pool.wait_ge(made, 2)
                    nc.gpsimd.affine_select(out=ident[:], in_=ident[:], compare_op=ALU.not_equal, fill=1.0,
                                            base=0, pattern=[[-1, P]], channel_multiplier=1).then_inc(made, 1)
                    for k, at in enumerate((0, -F)):
                        nc.gpsimd.affine_select(out=fold[:], in_=fold[:], compare_op=ALU.not_equal, fill=1.0,
                                                base=at, pattern=[[-1, F]], channel_multiplier=1).then_inc(made, 1)
                        pool.wait_ge(made, 4 + k)

                @block.vector
                def _(dve):
                    dve.wait_ge(loaded, 32)
                    nc.vector.tensor_scalar(mask[:], adj_rows[:], 0.0, MASKED, ALU.is_equal, ALU.mult).then_inc(masked, 1)
        def layer(k, norm_and_attend):
            if k not in layers:
                return
            with nc.cleanup_on_exit(), ExitStack() as own:
                norm_and_attend(own)

        def layer_0(own):
            with ExitStack() as norm:
                layer_norm_relu(nc, norm, B, x, hx, "ln0")
            layer0(nc, own, B, x, hx, ident, fold, adj, *L0)

        def layer_1(own):
            with ExitStack() as norm:
                layer_norm_relu(nc, norm, B, x, hx, "ln1")
            layer1(nc, own, B, x, hx, mask, ident, fold, *L1)

        def layer_2(own):
            with ExitStack() as norm:
                layer_norm_relu(nc, norm, B, x, hx, "ln2")
            edges = own.enter_context(nc.sbuf_tensor("edges", [P, NT, N], F32))
            load_adjacency(nc, adj, edges)
            edge_layer(nc, own, B, x, hx, edges, ident, "l2", *L2)

        def layer_3(own):
            with ExitStack() as norm:
                layer_norm_relu(nc, norm, B, x, hx, "ln3")
            edge_layer(nc, own, B, x, hx, mask, ident, "l3", *L3, None)

        for k, norm_and_attend in enumerate((layer_0, layer_1, layer_2, layer_3)):
            layer(k, norm_and_attend)
        with nc.Block() as block:
            @block.sync
            def _(sp):
                sp.dma_start(out.rearrange("b (k p) f -> p (b k) f", p=P), x[:]).then_inc(stored, 16)
                sp.wait_ge(stored, 16)


_INS = ['x', 'adj', 'L0_gnn_H', 'L0_gnn_W', 'L0_gnn_W_ind', 'L0_gnn_a_node', 'L0_gnn_a_gn', 'L0_gnn_a_ge',
        'L0_gnn_fcW', 'L0_gnn_fcb', 'L0_gnn_av', 'L1_gnn_Wh', 'L1_gnn_bh', 'L1_gnn_W_out', 'L1_gnn_b_out',
        'L2_gnn_weight', 'L2_gnn_a', 'L2_gnn_bias', 'L3_gnn_W', 'L3_gnn_a']
_OUTS = [((8, 1024, 64), 'float32')]


def kernel(**inputs):
    import numpy as _np
    import concourse.bacc as _bacc
    from concourse import mybir as _mybir
    from concourse.bass_utils import run_bass_kernel_spmd as _run

    nc = _bacc.Bacc("TRN2", target_bir_lowering=False, num_devices=1)
    arrays, args = {}, {}
    for name in _INS:
        arrays[f"in_{name}_dram"] = _np.ascontiguousarray(inputs[name])
        args[name] = nc.dram_tensor(f"in_{name}_dram", arrays[f"in_{name}_dram"].shape,
                                    _mybir.dt.from_np(arrays[f"in_{name}_dram"].dtype), kind="ExternalInput").ap()
    shape, dtype = _OUTS[0]
    out = nc.dram_tensor("out_0_dram", shape, _mybir.dt.from_np(_np.dtype(dtype)), kind="ExternalOutput").ap()
    of_layer = [[args[n] for n in _INS if n.startswith(f"L{k}_")] for k in range(4)]
    build(nc, shape[0], (0, 1, 2, 3), args["x"], args["adj"], *of_layer, out)
    r = _run(nc, [arrays], core_ids=[0])
    return r.results[0]["out_0_dram"]
```

```python
from contextlib import ExitStack

import concourse.bass as bass
from concourse import mybir

ALU = mybir.AluOpType
ACT = mybir.ActivationFunctionType
AX = mybir.AxisListType
F32 = mybir.dt.float32
F32R = mybir.dt.float32r
BF16 = mybir.dt.bfloat16

P = 128
N = 1024
F = 64
NT = N // P
HALF = 512
TPH = HALF // P
HEADS = 8
HID = 128
MASKED = -1.0e16
EPS = 1e-5


def layer_norm_relu(nc, ctx, B, x, hx, name):
    rows = B * NT
    stat = ctx.enter_context(nc.sbuf_tensor(f"{name}_stat", [P, 4, rows], F32))
    sq = ctx.enter_context(nc.sbuf_tensor(f"{name}_sq", [P, rows, F], F32))
    total, mean, var, rstd = (stat[:, i, :] for i in range(4))
    step = nc.alloc_semaphore(f"{name}_dve_step")
    squared = nc.alloc_semaphore(f"{name}_squared")
    rooted = nc.alloc_semaphore(f"{name}_rooted")

    def over_features(col):
        return col.unsqueeze(2).broadcast_to([P, rows, F])

    with nc.Block() as block:
        @block.vector
        def _(dve):
            nc.vector.tensor_reduce(total, x[:], AX.X, ALU.add).then_inc(step, 1)
            dve.wait_ge(step, 1)
            nc.vector.tensor_scalar(mean, total, 1.0 / F, None, ALU.mult).then_inc(step, 1)
            dve.wait_ge(step, 2)
            nc.vector.tensor_tensor(hx[:], x[:], over_features(mean), ALU.subtract).then_inc(step, 1)
            dve.wait_ge(squared, 1)
            nc.vector.tensor_reduce(total, sq[:], AX.X, ALU.add).then_inc(step, 1)
            dve.wait_ge(step, 4)
            nc.vector.tensor_scalar(var, total, 1.0 / F, EPS, ALU.mult, ALU.add).then_inc(step, 1)
            dve.wait_ge(rooted, 1)
            nc.vector.reciprocal(rstd, mean).then_inc(step, 1)
            dve.wait_ge(step, 6)
            nc.vector.scalar_tensor_tensor(out=hx[:], in0=hx[:], scalar=0.0, in1=over_features(rstd),
                                           op0=ALU.max, op1=ALU.mult).then_inc(step, 1)

        @block.scalar
        def _(act):
            act.wait_ge(step, 3)
            nc.scalar.activation(sq[:], hx[:], ACT.Square).then_inc(squared, 1)
            act.wait_ge(step, 5)
            nc.scalar.activation(mean, var, ACT.Sqrt).then_inc(rooted, 1)


def layer0(nc, ctx, B, x, hx, ident, fold, adj, H, W, W_ind, a_node, a_gn, a_ge, fcW, fcb, av):
    sb = lambda n, s, d=F32: ctx.enter_context(nc.sbuf_tensor(f"l0_{n}", s, d))
    sem = lambda n: nc.alloc_semaphore(f"l0_{n}")
    E = H.shape[1]
    PAIRS = E // 2
    ps_a, ps_b, ps_c, ps_d = (ctx.enter_context(nc.psum_tensor(f"l0_ps_{n}", [P, N], F32)) for n in "abcd")
    halves = [slice(q * HALF, (q + 1) * HALF) for q in range(2)]

    adj_t = sb("adj_t", [P, NT, N])
    mask_rows = sb("mask_rows", [P, NT, E])
    mask_cols = sb("mask_cols", [E, N])
    w_st = sb("w_st", [P, P], F32R)
    wi_st = sb("wi_st", [P, P], F32R)
    v_st = sb("v_st", [P, 2, P], F32R)
    fcw, fcb_col, age_col = sb("fcw", [F, P]), sb("fcb_col", [P, 1]), sb("age_col", [F, 1])
    av_rep, av_neg = sb("av_rep", [P, P]), sb("av_neg", [P, P])
    ones = sb("ones", [P, P])
    fold2 = sb("fold2", [P, 2, F])

    with ExitStack() as own:
        mine = lambda n, s, d=F32: own.enter_context(nc.sbuf_tensor(f"l0_{n}", s, d))
        rows = mine("rows", [P, NT, N])
        h_rows = mine("h_rows", [P, NT, E])
        w_in, wi_in = mine("w_in", [P, 2, F]), mine("wi_in", [P, 2, F])
        w_t = mine("w_t", [F, P])
        cols = mine("cols", [F, 2])
        a_rep = mine("a_rep", [F, 2, P])
        av_col = mine("av_col", [P, 1])
        deg = mine("deg", [P, NT, 3])
        names = ("loaded adj_in summed floored inverted scaled hmask spread w_turned w_copied v_ready v_hi w_hi "
                 "w_lo turned untied hm_turned hm_copied const")
        S = {n: nc.alloc_semaphore(f"l0s_{n}") for n in names.split()}
        SMALL = 15 * 16
        with nc.Block() as block:
            @block.sync
            def _(sp):
                sp.dma_start(rows[:], adj.rearrange("(k p) m -> p k m", p=P)).then_inc(S["adj_in"], 16)
                sp.dma_start(h_rows[:], H.rearrange("(k p) e -> p k e", p=P)).then_inc(S["loaded"], 16)
                for to, src in ((w_in, W), (wi_in, W_ind)):
                    for r in range(2):
                        for c in range(2):
                            sp.dma_start(to[r * F:(r + 1) * F, c, :], src).then_inc(S["loaded"], 16)
                sp.dma_start(fcw[:], fcW).then_inc(S["loaded"], 16)
                with nc.allow_non_contiguous_dma(reason="a few hundred numbers"):
                    col = lambda v: v.rearrange("(f o) -> f o", o=1)
                    for to, src in ((fcb_col[:], fcb), (age_col[:], a_ge), (cols[:, 0:1], a_node),
                                    (cols[:, 1:2], a_gn), (av_col[:], av)):
                        sp.dma_start(to, col(src)).then_inc(S["loaded"], 16)
                sp.wait_ge(S["loaded"], SMALL)
                sp.wait_ge(S["adj_in"], 16)

            @block.gpsimd
            def _(pool):
                nc.gpsimd.memset(ones[:], 1.0).then_inc(S["const"], 1)
                nc.gpsimd.tensor_copy(fold2[:], fold[:].unsqueeze(1).broadcast_to([P, 2, F])).then_inc(S["const"], 1)

            @block.vector
            def _(dve):
                dve.wait_ge(S["loaded"], SMALL)
                nc.vector.tensor_copy(a_rep[:], cols[:].unsqueeze(2).broadcast_to([F, 2, P])).then_inc(S["spread"], 1)
                nc.vector.tensor_copy(av_rep[:], av_col[:].broadcast_to([P, P])).then_inc(S["spread"], 1)
                nc.vector.tensor_scalar(av_neg[:], av_col[:].broadcast_to([P, P]), -1.0, None,
                                        ALU.mult).then_inc(S["spread"], 1)
                nc.vector.tensor_scalar(mask_rows[:], h_rows[:], 0.0, MASKED, ALU.is_le, ALU.mult)\
                    .then_inc(S["hmask"], 1)
                dve.wait_ge(S["w_turned"], 1)
                nc.vector.tensor_copy(w_t[:], ps_a[0:F, 0:P]).then_inc(S["w_copied"], 1)
                dve.wait_ge(S["w_hi"], 2)
                for k, (to, src) in enumerate(((w_st, w_in), (wi_st, wi_in))):
                    nc.vector.tensor_tensor(to[F:P, :], src[F:P].rearrange("p c f -> p (c f)"),
                                            to[F:P, :].bitcast(F32), ALU.subtract).then_inc(S["w_lo"], 1)
                dve.wait_ge(S["v_hi"], 1)
                nc.vector.tensor_tensor(v_st[F:P], ps_b[F:P, 0:2 * P].rearrange("p (c n) -> p c n", n=P),
                                        v_st[F:P].bitcast(F32), ALU.subtract).then_inc(S["w_lo"], 1)
                dve.wait_ge(S["hm_turned"], 1)
                nc.vector.tensor_copy(mask_cols[:], ps_d[0:E, :]).then_inc(S["hm_copied"], 1)
                dve.wait_ge(S["adj_in"], 16)
                nc.vector.tensor_reduce(deg[:, :, 0], rows[:], AX.X, ALU.add).then_inc(S["summed"], 1)
                dve.wait_ge(S["summed"], 1)
                nc.vector.tensor_scalar(deg[:, :, 1], deg[:, :, 0], 1.0, None, ALU.max).then_inc(S["floored"], 1)
                dve.wait_ge(S["floored"], 1)
                nc.vector.reciprocal(deg[:, :, 2], deg[:, :, 1]).then_inc(S["inverted"], 1)
                dve.wait_ge(S["inverted"], 1)
                for k in range(NT):
                    nc.vector.tensor_scalar(rows[:, k, :], rows[:, k, :], deg[:, k, 2:3], None, ALU.mult)\
                        .then_inc(S["scaled"], 1)
                for m in range(NT):
                    if m % 2 == 0:
                        dve.wait_ge(S["turned"], m + 1)
                        nc.vector.tensor_copy(adj_t[:, m, :], ps_a[:]).then_inc(S["untied"], 1)

            @block.scalar
            def _(act):
                act.wait_ge(S["loaded"], SMALL)
                for to, src in ((w_st, w_in), (wi_st, wi_in)):
                    nc.scalar.activation(to[:], src[:].rearrange("p c f -> p (c f)"), ACT.Copy).then_inc(S["w_hi"], 1)
                act.wait_ge(S["v_ready"], 1)
                nc.scalar.activation(v_st[:], ps_b[:, 0:2 * P].rearrange("p (c n) -> p c n", n=P), ACT.Copy)\
                    .then_inc(S["v_hi"], 1)
                for m in range(1, NT, 2):
                    act.wait_ge(S["turned"], m + 1)
                    nc.scalar.activation(adj_t[:, m, :], ps_c[:], ACT.Copy).then_inc(S["v_hi"], 1)

            @block.tensor
            def _(pe):
                pe.wait_ge(S["loaded"], SMALL)
                nc.tensor.transpose(ps_a[0:F, 0:P], w_in[:, 0, :], ident[:]).then_inc(S["w_turned"], 1)
                pe.wait_ge(S["hmask"], 1)
                for k in range(NT):
                    last = nc.tensor.transpose(ps_d[0:E, k * P:(k + 1) * P], mask_rows[:, k, :], ident[:])
                last.then_inc(S["hm_turned"], 1)
                pe.wait_ge(S["w_copied"], 1)
                pe.wait_ge(S["spread"], 1)
                nc.tensor.matmul(ps_b[:, 0:2 * P], w_t[:], a_rep[:].rearrange("p c n -> p (c n)"),
                                 start=True, stop=True).then_inc(S["v_ready"], 1)
                pe.wait_ge(S["scaled"], NT)
                for m in range(NT):
                    bank = ps_a if m % 2 == 0 else ps_c
                    if m >= 2:
                        pe.wait_ge(S["untied"] if m % 2 == 0 else S["v_hi"], m // 2 + m % 2)
                    for k in range(NT):
                        last = nc.tensor.transpose(bank[:, k * P:(k + 1) * P], rows[:, k, m * P:(m + 1) * P], ident[:])
                    last.then_inc(S["turned"], 1)

    pair = sb("pair", [P, NT, 2, F])
    xhh, xll = sb("xhh", [P, N], F32R), sb("xll", [P, N], F32R)
    h_t = sb("h_t", [P, N])
    h_n = sb("h_n", [P, NT, P])
    al = sb("al", [E, N])
    al_t = sb("al_t", [P, NT, E])
    al_stat = sb("al_stat", [E, 3])
    agg2, nagg2 = sb("agg2", [P, PAIRS]), sb("nagg2", [P, PAIRS])
    agg_td = sb("agg_td", [F, 2, E])
    agg_e = sb("agg_e", [E, P])
    he_e, he = sb("he_e", [F, E]), sb("he", [F, E])
    u_t = sb("u_t", [P, E])
    age = sb("age", [P, 1])
    beta = sb("beta", [P, N])
    bhl, chl = sb("bhl", [P, N], F32R), sb("chl", [P, N], F32R)
    lc = sb("lc", [P, NT, E])
    lc_stat = sb("lc_stat", [P, 3, NT])
    c_n = sb("c_n", [P, NT, 2, E])
    m1, c1 = sb("m1", [E, N]), sb("c1", [E, N])
    hlin = sb("hlin", [P, N])
    zc = [sb(f"zc{i}", [P, N]) for i in range(2)]
    r = [sb(f"r{i}", [P, N]) for i in range(4)]
    ex = [sb(f"ex{i}", [P, N]) for i in range(2)]
    u = [sb(f"u{i}", [P, N]) for i in range(2)]
    sel_b, sel_c = ([sb(f"sel_{n}{i}", [P, 2, F], F32R) for i in range(2)] for n in "bc")
    g_t, ind = beta, h_t
    xw = h_n
    tg, ti = zc[0], zc[1]
    mix = r[0]
    res = r[1]

    names = ("paired xt hh ll ht ht_out v hg hn hn_out v02 lean peak alex alinv alnorm al_turned al_out agg "
             "agg_out he_ex he_min he_done age ut ut_out se age_out tanh_b beta bhi blo lc mx lcs lce lcsum lcinv c_n "
             "c_turned chi m1 c1 clo lin bsum hlin g xw xw_out ind ind_out sg sg_out si si_out diff wt wt2 d dw "
             "res res_t added passed pe_passed")
    S = {n: sem(n) for n in names.split()}
    names = "selb selc b_in zc_done r_done ex_done t_done c_in u_done folded"
    T = {n: sem(n) for n in names.split()}
    LAG = 3

    with nc.Block() as block:
        def pairs_of(loop, step):
            ends = lambda s: lambda k: 0 <= s - k < PAIRS
            for s in range(4):
                step(s, s % 4, ends(s))
            with loop(4, PAIRS - 7, 4) as s0:
                for j in range(4):
                    step(s0 + j, j, lambda k: True)
            for s in range(PAIRS - 4, PAIRS + LAG + 1):
                step(s, s % 4, ends(s))

        @block.gpsimd
        def _(pool):
            with pool.Fori(0, B) as b:
                nc.gpsimd.tensor_copy(pair[:], hx[:, bass.ds(b * NT, NT), :].unsqueeze(2)
                                      .broadcast_to([P, NT, 2, F])).then_inc(S["paired"], 1)

                def step(s, j, has):
                    if has(1):
                        pool.wait_ge(T["ex_done"], PAIRS * b + s)
                        nc.gpsimd.tensor_tensor(r[(j - 1) % 4][:], r[(j - 1) % 4][:], ex[(j - 1) % 2][:], ALU.add)\
                            .then_inc(T["t_done"], 1)

                pairs_of(pool.Fori, step)

        @block.tensor
        def _(pe):
            with pe.Fori(0, B) as b:
                after = lambda name: pe.wait_ge(S[name], b + 1)

                def product(out, lhs_t, parts):
                    for c in halves:
                        for part in parts:
                            last = nc.tensor.matmul(out[:, c], lhs_t, part[:, c], start=(part is parts[0]),
                                                    stop=(part is parts[-1]))
                    return last

                def rows_of(out, weights):
                    for k in range(NT):
                        c = slice(k * P, (k + 1) * P)
                        for part in (xhh, xll):
                            last = nc.tensor.matmul(out[:, c], part[:, c], weights[:], start=(part is xhh),
                                                    stop=(part is xll))
                    return last

                after("paired")
                for k in range(NT):
                    last = nc.tensor.transpose(ps_a[:, k * P:(k + 1) * P],
                                               pair[:, k].rearrange("p c f -> p (c f)"), ident[:])
                last.then_inc(S["xt"], 1)
                after("ll")
                product(ps_a, v_st[:, 0], (xhh, xll)).then_inc(S["v"], 1)
                rows_of(ps_d, w_st).then_inc(S["hn"], 1)
                product(ps_b, w_st[:], (xhh, xll)).then_inc(S["ht"], 1)
                product(ps_c, v_st[:, 1], (xhh, xll)).then_inc(S["hg"], 1)
                after("alnorm")
                pe.sem_inc(S["pe_passed"], 1)
                for k in range(NT):
                    last = nc.tensor.transpose(ps_a[:, k * E:(k + 1) * E], al[:, k * P:(k + 1) * P], ident[0:E, 0:E])
                last.then_inc(S["al_turned"], 1)
                after("al_out")
                after("hn_out")
                after("ht_out")
                for k in range(NT):
                    nc.tensor.matmul(ps_b[:, 0:E], h_n[:, k, :], al_t[:, k, :], start=(k == 0), stop=(k == NT - 1))
                for k in range(NT):
                    last = nc.tensor.matmul(ps_b[0:E, HALF:HALF + P], al_t[:, k, :], h_n[:, k, :],
                                            start=(k == 0), stop=(k == NT - 1))
                last.then_inc(S["agg"], 1)
                after("agg_out")
                nc.tensor.matmul(ps_a[:, 0:1], agg_td[:].rearrange("p c e -> p (c e)"), age_col[:],
                                 start=True, stop=True).then_inc(S["age"], 1)
                after("he_done")
                nc.tensor.matmul(ps_a[:, HALF:HALF + E], fcw[:], he[:], start=True, stop=True).then_inc(S["ut"], 1)
                after("ut_out")
                after("age_out")
                nc.tensor.matmul(ps_a[:, 0:E], av_rep[:], u_t[:], start=True, stop=True).then_inc(S["se"], 1)
                after("c_n")
                for k in range(NT):
                    last = nc.tensor.transpose(ps_d[:, k * P:(k + 1) * P],
                                               c_n[:, k].rearrange("p c e -> p (c e)"), ident[:])
                last.then_inc(S["c_turned"], 1)
                after("m1")
                product(ps_a, ones[0:E, :], (m1,)).then_inc(S["bsum"], 1)
                after("c1")
                after("tanh_b")
                for c in halves:
                    last = nc.tensor.matmul(ps_c[:, c], agg_e[:], c1[:, c], start=True, stop=False)
                last.then_inc(S["lin"], 1)
                after("hlin")
                after("blo")
                after("clo")

                column = lambda sel, j: sel[j % 2][:].rearrange("p c f -> p (c f)")

                def step(s, j, has):
                    n = PAIRS * b + s
                    if has(3):
                        pe.wait_ge(T["selc"], n - 2)
                        if has(4):
                            pe.wait_ge(T["u_done"], n - 3)
                        product(ps_d, column(sel_c, j - 3), (chl,)).then_inc(T["c_in"], 1)
                    if has(-1):
                        pe.wait_ge(T["selb"], n + 2)
                        if has(1):
                            pe.wait_ge(T["zc_done"], n)
                        product((ps_a, ps_b)[(j + 1) % 2], column(sel_b, j + 1), (bhl,)).then_inc(T["b_in"], 1)
                    if has(4):
                        pe.wait_ge(T["u_done"], n - 3)
                        final = isinstance(s, int) and s == PAIRS + LAG
                        for c in halves:
                            last = nc.tensor.matmul(ps_c[:, c], fold2[:].rearrange("p c f -> p (c f)"),
                                                    u[(j - 4) % 2][:, c], start=False, stop=final)
                        last.then_inc(T["folded"], 1)

                pe.wait_ge(T["selb"], PAIRS * b + 1)
                product(ps_a, column(sel_b, 0), (bhl,)).then_inc(T["b_in"], 1)
                pairs_of(pe.Fori, step)
                pe.wait_ge(T["zc_done"], PAIRS * b + PAIRS)
                rows_of(ps_a, wi_st).then_inc(S["xw"], 1)
                after("xw_out")
                for c in halves:
                    for m in range(NT):
                        last = nc.tensor.matmul(ps_b[:, c], xw[:, m, :], adj_t[:, m, c], start=(m == 0),
                                                stop=(m == NT - 1))
                last.then_inc(S["ind"], 1)
                after("g")
                product(ps_a, fcw[:], (g_t[0:F, :],)).then_inc(S["sg"], 1)
                after("ind_out")
                product(ps_d, fcw[:], (ind[0:F, :],)).then_inc(S["si"], 1)
                after("sg_out")
                after("si_out")
                for c in halves:
                    nc.tensor.matmul(ps_c[:, c], av_rep[:], tg[:, c], start=True, stop=False)
                    last = nc.tensor.matmul(ps_c[:, c], av_neg[:], ti[:, c], start=False, stop=True)
                last.then_inc(S["diff"], 1)
                after("res")
                pe.sem_inc(S["pe_passed"], 1)
                for k in range(NT):
                    last = nc.tensor.transpose(ps_b[:, k * F:(k + 1) * F], res[0:F, k * P:(k + 1) * P], ident[0:F, 0:F])
                last.then_inc(S["res_t"], 1)

        @block.vector
        def _(dve):
            with dve.Fori(0, B) as b:
                after = lambda name: dve.wait_ge(S[name], b + 1)
                tt, ts, stt = nc.vector.tensor_tensor, nc.vector.tensor_scalar, nc.vector.scalar_tensor_tensor
                after("hh")
                tt(xll[:], ps_a[:], xhh[:].bitcast(F32), ALU.subtract).then_inc(S["ll"], 1)
                after("v02")
                stt(out=al[:], in0=ps_a[0:E, :], scalar=1.0, in1=m1[:], op0=ALU.mult, op1=ALU.max)\
                    .then_inc(S["lean"], 1)
                after("lean")
                dve.sem_inc(S["passed"], 1)
                nc.vector.tensor_tensor_reduce(out=al[:], in0=al[:], in1=mask_cols[:], scale=-1.0, scalar=3.0e38,
                                               op0=ALU.add, op1=ALU.min, accum_out=al_stat[:, 0:1])\
                    .then_inc(S["peak"], 1)
                after("alex")
                nc.vector.reciprocal(al_stat[:, 2:3], al_stat[:, 1:2]).then_inc(S["alinv"], 1)
                after("alinv")
                ts(al[:], al[:], al_stat[:, 2:3], None, ALU.mult).then_inc(S["alnorm"], 1)
                after("al_turned")
                nc.vector.tensor_copy(al_t[:].rearrange("p k e -> p (k e)"), ps_a[:, 0:NT * E]).then_inc(S["al_out"], 1)
                after("agg")
                for c in range(2):
                    part = ps_b[c * F:(c + 1) * F, c * PAIRS:(c + 1) * PAIRS]
                    nc.vector.tensor_copy(agg2[c * F:(c + 1) * F, :], part)
                    ts(nagg2[c * F:(c + 1) * F, :], part, -1.0, None, ALU.mult)
                    nc.vector.tensor_copy(agg_td[:, c, :], ps_b[0:F, 0:E])
                nc.vector.tensor_copy(agg_e[:], ps_b[0:E, HALF:HALF + P]).then_inc(S["agg_out"], 1)
                after("he_ex")
                ts(he_e[:], he_e[:], 1.0, -1.0, ALU.min, ALU.add).then_inc(S["he_min"], 1)
                after("he_min")
                stt(out=he[:], in0=agg_td[:, 0, :], scalar=0.0, in1=he_e[:], op0=ALU.max, op1=ALU.add)\
                    .then_inc(S["he_done"], 1)
                after("tanh_b")
                ts(beta[:], beta[:], 0.5, 0.5, ALU.mult, ALU.add).then_inc(S["beta"], 1)
                after("bhi")
                tt(bhl[F:P, :], beta[F:P, :], bhl[F:P, :].bitcast(F32), ALU.subtract).then_inc(S["blo"], 1)
                wide = [P, NT, E]
                over_e = lambda i: lc_stat[:, i, :].unsqueeze(2).broadcast_to(wide)
                after("se")
                tt(lc[:], mask_rows[:], ps_a[:, 0:E].unsqueeze(1).broadcast_to(wide), ALU.add).then_inc(S["lc"], 1)
                after("lc")
                nc.vector.tensor_reduce(lc_stat[:, 0, :], lc[:], AX.X, ALU.max).then_inc(S["mx"], 1)
                after("mx")
                tt(lc[:], lc[:], over_e(0), ALU.subtract).then_inc(S["lcs"], 1)
                after("lce")
                nc.vector.tensor_reduce(lc_stat[:, 1, :], lc[:], AX.X, ALU.add).then_inc(S["lcsum"], 1)
                after("lcsum")
                nc.vector.reciprocal(lc_stat[:, 2, :], lc_stat[:, 1, :]).then_inc(S["lcinv"], 1)
                after("lcinv")
                for c in range(2):
                    last = tt(c_n[:, :, c, :], lc[:], over_e(2), ALU.mult)
                last.then_inc(S["c_n"], 1)
                after("c_turned")
                after("chi")
                tt(m1[:], ps_d[0:E, :], beta[0:E, :], ALU.mult).then_inc(S["m1"], 1)
                after("m1")
                tt(c1[:], ps_d[0:E, :], m1[:], ALU.subtract).then_inc(S["c1"], 1)
                tt(chl[F:P, :], ps_d[F:P, :], chl[F:P, :].bitcast(F32), ALU.subtract).then_inc(S["clo"], 1)
                after("bsum")
                tt(hlin[:], h_t[:], ps_a[:], ALU.mult).then_inc(S["hlin"], 1)

                def step(s, j, has):
                    n = PAIRS * b + s
                    if has(0):
                        if has(2):
                            dve.wait_ge(T["r_done"], n - 1)
                        dve.wait_ge(T["b_in"], n + 1)
                        stt(out=zc[j % 2][:], in0=h_t[:], scalar=agg2[:, bass.ds(s, 1)], in1=(ps_a, ps_b)[j % 2][:],
                            op0=ALU.subtract, op1=ALU.mult).then_inc(T["zc_done"], 1)
                    if has(3):
                        dve.wait_ge(T["t_done"], n - 2)
                        if has(5):
                            dve.wait_ge(T["folded"], n - 4)
                        dve.wait_ge(T["c_in"], n - 2)
                        tt(u[(j - 3) % 2][:], r[(j - 3) % 4][:], ps_d[:], ALU.mult).then_inc(T["u_done"], 1)

                pairs_of(dve.Fori, step)
                dve.wait_ge(T["folded"], PAIRS * b + PAIRS)
                stt(out=g_t[:], in0=ps_c[:], scalar=-1.0, in1=hlin[:], op0=ALU.add, op1=ALU.add).then_inc(S["g"], 1)
                after("ind_out")
                after("g")
                tt(res[:], g_t[:], ind[:], ALU.subtract).then_inc(S["d"], 1)
                after("wt")
                ts(mix[:], mix[:], 0.5, 0.5, ALU.mult, ALU.add).then_inc(S["wt2"], 1)
                after("wt2")
                tt(res[:], res[:], mix[:], ALU.mult).then_inc(S["dw"], 1)
                after("dw")
                tt(res[:], res[:], ind[:], ALU.add).then_inc(S["res"], 1)
                after("res_t")
                rows = x[:, bass.ds(b * NT, NT), :]
                tt(rows, rows, ps_b[:, 0:NT * F].rearrange("p (k f) -> p k f", f=F), ALU.add).then_inc(S["added"], 1)

        @block.scalar
        def _(act):
            with act.Fori(0, B) as b:
                after = lambda name: act.wait_ge(S[name], b + 1)
                fn = nc.scalar.activation
                after("xt")
                fn(xhh[:], ps_a[:], ACT.Copy).then_inc(S["hh"], 1)
                after("v")
                fn(m1[:], ps_a[0:E, :], ACT.Copy, scale=0.2).then_inc(S["v02"], 1)
                after("hn")
                fn(h_n[:].rearrange("p k c -> p (k c)"), ps_d[:], ACT.Copy).then_inc(S["hn_out"], 1)
                after("ht")
                fn(h_t[:], ps_b[:], ACT.Copy).then_inc(S["ht_out"], 1)
                after("peak")
                fn(al[:], al[:], ACT.Exp, bias=al_stat[:, 0:1], scale=-1.0, accum_out=al_stat[:, 1:2])\
                    .then_inc(S["alex"], 1)
                after("agg_out")
                fn(he_e[:], agg_td[:, 0, :], ACT.Exp).then_inc(S["he_ex"], 1)
                after("age")
                fn(age[:], ps_a[:, 0:1], ACT.Copy, scale=0.5).then_inc(S["age_out"], 1)
                after("ut")
                fn(u_t[:], ps_a[:, HALF:HALF + E], ACT.Tanh, bias=fcb_col[:, 0:1]).then_inc(S["ut_out"], 1)
                after("hg")
                after("age_out")
                fn(beta[:], ps_c[:], ACT.Tanh, bias=age[:, 0:1], scale=0.5).then_inc(S["tanh_b"], 1)
                after("beta")
                fn(bhl[:], beta[:], ACT.Copy).then_inc(S["bhi"], 1)
                after("lcs")
                fn(lc[:], lc[:], ACT.Exp).then_inc(S["lce"], 1)
                after("c_turned")
                fn(chl[:], ps_d[:], ACT.Copy).then_inc(S["chi"], 1)

                def select(to, k, done):
                    src = fold[:].rearrange("p (c k) -> p c k", k=PAIRS)[:, :, bass.ds(k, 1)]
                    fn(to[:], src.broadcast_to([P, 2, F]), ACT.Copy).then_inc(done, 1)

                for k in range(2):
                    select(sel_b[k], k, T["selb"])

                def step(s, j, has):
                    n = PAIRS * b + s
                    if has(2):
                        if has(4):
                            act.wait_ge(T["c_in"], n - 3)
                            act.sem_inc(S["passed"], 1)
                        select(sel_c[j % 2], s - 2, T["selc"])
                    if has(-2):
                        act.wait_ge(T["b_in"], n + 1)
                        act.sem_inc(S["passed"], 1)
                        select(sel_b[j % 2], s + 2, T["selb"])
                    if has(0):
                        if has(4):
                            act.wait_ge(T["u_done"], n - 3)
                        act.wait_ge(T["zc_done"], n + 1)
                        act.sem_inc(S["passed"], 1)
                        fn(r[j % 4][:], zc[j % 2][:], ACT.Relu, bias=nagg2[:, bass.ds(s, 1)], scale=-1.0)\
                            .then_inc(T["r_done"], 1)
                    if has(1):
                        if has(3):
                            act.wait_ge(T["t_done"], n - 2)
                        act.wait_ge(T["r_done"], n)
                        fn(ex[(j - 1) % 2][:], r[(j - 1) % 4][:], ACT.Exp, scale=-1.0).then_inc(T["ex_done"], 1)

                pairs_of(act.Fori, step)
                after("xw")
                fn(xw[:].rearrange("p k c -> p (k c)"), ps_a[:], ACT.Copy).then_inc(S["xw_out"], 1)
                after("ind")
                fn(ind[:], ps_b[:], ACT.Copy).then_inc(S["ind_out"], 1)
                after("sg")
                fn(tg[:], ps_a[:], ACT.Tanh, bias=fcb_col[:, 0:1]).then_inc(S["sg_out"], 1)
                after("si")
                fn(ti[:], ps_d[:], ACT.Tanh, bias=fcb_col[:, 0:1]).then_inc(S["si_out"], 1)
                after("diff")
                fn(mix[:], ps_c[:], ACT.Tanh, scale=0.5).then_inc(S["wt"], 1)


class Attention:

    def __init__(self, nc, ctx, name):
        sb = lambda n, s, d=F32: ctx.enter_context(nc.sbuf_tensor(f"{name}_{n}", s, d))
        sem = lambda n: nc.alloc_semaphore(f"{name}_{n}")
        ps = lambda n, s: ctx.enter_context(nc.psum_tensor(f"{name}_{n}", s, F32))
        sem = lambda n: nc.alloc_semaphore(f"{name}_{n}")
        self.nc = nc
        self.pair = sb("pair", [P, NT, 2, F])
        self.paired = sem("paired")
        self.prob = [sb(f"prob{i}", [P, N]) for i in range(4)]
        self.negmax = sb("negmax", [P, 4])
        self.rowsum = sb("rowsum", [P, 4])
        self.rowinv = sb("rowinv", [P, 4])
        self.pt_hi = [sb(f"pt_hi{i}", [P, NT, HALF], F32R) for i in range(2)]
        self.pt_lo = [sb(f"pt_lo{i}", [P, NT, HALF], F32R) for i in range(2)]
        self.z = [sb(f"z{i}", [P, HALF]) for i in range(2)]
        self.ps_score = [ps(f"ps_score{i}", [P, N]) for i in range(2)]
        self.ps_turn = [ps(f"ps_turn{i}", [P, HALF]) for i in range(2)]
        self.ps_z = ps("ps_z", [P, HALF])
        self.ps_post = ps("ps_post", [P, HALF])
        self.xhh = sb("xhh", [P, N], F32R)
        self.xll = sb("xll", [P, N], F32R)
        self.xhl = sb("xhl", [P, N], F32R)
        self.xm = sb("xm", [P, NT, P], F32R)
        self.scored = sem("scored")
        self.masked = sem("masked")
        self.exped = sem("exped")
        self.dve_passed, self.pool_passed = sem("dve_passed"), sem("pool_passed")
        self.inverted = sem("inverted")
        self.normed = sem("normed")
        self.turned = sem("turned")
        self.high = sem("high")
        self.low = sem("low")
        self.summed = sem("summed")
        self.copied = sem("copied")
        self.posted = sem("posted")
        self.finished = sem("finished")
        self.xt_ready = sem("xt_ready")
        self.hh_ready = sem("hh_ready")
        self.ll_ready = sem("ll_ready")
        self.hl_ready = sem("hl_ready")
        self.xm_turned = sem("xm_turned")
        self.xm_ready = sem("xm_ready")

    def dve_credits(self, dve):
        dve.sem_inc(self.masked, 2)
        dve.sem_inc(self.low, 2)
        dve.sem_inc(self.copied, 1)

    def pe_credits(self, pe):
        pe.sem_inc(self.turned, 8)
        pe.sem_inc(self.summed, 2)
        pe.sem_inc(self.posted, 2)

    def pe_score_free(self, pe, u, i):
        pe.wait_ge(self.masked, 8 * u + i + 1)

    def dve_mask_add(self, dve, u, i, mask):
        dve.wait_ge(self.turned, 16 * u + 2 * i + 2)
        dve.wait_ge(self.scored, 8 * u + i + 1)
        dve.sem_inc(self.dve_passed, 1)
        self.nc.vector.tensor_tensor_reduce(
            out=self.prob[i % 4][:], in0=self.ps_score[i % 2][:], in1=mask, scale=-1.0, scalar=3.0e38,
            op0=ALU.add, op1=ALU.min, accum_out=self.negmax[:, i % 4:i % 4 + 1]).then_inc(self.masked, 1)

    def act_exp(self, act, u, i):
        act.wait_ge(self.masked, 8 * u + i + 3)
        c = slice(i % 4, i % 4 + 1)
        self.nc.scalar.activation(self.prob[i % 4][:], self.prob[i % 4][:], ACT.Exp, bias=self.negmax[:, c],
                                  scale=-1.0, accum_out=self.rowsum[:, c]).then_inc(self.exped, 1)

    def dve_invert(self, dve, u, i):
        dve.wait_ge(self.exped, 8 * u + i + 1)
        c = slice(i % 4, i % 4 + 1)
        self.nc.vector.reciprocal(self.rowinv[:, c], self.rowsum[:, c]).then_inc(self.inverted, 1)

    def pool_norm(self, pool, u, i):
        pool.wait_ge(self.inverted, 8 * u + i + 1)
        pool.sem_inc(self.pool_passed, 1)
        self.nc.gpsimd.tensor_scalar(self.prob[i % 4][:], self.prob[i % 4][:], self.rowinv[:, i % 4:i % 4 + 1],
                                     1.0, ALU.mult, ALU.mult).then_inc(self.normed, 1)

    def pe_turn(self, pe, u, i, ident):
        pe.wait_ge(self.normed, 8 * u + i + 1)
        for j in range(2):
            pe.wait_ge(self.low, 16 * u + 2 * i + j + 1)
            for k in range(TPH):
                m = TPH * j + k
                last = self.nc.tensor.transpose(self.ps_turn[j][:, k * P:(k + 1) * P],
                                                self.prob[i % 4][:, m * P:(m + 1) * P], ident[:])
            last.then_inc(self.turned, 1)

    def part(self, parts, i, j):
        return parts[i // TPH][:, TPH * j:TPH * (j + 1), (i % TPH) * P:(i % TPH + 1) * P]

    def act_high(self, act, u, i, j):
        act.wait_ge(self.turned, 16 * u + 2 * i + j + 9)
        if i % TPH == 0 and j == 0:
            act.wait_ge(self.summed, 2 * u + i // TPH + 1)
        self.nc.scalar.activation(self.part(self.pt_hi, i, j),
                                  self.ps_turn[j][:].rearrange("p (k n) -> p k n", n=P),
                                  ACT.Copy).then_inc(self.high, 1)

    def dve_low(self, dve, u, i, j):
        dve.wait_ge(self.high, 16 * u + 2 * i + j + 1)
        if i % TPH == 0 and j == 0:
            dve.wait_ge(self.summed, 2 * u + i // TPH + 1)
        self.nc.vector.tensor_tensor(self.part(self.pt_lo, i, j),
                                     self.ps_turn[j][:].rearrange("p (k n) -> p k n", n=P),
                                     self.part(self.pt_hi, i, j).bitcast(F32), ALU.subtract).then_inc(self.low, 1)

    def pe_sum(self, pe, u, q, quarter=None):
        if quarter in (None, 0):
            pe.wait_ge(self.low, 16 * u + 8 * (q + 1) + 2)
            pe.wait_ge(self.copied, 2 * u + q + 1)
        for k in range(2 * NT) if quarter is None else range(4 * quarter, 4 * quarter + 4):
            part, m = (self.pt_hi, self.pt_lo)[k // NT], k % NT
            last = self.nc.tensor.matmul(self.ps_z[:], self.xm[:, m, :], part[q][:, m, :],
                                         start=(k == 0), stop=(k == 2 * NT - 1))
        if quarter in (None, 3):
            last.then_inc(self.summed, 1)

    def act_copy(self, act, u, q):
        act.wait_ge(self.summed, 2 * u + q + 3)
        act.wait_ge(self.posted, 2 * u + q + 1)
        self.nc.scalar.activation(self.z[q][:], self.ps_z[:], ACT.Copy).then_inc(self.copied, 1)

    def dve_copy(self, dve, u, q):
        dve.wait_ge(self.summed, 2 * u + q + 3)
        dve.wait_ge(self.posted, 2 * u + q + 1)
        self.nc.vector.tensor_copy(self.z[q][:], self.ps_z[:]).then_inc(self.copied, 1)

    def act_xhh(self, act, b, n, src=None):
        if src is None:
            src = self.ps_score[0]
            act.wait_ge(self.xt_ready, b + 1)
        self.nc.scalar.activation(self.xhh[:], src[:], ACT.Copy).then_inc(self.hh_ready, 1)

    def dve_xll(self, dve, n, src=None):
        dve.wait_ge(self.hh_ready, n + 1)
        self.nc.vector.tensor_tensor(self.xll[:], (src or self.ps_score[0])[:], self.xhh[:].bitcast(F32),
                                     ALU.subtract).then_inc(self.ll_ready, 1)

    def act_xhl(self, act, n):
        act.wait_ge(self.ll_ready, n + 1)
        for rows, part in ((slice(0, F), self.xhh), (slice(F, P), self.xll)):
            self.nc.scalar.activation(self.xhl[rows, :], part[rows, :].bitcast(F32), ACT.Copy)\
                .then_inc(self.hl_ready, 1)

    def pe_xm_turn(self, pe, n, ident):
        pe.wait_ge(self.hl_ready, 2 * n + 2)
        for k in range(NT):
            last = self.nc.tensor.transpose(self.ps_score[1][:, k * P:(k + 1) * P],
                                            self.xhl[:, k * P:(k + 1) * P].bitcast(F32), ident[:])
        last.then_inc(self.xm_turned, 1)

    def dve_xm(self, dve, n):
        dve.wait_ge(self.xm_turned, n + 1)
        self.nc.vector.tensor_copy(self.xm[:].rearrange("p k c -> p (k c)"), self.ps_score[1][:])\
            .then_inc(self.xm_ready, 1)

    def pool_pair(self, pool, b, hx):
        self.nc.gpsimd.tensor_copy(
            self.pair[:], hx[:, bass.ds(b * NT, NT), :].unsqueeze(2).broadcast_to([P, NT, 2, F]))\
            .then_inc(self.paired, 1)

    def pe_x_turn(self, pe, b, ident):
        pe.wait_ge(self.paired, b + 1)
        for k in range(NT):
            last = self.nc.tensor.transpose(self.ps_score[0][:, k * P:(k + 1) * P],
                                            self.pair[:, k].rearrange("p c f -> p (c f)"), ident[:])
        last.then_inc(self.xt_ready, 1)


def layer1(nc, ctx, B, x, hx, mask, ident, fold, Wh, bh, W_out, b_out):
    sb = lambda n, s, d=F32: ctx.enter_context(nc.sbuf_tensor(n, s, d))
    sem = lambda n: nc.alloc_semaphore(n)
    UNITS = HEADS + 1
    ww = sb("ww", [P, HEADS, HID])
    g = sb("g", [P, HEADS, P], F32R)
    bcol = sb("bcol", [P, HEADS])
    wo = sb("wo", [P, HEADS, 2, F])
    bout = sb("bout", [P, F])
    at = Attention(nc, ctx, "l1")
    loaded, wt_ready, wt_done, g_ready, g_hi, g_lo = (
        sem(f"l1_{n}") for n in ("loaded", "wt_ready", "wt_done", "g_ready", "g_hi", "g_lo"))
    LOADS = 6 * 16
    wt = at.prob[0]

    with nc.Block() as block:
        @block.sync
        def _(sp):
            sp.dma_start(ww[0:F], Wh.rearrange("h c d -> c h d")).then_inc(loaded, 16)
            sp.dma_start(ww[F:P], Wh.rearrange("h c d -> c h d")).then_inc(loaded, 16)
            with nc.allow_non_contiguous_dma(reason="a small transposed load"):
                sp.dma_start(bcol[:], bh.rearrange("h d -> d h")).then_inc(loaded, 16)
            for c in range(2):
                sp.dma_start(wo[:, :, c, :], W_out.rearrange("(h d) f -> d h f", d=HID)).then_inc(loaded, 16)
            sp.dma_start(bout[:], b_out.rearrange("(o f) -> o f", o=1).broadcast_to([P, F])).then_inc(loaded, 16)
            sp.wait_ge(loaded, LOADS)

        @block.tensor
        def _(pe):
            pe.wait_ge(loaded, LOADS)
            for h in range(HEADS):
                last = nc.tensor.transpose(at.ps_score[0][:, h * P:(h + 1) * P], ww[:, h, :], ident[:])
            last.then_inc(wt_ready, 1)
            pe.wait_ge(wt_done, 1)
            for h in range(HEADS):
                w = wt[:, h * P:(h + 1) * P]
                last = nc.tensor.matmul(at.ps_score[1][:, h * P:(h + 1) * P], w, w, start=True, stop=True)
            last.then_inc(g_ready, 1)

        @block.vector
        def _(dve):
            dve.wait_ge(wt_ready, 1)
            nc.vector.tensor_copy(wt[:], at.ps_score[0][:]).then_inc(wt_done, 1)
            dve.wait_ge(g_hi, 1)
            nc.vector.tensor_tensor(g[F:P], at.ps_score[1][F:P, :].rearrange("p (h c) -> p h c", c=P),
                                    g[F:P].bitcast(F32), ALU.subtract).then_inc(g_lo, 1)

        @block.scalar
        def _(act):
            act.wait_ge(g_ready, 1)
            nc.scalar.activation(g[:], at.ps_score[1][:].rearrange("p (h c) -> p h c", c=P),
                                 ACT.Copy).then_inc(g_hi, 1)

    y = [sb(f"y{i}", [P, N], F32R) for i in range(2)]
    gs = [sb(f"gs{i}", [P, P], F32R) for i in range(2)]
    ws = [sb(f"ws{i}", [P, HID]) for i in range(2)]
    wos = [sb(f"wos{i}", [P, P]) for i in range(2)]
    bs = [sb(f"bs{i}", [P, 1]) for i in range(2)]
    biased = [sb(f"biased{i}", [P, HALF]) for i in range(2)]
    cat = [sb(f"cat{i}", [P, HALF]) for i in range(2)]
    hout = sb("hout", [P, N])
    last_act = sb("last_act", [P, TPH, F])
    g_staged, w_staged = sem("l1_g_staged"), sem("l1_w_staged")
    projected = sem("l1_projected")
    y_hi, y_lo = sem("l1_y_hi"), sem("l1_y_lo")
    cat_biased = sem("l1_cat_biased")
    cat_done = sem("l1_cat_done")
    mixed = sem("l1_mixed")
    hout_done = sem("l1_hout_done")
    zeroed = sem("l1_zeroed")
    out_sum = sem("l1_out_sum")

    with nc.Block() as block:

        not_first = lambda h: not (isinstance(h, int) and h == 1)

        def heads_of(loop, unit):
            unit(0, 0, False, True, True)
            unit(1, 1, True, True, True)
            with loop(2, HEADS - 2, 2) as h:
                unit(h, 0, True, True, True)
                unit(h + 1, 1, True, True, True)
            unit(HEADS - 2, 0, True, True, True)
            unit(HEADS - 1, 1, True, True, False)
            unit(HEADS, 0, True, False, False)

        @block.tensor
        def _(pe):
            at.pe_credits(pe)
            pe.sem_inc(mixed, 2)
            with pe.Fori(0, B) as b:
                u0, n0 = b * UNITS, b * (2 * HEADS)

                def project(h, par, q):
                    if q == 0:
                        pe.wait_ge(g_staged, HEADS * b + h + 1)
                    else:
                        pe.wait_ge(y_lo, n0 + 2 * h + 1)
                    c = slice(q * HALF, (q + 1) * HALF)
                    nc.tensor.matmul(at.ps_post[:], gs[par][:], at.xhh[:, c], start=True, stop=False)
                    nc.tensor.matmul(at.ps_post[:], gs[par][:], at.xll[:, c], start=False, stop=True)\
                        .then_inc(projected, 1)

                def score(u, i, operand):
                    at.pe_score_free(pe, u, i)
                    for q in range(2):
                        c = slice(q * HALF, (q + 1) * HALF)
                        for part in (at.xhh, at.xll):
                            last = nc.tensor.matmul(at.ps_score[i % 2][:, c], operand[:, i * P:(i + 1) * P],
                                                    part[:, c], start=(part is at.xhh), stop=(part is at.xll))
                    last.then_inc(at.scored, 1)

                def post(h, par, q):
                    if q == 0:
                        pe.wait_ge(w_staged, 3 * HEADS * b + 3 * h + 3)
                    pe.wait_ge(at.copied, 2 * u0 + 2 * h + q + 2)
                    nc.tensor.matmul(at.ps_post[:], ws[par][:], at.z[q][:], start=True, stop=True)\
                        .then_inc(at.posted, 1)

                def mix(h, par, q):
                    pe.wait_ge(cat_done, n0 + 2 * h + q + 1)
                    nc.tensor.matmul(at.ps_post[:], wos[par][:], cat[q][:], start=True, stop=True)\
                        .then_inc(mixed, 1)

                def unit(h, par, prev, current, following):
                    u = u0 + h
                    if current:
                        pe.wait_ge(y_lo, n0 + 2 * h + 2)
                    for i in range(NT):
                        if current:
                            score(u, i, y[par])
                        if i == 1 and prev and not_first(h):
                            mix(h - 2, par, 1)
                        if i == 4 and prev:
                            mix(h - 1, 1 - par, 0)
                        if i == 5 and following:
                            if prev:
                                pe.wait_ge(hout_done, n0 + 2 * h - 1)
                            project(h + 1, 1 - par, 0)
                        if i == 6 and following:
                            project(h + 1, 1 - par, 1)
                        if i >= 2 and current:
                            at.pe_turn(pe, u, i - 2, ident)
                        elif i < 2 and prev:
                            at.pe_turn(pe, u - 1, i + 6, ident)
                        if prev and i == 2:
                            if not_first(h):
                                pe.wait_ge(hout_done, n0 + 2 * h - 2)
                            post(h - 1, 1 - par, 0)
                        if prev and i == 7:
                            if following:
                                pe.wait_ge(y_lo, n0 + 2 * h + 4)
                            else:
                                pe.wait_ge(hout_done, n0 + 2 * h - 1)
                            post(h - 1, 1 - par, 1)
                        if i >= 6 and current:
                            at.pe_sum(pe, u, 0, i - 6)
                        elif i < 2 and prev:
                            at.pe_sum(pe, u - 1, 0, i + 2)
                        elif 2 <= i < 6 and prev:
                            at.pe_sum(pe, u - 1, 1, i - 2)
                    if not current:
                        mix(h - 1, 1 - par, 1)

                at.pe_x_turn(pe, b, ident)
                at.pe_xm_turn(pe, 2 * b, ident)
                project(0, 0, 0)
                project(0, 0, 1)
                pe.wait_ge(at.xm_ready, 2 * b + 1)
                heads_of(pe.Fori, unit)
                at.pe_xm_turn(pe, 2 * b + 1, ident)
                pe.wait_ge(at.xm_ready, 2 * b + 2)
                u = u0 + HEADS
                for i in range(NT + 2):
                    if i < NT:
                        score(u, i, at.xhl)
                    if i >= 2:
                        at.pe_turn(pe, u, i - 2, ident)
                    if i >= 6:
                        at.pe_sum(pe, u, 0, i - 6)
                at.pe_sum(pe, u, 1)
                for q in range(2):
                    pe.wait_ge(at.copied, 2 * u + q + 2)
                    if q == 0:
                        pe.wait_ge(hout_done, n0 + 2 * HEADS)
                    else:
                        pe.wait_ge(out_sum, 6 * b + 1)
                    for i in range(TPH):
                        last = nc.tensor.matmul(at.ps_post[:, i * F:(i + 1) * F],
                                                at.z[q][:, i * P:(i + 1) * P], fold[:], start=True, stop=True)
                    last.then_inc(at.posted, 1)

        @block.vector
        def _(dve):
            at.dve_credits(dve)
            with dve.Fori(0, B) as b:
                u0, n0 = b * UNITS, b * (2 * HEADS)

                def tile(u, i, prev, current, between=lambda: None):
                    if i >= 1 and current:
                        at.dve_invert(dve, u, i - 1)
                    elif i < 1 and prev:
                        at.dve_invert(dve, u - 1, NT - 1)
                    if current:
                        at.dve_mask_add(dve, u, i, mask[:, i, :])
                    between()
                    for j in range(2):
                        if i >= 2 and current:
                            at.dve_low(dve, u, i - 2, j)
                        elif i < 2 and prev:
                            at.dve_low(dve, u - 1, i + 6, j)

                def leaky(h, q):
                    dve.wait_ge(cat_biased, n0 + 2 * h + q + 1)
                    dve.wait_ge(mixed, n0 + 2 * h + q + 1)
                    nc.vector.scalar_tensor_tensor(out=cat[q][:], in0=biased[q][:], scalar=0.01, in1=biased[q][:],
                                                   op0=ALU.mult, op1=ALU.max).then_inc(cat_done, 1)

                def accumulate(h, q):
                    dve.wait_ge(mixed, n0 + 2 * h + q + 3)
                    c = slice(q * HALF, (q + 1) * HALF)
                    nc.vector.tensor_tensor(hout[:, c], at.ps_post[:], hout[:, c], ALU.add).then_inc(hout_done, 1)

                def split_y(h, par, q):
                    dve.wait_ge(y_hi, n0 + 2 * h + q + 1)
                    c = slice(q * HALF, (q + 1) * HALF)
                    nc.vector.tensor_tensor(y[par][F:P, c], at.ps_post[F:P, :], y[par][F:P, c].bitcast(F32),
                                            ALU.subtract).then_inc(y_lo, 1)

                def unit(h, par, prev, current, following):
                    u = u0 + h

                    def between(i):
                        if i == 0 and prev and not_first(h):
                            leaky(h - 2, 1)
                        if i == 3 and prev:
                            leaky(h - 1, 0)
                        if i == 1 and prev and not_first(h):
                            accumulate(h - 2, 1)
                        if i == 4 and prev:
                            accumulate(h - 1, 0)
                        if i in (5, 6) and following:
                            split_y(h + 1, 1 - par, i - 5)

                    for i in range(NT):
                        tile(u, i, prev, current, lambda: between(i))
                    if not current:
                        leaky(h - 1, 1)
                        accumulate(h - 1, 1)

                dve.wait_ge(zeroed, b + 1)
                at.dve_xll(dve, 2 * b)
                at.dve_xm(dve, 2 * b)
                split_y(0, 0, 0)
                split_y(0, 0, 1)
                heads_of(dve.Fori, unit)
                at.dve_xll(dve, 2 * b + 1, hout)
                at.dve_xm(dve, 2 * b + 1)
                u = u0 + HEADS
                for i in range(NT):
                    tile(u, i, False, True)
                for i in range(2):
                    tile(u + 1, i, True, False)
                for q in range(2):
                    dve.wait_ge(at.posted, 2 * u + q + 3)
                    nc.vector.tensor_tensor(last_act[:], at.ps_post[:, 0:TPH * F].rearrange("p (i f) -> p i f", f=F),
                                            bout[:].unsqueeze(1).broadcast_to([P, TPH, F]), ALU.add)\
                        .then_inc(out_sum, 1)
                    dve.wait_ge(out_sum, 6 * b + 3 * q + 1)
                    nc.vector.scalar_tensor_tensor(out=last_act[:], in0=last_act[:], scalar=0.01,
                                                   in1=last_act[:], op0=ALU.mult, op1=ALU.max)\
                        .then_inc(out_sum, 1)
                    dve.wait_ge(out_sum, 6 * b + 3 * q + 2)
                    rows = x[:, bass.ds(b * NT + q * TPH, TPH), :]
                    nc.vector.tensor_tensor(rows, rows, last_act[:], ALU.add).then_inc(out_sum, 1)
                    dve.wait_ge(out_sum, 6 * b + 3 * q + 3)

        @block.scalar
        def _(act):
            with act.Fori(0, B) as b:
                u0, n0 = b * UNITS, b * (2 * HEADS)

                def tile(u, i, prev, current):
                    for j in range(2):
                        if i >= 2 and current:
                            at.act_high(act, u, i - 2, j)
                        elif i < 2 and prev:
                            at.act_high(act, u - 1, i + 6, j)
                    if current:
                        at.act_exp(act, u, i)

                def high_y(h, par, q):
                    act.wait_ge(projected, n0 + 2 * h + q + 1)
                    nc.scalar.activation(y[par][:, q * HALF:(q + 1) * HALF], at.ps_post[:], ACT.Copy)\
                        .then_inc(y_hi, 1)

                def bias(h, par, q):
                    act.wait_ge(at.posted, 2 * u0 + 2 * h + q + 3)
                    nc.scalar.activation(biased[q][:], at.ps_post[:], ACT.Identity, bias=bs[par][:, 0:1])\
                        .then_inc(cat_biased, 1)

                def unit(h, par, prev, current, following):
                    u = u0 + h
                    for i in range(NT):
                        if i in (5, 6) and following:
                            high_y(h + 1, 1 - par, i - 5)
                        if i in (2, 6) and prev:
                            at.act_copy(act, u - 1, (i - 2) // 4)
                        tile(u, i, prev, current)
                        if i in (2, 7) and prev:
                            bias(h - 1, 1 - par, (i - 2) // 5)

                at.act_xhh(act, b, 2 * b)
                at.act_xhl(act, 2 * b)
                high_y(0, 0, 0)
                high_y(0, 0, 1)
                heads_of(act.Fori, unit)
                act.wait_ge(hout_done, n0 + 2 * HEADS)
                at.act_xhh(act, b, 2 * b + 1, hout)
                at.act_xhl(act, 2 * b + 1)
                u = u0 + HEADS
                for i in range(NT):
                    tile(u, i, False, True)
                for i in range(2):
                    tile(u + 1, i, True, False)
                at.act_copy(act, u, 0)
                at.act_copy(act, u, 1)

        @block.gpsimd
        def _(pool):
            with pool.Fori(0, B) as b:
                u0, n0 = b * UNITS, b * (2 * HEADS)

                def stage_g(h, par):
                    nc.gpsimd.tensor_copy(gs[par][:], g[:, bass.ds(h, 1), :].bitcast(F32).rearrange("p o c -> p (o c)"))\
                        .then_inc(g_staged, 1)

                def stage_w(h, par):
                    for out, src in ((ws[par][:], ww[:, bass.ds(h, 1), :].rearrange("p o c -> p (o c)")),
                                     (wos[par][:], wo[:, bass.ds(h, 1)].rearrange("p o c f -> p (o c f)")),
                                     (bs[par][:], bcol[:, bass.ds(h, 1)])):
                        nc.gpsimd.tensor_copy(out, src).then_inc(w_staged, 1)

                def unit(h, par, prev, current, following):
                    u = u0 + h
                    for i in range(NT):
                        if i == 0 and following:
                            pool.wait_ge(projected, n0 + 2 * h + 2)
                            pool.sem_inc(at.pool_passed, 1)
                            stage_g(h + 1, 1 - par)
                        if current:
                            at.pool_norm(pool, u, i)
                        if i == 3 and current:
                            if prev and not_first(h):
                                pool.wait_ge(hout_done, n0 + 2 * h - 2)
                                pool.sem_inc(at.pool_passed, 1)
                            stage_w(h, par)

                nc.gpsimd.memset(hout[:], 0.0).then_inc(zeroed, 1)
                at.pool_pair(pool, b, hx)
                stage_g(0, 0)
                heads_of(pool.Fori, unit)
                for i in range(NT):
                    at.pool_norm(pool, u0 + HEADS, i)


def edge_layer(nc, ctx, B, x, hx, pairs, ident, name, W, a, bias):
    sb = lambda n, s, d=F32: ctx.enter_context(nc.sbuf_tensor(f"{name}_{n}", s, d))
    sem = lambda n: nc.alloc_semaphore(f"{name}_{n}")
    weighted = bias is not None
    SLOPE = 0.2
    at = Attention(nc, ctx, name)
    given = sb("given", [P, P])
    other = sb("other", [P, P])
    acol = sb("acol", [F, 2])
    arep = sb("arep", [F, 2, P])
    dst = sb("dst", [P, P], F32R)
    src_hi, src_lo = sb("src_hi", [P, P], F32R), sb("src_lo", [P, P], F32R)
    brow = sb("brow", [P, F])
    loaded, spread, turned, copied, mixed, split = (
        sem(n) for n in ("loaded", "spread", "w_turned", "w_copied", "mixed", "split"))
    loads = 5 if weighted else 4
    a_flat = a.rearrange("(c f) o -> f (c o)", f=F) if weighted else a.rearrange("(c f) -> f c", f=F)

    with nc.Block() as block:
        @block.sync
        def _(sp):
            for c in range(2):
                to = given[c * F:(c + 1) * F, 0:F] if weighted else given[0:F, c * F:(c + 1) * F]
                sp.dma_start(to, W).then_inc(loaded, 16)
            with nc.allow_non_contiguous_dma(reason="128 numbers"):
                for c in range(2):
                    sp.dma_start(acol[:, c:c + 1], a_flat[:, c:c + 1]).then_inc(loaded, 16)
            if weighted:
                sp.dma_start(brow[:], bias.rearrange("(o f) -> o f", o=1).broadcast_to([P, F])).then_inc(loaded, 16)
            sp.wait_ge(loaded, 16 * loads)

        @block.tensor
        def _(pe):
            pe.wait_ge(loaded, 16 * loads)
            if weighted:
                nc.tensor.transpose(at.ps_post[0:F, 0:P], given[:, 0:F], ident[:]).then_inc(turned, 1)
            else:
                nc.tensor.transpose(at.ps_post[:, 0:F], given[0:F, :], ident[0:F, 0:F]).then_inc(turned, 1)
            pe.wait_ge(copied, 1)
            pe.wait_ge(spread, 1)
            lhs = other[0:F, :] if weighted else given[0:F, :]
            nc.tensor.matmul(at.ps_z[:, 0:2 * P], lhs, arep[:].rearrange("p c n -> p (c n)"),
                             start=True, stop=True).then_inc(mixed, 1)

        @block.vector
        def _(dve):
            dve.wait_ge(loaded, 16 * loads)
            nc.vector.tensor_copy(arep[:], acol[:].unsqueeze(2).broadcast_to([F, 2, P])).then_inc(spread, 1)
            dve.wait_ge(turned, 1)
            if weighted:
                nc.vector.tensor_copy(other[0:F, :], at.ps_post[0:F, 0:P]).then_inc(copied, 1)
            else:
                nc.vector.tensor_copy(other[:, 0:F], at.ps_post[:, 0:F]).then_inc(copied, 1)
            dve.wait_ge(split, 2)
            nc.vector.tensor_tensor(src_lo[:], at.ps_z[:, 0:P], src_hi[:].bitcast(F32), ALU.subtract).then_inc(split, 1)
            nc.vector.tensor_tensor(dst[F:P, :], at.ps_z[F:P, P:2 * P], dst[F:P, :].bitcast(F32),
                                    ALU.subtract).then_inc(split, 1)

        @block.scalar
        def _(act):
            act.wait_ge(mixed, 1)
            nc.scalar.activation(src_hi[:], at.ps_z[:, 0:P], ACT.Copy).then_inc(split, 1)
            nc.scalar.activation(dst[:], at.ps_z[:, P:2 * P], ACT.Copy).then_inc(split, 1)

    wst = given[:, 0:F] if weighted else other[:, 0:F]
    d1, d02 = sb("d1", [P, N]), sb("d02", [P, N])
    s08, s02 = sb("s08", [P, NT, 2]), sb("s02", [P, NT, 2])
    e, new = sb("e", [P, TPH, F]), sb("new", [P, TPH, F])
    projected, termed, leaned, shifted, peaked, exped_out, out_step = (
        sem(n) for n in ("projected", "termed", "leaned", "shifted", "peaked", "exped_out", "out_step"))
    OUT = 2 if weighted else 3

    with nc.Block() as block:
        @block.tensor
        def _(pe):
            at.pe_credits(pe)
            with pe.Fori(0, B) as b:
                at.pe_x_turn(pe, b, ident)
                at.pe_xm_turn(pe, b, ident)
                for q in range(2):
                    c = slice(q * HALF, (q + 1) * HALF)
                    nc.tensor.matmul(at.ps_score[0][:, c], dst[:], at.xhh[:, c], start=True, stop=False)
                    nc.tensor.matmul(at.ps_score[0][:, c], dst[:], at.xll[:, c], start=False, stop=True)\
                        .then_inc(projected, 1)
                for i in range(NT):
                    for part in (src_hi, src_lo):
                        last = nc.tensor.matmul(at.ps_post[:, 2 * i:2 * i + 2], at.xhl[:, i * P:(i + 1) * P],
                                                part[:, 0:2], start=(part is src_hi), stop=(part is src_lo))
                last.then_inc(projected, 1)
                pe.wait_ge(at.xm_ready, b + 1)
                for i in range(NT):
                    at.pe_turn(pe, b, i, ident)
                    if i == 5:
                        at.pe_sum(pe, b, 0)
                at.pe_sum(pe, b, 1)
                for q in range(2):
                    pe.wait_ge(at.copied, 2 * b + q + 2)
                    if q == 1:
                        pe.wait_ge(out_step, 2 * OUT * b + OUT)
                    for i in range(TPH):
                        last = nc.tensor.matmul(at.ps_post[:, i * F:(i + 1) * F],
                                                at.z[q][:, i * P:(i + 1) * P], wst, start=True, stop=True)
                    last.then_inc(at.posted, 1)

        @block.vector
        def _(dve):
            at.dve_credits(dve)
            with dve.Fori(0, B) as b:
                def lean(i):
                    dve.wait_ge(at.turned, 16 * b + 2 * i + 2)
                    nc.vector.scalar_tensor_tensor(out=at.prob[i % 4][:], in0=d1[:], scalar=s08[:, i, 0:1],
                                                   in1=d02[:], op0=ALU.add, op1=ALU.max).then_inc(leaned, 1)

                def peak(i):
                    p, c = at.prob[i % 4][:], slice(i % 4, i % 4 + 1)
                    if weighted:
                        dve.wait_ge(shifted, 8 * b + i + 1)
                        dve.sem_inc(at.dve_passed, 1)
                        nc.vector.tensor_tensor_reduce(out=p, in0=p, in1=pairs[:, i, :], scale=1.0, scalar=-3.0e38,
                                                       op0=ALU.mult, op1=ALU.max,
                                                       accum_out=at.negmax[:, c]).then_inc(peaked, 1)
                        dve.wait_ge(peaked, 8 * b + i + 1)
                        nc.vector.tensor_scalar(at.negmax[:, c], at.negmax[:, c], -1.0, None,
                                                ALU.mult).then_inc(at.masked, 1)
                    else:
                        dve.wait_ge(leaned, 8 * b + i + 1)
                        dve.sem_inc(at.dve_passed, 1)
                        nc.vector.tensor_tensor_reduce(out=p, in0=p, in1=pairs[:, i, :], scale=-1.0, scalar=3.0e38,
                                                       op0=ALU.add, op1=ALU.min,
                                                       accum_out=at.negmax[:, c]).then_inc(at.masked, 1)

                at.dve_xll(dve, b)
                at.dve_xm(dve, b)
                dve.wait_ge(termed, 4 * b + 4)
                lean(0)
                for i in range(NT + 3):
                    if i + 1 < NT:
                        lean(i + 1)
                    if i < NT:
                        peak(i)
                    if i >= 1 and i <= NT:
                        at.dve_invert(dve, b, i - 1)
                    if i >= 3:
                        for j in range(2):
                            at.dve_low(dve, b, i - 3, j)
                    if i == 7:
                        at.dve_copy(dve, b, 0)
                at.dve_copy(dve, b, 1)
                for q in range(2):
                    step = 2 * OUT * b + OUT * q
                    v = at.ps_post[:, 0:TPH * F].rearrange("p (i f) -> p i f", f=F)
                    if weighted:
                        dve.wait_ge(at.posted, 2 * b + q + 3)
                        nc.vector.tensor_tensor(new[:], v, brow[:].unsqueeze(1).broadcast_to([P, TPH, F]),
                                                ALU.add).then_inc(out_step, 1)
                    else:
                        dve.wait_ge(exped_out, 2 * b + q + 1)
                        nc.vector.tensor_scalar(e[:], e[:], 1.0, -1.0, ALU.min, ALU.add).then_inc(out_step, 1)
                        dve.wait_ge(out_step, step + 1)
                        nc.vector.scalar_tensor_tensor(out=new[:].rearrange("p i f -> p (i f)"), in0=at.ps_post[:, 0:TPH * F], scalar=0.0,
                                                       in1=e[:].rearrange("p i f -> p (i f)"),
                                                       op0=ALU.max, op1=ALU.add).then_inc(out_step, 1)
                    dve.wait_ge(out_step, step + OUT - 1)
                    rows = x[:, bass.ds(b * NT + q * TPH, TPH), :]
                    nc.vector.tensor_tensor(rows, rows, new[:], ALU.add).then_inc(out_step, 1)
                    dve.wait_ge(out_step, step + OUT)

        @block.scalar
        def _(act):
            with act.Fori(0, B) as b:
                def exp(i):
                    act.wait_ge(at.masked, 8 * b + i + 3)
                    c = slice(i % 4, i % 4 + 1)
                    nc.scalar.activation(at.prob[i % 4][:], at.prob[i % 4][:], ACT.Exp, bias=at.negmax[:, c],
                                         scale=1.0 if weighted else -1.0,
                                         accum_out=at.rowsum[:, c]).then_inc(at.exped, 1)

                def shift(i):
                    act.wait_ge(leaned, 8 * b + i + 1)
                    nc.scalar.activation(at.prob[i % 4][:], at.prob[i % 4][:], ACT.Identity,
                                         bias=s02[:, i, 0:1]).then_inc(shifted, 1)

                at.act_xhh(act, b, b)
                at.act_xhl(act, b)
                act.wait_ge(projected, 3 * b + 3)
                nc.scalar.activation(d1[:], at.ps_score[0][:], ACT.Copy).then_inc(termed, 1)
                nc.scalar.activation(d02[:], at.ps_score[0][:], ACT.Copy, scale=SLOPE).then_inc(termed, 1)
                src = at.ps_post[:, 0:2 * NT].rearrange("p (i c) -> p i c", c=2)
                nc.scalar.activation(s08[:], src, ACT.Copy, scale=1.0 - SLOPE).then_inc(termed, 1)
                nc.scalar.activation(s02[:], src, ACT.Copy, scale=SLOPE).then_inc(termed, 1)
                if weighted:
                    act.wait_ge(termed, 4 * b + 4)
                    shift(0)
                for i in range(NT + 2):
                    if weighted and i + 1 < NT:
                        shift(i + 1)
                    if i < NT:
                        exp(i)
                    if i >= 2:
                        for j in range(2):
                            at.act_high(act, b, i - 2, j)
                if not weighted:
                    for q in range(2):
                        act.wait_ge(at.posted, 2 * b + q + 3)
                        if q == 1:
                            act.wait_ge(out_step, 2 * OUT * b + OUT)
                        nc.scalar.activation(e[:], at.ps_post[:, 0:TPH * F].rearrange("p (i f) -> p i f", f=F),
                                             ACT.Exp).then_inc(exped_out, 1)

        @block.gpsimd
        def _(pool):
            with pool.Fori(0, B) as b:
                at.pool_pair(pool, b, hx)
                for i in range(NT):
                    at.pool_norm(pool, b, i)


def load_adjacency(nc, adj, pairs):
    loaded, set_ones = nc.alloc_semaphore("adj_loaded"), nc.alloc_semaphore("adj_ones")
    with nc.Block() as block:
        @block.sync
        def _(sp):
            sp.dma_start(pairs[:], adj.rearrange("(k p) m -> p k m", p=P)).then_inc(loaded, 16)
            sp.wait_ge(loaded, 16)

        @block.gpsimd
        def _(pool):
            pool.wait_ge(loaded, 16)
            nc.gpsimd.affine_select(out=pairs[:], in_=pairs[:], compare_op=ALU.not_equal, fill=1.0, base=0,
                                    pattern=[[P, NT], [-1, N]], channel_multiplier=1).then_inc(set_ones, 1)


def build(nc, B, layers, x_in, adj, L0, L1, L2, L3, out):
    with ExitStack() as ctx:
        sb = lambda n, s, d=F32: ctx.enter_context(nc.sbuf_tensor(n, s, d))
        sem = lambda n: ctx.enter_context(nc.semaphore(n))
        x = sb("x", [P, B * NT, F])
        hx = sb("hx", [P, B * NT, F])
        mask = sb("mask", [P, NT, N], BF16)
        ident = sb("ident", [P, P])
        fold = sb("fold", [P, F])
        loaded, made, masked, stored = sem("loaded"), sem("made"), sem("mask_made"), sem("stored")
        with ExitStack() as own:
            adj_rows = own.enter_context(nc.sbuf_tensor("adj_rows", [P, NT, N], F32))
            with nc.Block() as block:
                @block.sync
                def _(sp):
                    sp.dma_start(x[:], x_in.rearrange("b (k p) f -> p (b k) f", p=P)).then_inc(loaded, 16)
                    sp.dma_start(adj_rows[:], adj.rearrange("(k p) m -> p k m", p=P)).then_inc(loaded, 16)
                    sp.wait_ge(loaded, 32)

                @block.gpsimd
                def _(pool):
                    nc.gpsimd.memset(ident[:], 0.0).then_inc(made, 1)
                    nc.gpsimd.memset(fold[:], 0.0).then_inc(made, 1)
                    pool.wait_ge(made, 2)
                    nc.gpsimd.affine_select(out=ident[:], in_=ident[:], compare_op=ALU.not_equal, fill=1.0,
                                            base=0, pattern=[[-1, P]], channel_multiplier=1).then_inc(made, 1)
                    for k, at in enumerate((0, -F)):
                        nc.gpsimd.affine_select(out=fold[:], in_=fold[:], compare_op=ALU.not_equal, fill=1.0,
                                                base=at, pattern=[[-1, F]], channel_multiplier=1).then_inc(made, 1)
                        pool.wait_ge(made, 4 + k)

                @block.vector
                def _(dve):
                    dve.wait_ge(loaded, 32)
                    nc.vector.tensor_scalar(mask[:], adj_rows[:], 0.0, MASKED, ALU.is_equal, ALU.mult).then_inc(masked, 1)
        def layer(k, norm_and_attend):
            if k not in layers:
                return
            with nc.cleanup_on_exit(), ExitStack() as own:
                norm_and_attend(own)

        def layer_0(own):
            with ExitStack() as norm:
                layer_norm_relu(nc, norm, B, x, hx, "ln0")
            layer0(nc, own, B, x, hx, ident, fold, adj, *L0)

        def layer_1(own):
            with ExitStack() as norm:
                layer_norm_relu(nc, norm, B, x, hx, "ln1")
            layer1(nc, own, B, x, hx, mask, ident, fold, *L1)

        def layer_2(own):
            with ExitStack() as norm:
                layer_norm_relu(nc, norm, B, x, hx, "ln2")
            edges = own.enter_context(nc.sbuf_tensor("edges", [P, NT, N], F32))
            load_adjacency(nc, adj, edges)
            edge_layer(nc, own, B, x, hx, edges, ident, "l2", *L2)

        def layer_3(own):
            with ExitStack() as norm:
                layer_norm_relu(nc, norm, B, x, hx, "ln3")
            edge_layer(nc, own, B, x, hx, mask, ident, "l3", *L3, None)

        for k, norm_and_attend in enumerate((layer_0, layer_1, layer_2, layer_3)):
            layer(k, norm_and_attend)
        with nc.Block() as block:
            @block.sync
            def _(sp):
                sp.dma_start(out.rearrange("b (k p) f -> p (b k) f", p=P), x[:]).then_inc(stored, 16)
                sp.wait_ge(stored, 16)


_INS = ['x', 'adj', 'L0_gnn_H', 'L0_gnn_W', 'L0_gnn_W_ind', 'L0_gnn_a_node', 'L0_gnn_a_gn', 'L0_gnn_a_ge',
        'L0_gnn_fcW', 'L0_gnn_fcb', 'L0_gnn_av', 'L1_gnn_Wh', 'L1_gnn_bh', 'L1_gnn_W_out', 'L1_gnn_b_out',
        'L2_gnn_weight', 'L2_gnn_a', 'L2_gnn_bias', 'L3_gnn_W', 'L3_gnn_a']
_OUTS = [((8, 1024, 64), 'float32')]


def kernel(**inputs):
    import numpy as _np
    import concourse.bacc as _bacc
    from concourse import mybir as _mybir
    from concourse.bass_utils import run_bass_kernel_spmd as _run

    nc = _bacc.Bacc("TRN2", target_bir_lowering=False, num_devices=1)
    arrays, args = {}, {}
    for name in _INS:
        arrays[f"in_{name}_dram"] = _np.ascontiguousarray(inputs[name])
        args[name] = nc.dram_tensor(f"in_{name}_dram", arrays[f"in_{name}_dram"].shape,
                                    _mybir.dt.from_np(arrays[f"in_{name}_dram"].dtype), kind="ExternalInput").ap()
    shape, dtype = _OUTS[0]
    out = nc.dram_tensor("out_0_dram", shape, _mybir.dt.from_np(_np.dtype(dtype)), kind="ExternalOutput").ap()
    of_layer = [[args[n] for n in _INS if n.startswith(f"L{k}_")] for k in range(4)]
    build(nc, shape[0], (0, 1, 2, 3), args["x"], args["adj"], *of_layer, out)
    r = _run(nc, [arrays], core_ids=[0])
    return r.results[0]["out_0_dram"]
```

```python
from contextlib import ExitStack

import concourse.bass as bass
from concourse import mybir

ALU = mybir.AluOpType
ACT = mybir.ActivationFunctionType
AX = mybir.AxisListType
F32 = mybir.dt.float32
F32R = mybir.dt.float32r
BF16 = mybir.dt.bfloat16

P = 128
N = 1024
F = 64
NT = N // P
HALF = 512
TPH = HALF // P
HEADS = 8
HID = 128
MASKED = -1.0e16
EPS = 1e-5


def layer_norm_relu(nc, ctx, B, x, hx, name, loads, x_loaded=None):
    rows = B * NT
    stat = ctx.enter_context(nc.sbuf_tensor(f"{name}_stat", [P, 4, rows], F32))
    sq = ctx.enter_context(nc.sbuf_tensor(f"{name}_sq", [P, rows, F], F32))
    total, mean, var, rstd = (stat[:, i, :] for i in range(4))
    parts = (slice(0, rows // 2), slice(rows // 2, rows))
    step = nc.alloc_semaphore(f"{name}_dve_step")
    squared = nc.alloc_semaphore(f"{name}_squared")
    rooted = nc.alloc_semaphore(f"{name}_rooted")

    def over_features(col):
        return col.unsqueeze(2).broadcast_to([P, rows, F])

    with nc.Block() as block:
        @block.sync
        def _(sp):
            loads(sp)

        @block.vector
        def _(dve):
            if x_loaded is not None:
                dve.wait_ge(x_loaded, 16)
            nc.vector.tensor_reduce(total, x[:], AX.X, ALU.add).then_inc(step, 1)
            dve.wait_ge(step, 1)
            nc.vector.tensor_scalar(mean, total, 1.0 / F, None, ALU.mult).then_inc(step, 1)
            dve.wait_ge(step, 2)
            for part in parts:
                nc.vector.tensor_tensor(hx[:, part], x[:, part], over_features(mean)[:, part], ALU.subtract)\
                    .then_inc(step, 1)
            for k, part in enumerate(parts):
                dve.wait_ge(squared, k + 1)
                nc.vector.tensor_reduce(total[:, part], sq[:, part], AX.X, ALU.add).then_inc(step, 1)
            dve.wait_ge(step, 6)
            nc.vector.tensor_scalar(var, total, 1.0 / F, EPS, ALU.mult, ALU.add).then_inc(step, 1)
            dve.wait_ge(rooted, 1)
            nc.vector.reciprocal(rstd, mean).then_inc(step, 1)
            dve.wait_ge(step, 8)
            nc.vector.scalar_tensor_tensor(out=hx[:], in0=hx[:], scalar=0.0, in1=over_features(rstd),
                                           op0=ALU.max, op1=ALU.mult).then_inc(step, 1)

        @block.scalar
        def _(act):
            for k, part in enumerate(parts):
                act.wait_ge(step, k + 3)
                nc.scalar.activation(sq[:, part], hx[:, part], ACT.Square).then_inc(squared, 1)
            act.wait_ge(step, 7)
            nc.scalar.activation(mean, var, ACT.Sqrt).then_inc(rooted, 1)


def layer0(nc, ctx, B, x_in, x, hx, mask, ident, fold, adj, H, W, W_ind, a_node, a_gn, a_ge, fcW, fcb, av):
    sb = lambda n, s, d=F32: ctx.enter_context(nc.sbuf_tensor(f"l0_{n}", s, d))
    sem = lambda n: nc.alloc_semaphore(f"l0_{n}")
    E = H.shape[1]
    PAIRS = E // 2
    ps_a, ps_b, ps_c, ps_d = (ctx.enter_context(nc.psum_tensor(f"l0_ps_{n}", [P, N], F32)) for n in "abcd")
    halves = [slice(q * HALF, (q + 1) * HALF) for q in range(2)]

    adj_t = sb("adj_t", [P, NT, N])
    mask_rows = sb("mask_rows", [P, NT, E])
    mask_cols = sb("mask_cols", [E, N])
    w_st = sb("w_st", [P, P], F32R)
    both_st = sb("both_st", [P, P], F32R)
    v_st = sb("v_st", [P, 2, P], F32R)
    fcw, fcb_col, age_col = sb("fcw", [F, P]), sb("fcb_col", [P, 1]), sb("age_col", [F, 1])
    av_rep, av_neg = sb("av_rep", [P, P]), sb("av_neg", [P, P])
    ones = sb("ones", [P, P])
    fold2 = sb("fold2", [P, 2, F])

    with ExitStack() as own:
        mine = lambda n, s, d=F32: own.enter_context(nc.sbuf_tensor(f"l0_{n}", s, d))
        rows = mine("rows", [P, NT, N])
        h_rows = mine("h_rows", [P, NT, E])
        w_in, both_in = mine("w_in", [P, 2, F]), mine("both_in", [P, 2, F])
        w_t = mine("w_t", [F, P])
        cols = mine("cols", [F, 2])
        a_rep = mine("a_rep", [F, 2, P])
        av_col = mine("av_col", [P, 1])
        deg = mine("deg", [P, NT, 3])
        names = ("x_in loaded adj_in mask_made summed floored inverted scaled hmask spread "
                 "w_turned w_copied v_ready v_hi w_hi "
                 "w_lo turned untied_even untied_odd hm_turned hm_copied const")
        S = {n: nc.alloc_semaphore(f"l0s_{n}") for n in names.split()}
        SMALL = 15 * 16

        def loads(sp):
            sp.dma_start(x[:], x_in.rearrange("b (k p) f -> p (b k) f", p=P)).then_inc(S["x_in"], 16)
            sp.dma_start(rows[:], adj.rearrange("(k p) m -> p k m", p=P)).then_inc(S["adj_in"], 16)
            sp.dma_start(h_rows[:], H.rearrange("(k p) e -> p k e", p=P)).then_inc(S["loaded"], 16)
            for to, sources in ((w_in, (W, W)), (both_in, (W, W_ind))):
                for r in range(2):
                    for c, src in enumerate(sources):
                        sp.dma_start(to[r * F:(r + 1) * F, c, :], src).then_inc(S["loaded"], 16)
            sp.dma_start(fcw[:], fcW).then_inc(S["loaded"], 16)
            with nc.allow_non_contiguous_dma(reason="a few hundred numbers"):
                col = lambda v: v.rearrange("(f o) -> f o", o=1)
                for to, src in ((fcb_col[:], fcb), (age_col[:], a_ge), (cols[:, 0:1], a_node),
                                (cols[:, 1:2], a_gn), (av_col[:], av)):
                    sp.dma_start(to, col(src)).then_inc(S["loaded"], 16)

        with nc.Block() as block:
            @block.gpsimd
            def _(pool):
                nc.gpsimd.memset(ident[:], 0.0).then_inc(S["const"], 1)
                nc.gpsimd.memset(fold[:], 0.0).then_inc(S["const"], 1)
                nc.gpsimd.memset(ones[:], 1.0).then_inc(S["const"], 1)
                pool.wait_ge(S["const"], 3)
                nc.gpsimd.affine_select(out=ident[:], in_=ident[:], compare_op=ALU.not_equal, fill=1.0, base=0,
                                        pattern=[[-1, P]], channel_multiplier=1).then_inc(S["const"], 1)
                for k, first in enumerate((0, -F)):
                    nc.gpsimd.affine_select(out=fold[:], in_=fold[:], compare_op=ALU.not_equal, fill=1.0,
                                            base=first, pattern=[[-1, F]], channel_multiplier=1)\
                        .then_inc(S["const"], 1)
                    pool.wait_ge(S["const"], 5 + k)
                nc.gpsimd.tensor_copy(fold2[:], fold[:].unsqueeze(1).broadcast_to([P, 2, F])).then_inc(S["const"], 1)

        with ExitStack() as norm:
            layer_norm_relu(nc, norm, B, x, hx, "ln0", loads, S["x_in"])

        with nc.Block() as block:

            @block.vector
            def _(dve):
                dve.wait_ge(S["loaded"], SMALL)
                nc.vector.tensor_copy(a_rep[:], cols[:].unsqueeze(2).broadcast_to([F, 2, P])).then_inc(S["spread"], 1)
                nc.vector.tensor_copy(av_rep[:], av_col[:].broadcast_to([P, P])).then_inc(S["spread"], 1)
                nc.vector.tensor_scalar(av_neg[:], av_col[:].broadcast_to([P, P]), -1.0, None,
                                        ALU.mult).then_inc(S["spread"], 1)
                nc.vector.tensor_scalar(mask_rows[:], h_rows[:], 0.0, MASKED, ALU.is_le, ALU.mult)\
                    .then_inc(S["hmask"], 1)
                dve.wait_ge(S["w_turned"], 1)
                nc.vector.tensor_copy(w_t[:], ps_a[0:F, 0:P]).then_inc(S["w_copied"], 1)
                dve.wait_ge(S["w_hi"], 2)
                for k, (to, src) in enumerate(((w_st, w_in), (both_st, both_in))):
                    nc.vector.tensor_tensor(to[F:P, :], src[F:P].rearrange("p c f -> p (c f)"),
                                            to[F:P, :].bitcast(F32), ALU.subtract).then_inc(S["w_lo"], 1)
                dve.wait_ge(S["v_hi"], 1)
                nc.vector.tensor_tensor(v_st[F:P], ps_b[F:P, 0:2 * P].rearrange("p (c n) -> p c n", n=P),
                                        v_st[F:P].bitcast(F32), ALU.subtract).then_inc(S["w_lo"], 1)
                dve.wait_ge(S["hm_turned"], 1)
                nc.vector.tensor_copy(mask_cols[:], ps_d[0:E, :]).then_inc(S["hm_copied"], 1)
                dve.wait_ge(S["adj_in"], 16)
                nc.vector.tensor_scalar(mask[:], rows[:], 0.0, MASKED, ALU.is_equal, ALU.mult)\
                    .then_inc(S["mask_made"], 1)
                dve.wait_ge(S["summed"], NT)
                nc.vector.tensor_scalar(deg[:, :, 1], deg[:, :, 0], 1.0, None, ALU.max).then_inc(S["floored"], 1)
                dve.wait_ge(S["floored"], 1)
                nc.vector.reciprocal(deg[:, :, 2], deg[:, :, 1]).then_inc(S["inverted"], 1)
                dve.wait_ge(S["inverted"], 1)
                dve.wait_ge(S["mask_made"], 1)
                for k in range(NT):
                    nc.vector.tensor_scalar(rows[:, k, :], rows[:, k, :], deg[:, k, 2:3], None, ALU.mult)\
                        .then_inc(S["scaled"], 1)
                for m in range(NT):
                    if m % 2 == 0:
                        dve.wait_ge(S["turned"], m + 1)
                        nc.vector.tensor_copy(adj_t[:, m, :], ps_a[:]).then_inc(S["untied_even"], 1)

            @block.scalar
            def _(act):
                act.wait_ge(S["adj_in"], 16)
                for k in range(NT):
                    nc.scalar.activation(adj_t[:, k, :], rows[:, k, :], ACT.Copy, accum_out=deg[:, k, 0:1])\
                        .then_inc(S["summed"], 1)
                act.wait_ge(S["loaded"], SMALL)
                for to, src in ((w_st, w_in), (both_st, both_in)):
                    nc.scalar.activation(to[:], src[:].rearrange("p c f -> p (c f)"), ACT.Copy).then_inc(S["w_hi"], 1)
                act.wait_ge(S["v_ready"], 1)
                nc.scalar.activation(v_st[:], ps_b[:, 0:2 * P].rearrange("p (c n) -> p c n", n=P), ACT.Copy)\
                    .then_inc(S["v_hi"], 1)
                for m in range(1, NT, 2):
                    act.wait_ge(S["turned"], m + 1)
                    nc.scalar.activation(adj_t[:, m, :], ps_c[:], ACT.Copy).then_inc(S["untied_odd"], 1)

            @block.tensor
            def _(pe):
                pe.wait_ge(S["loaded"], SMALL)
                nc.tensor.transpose(ps_a[0:F, 0:P], w_in[:, 0, :], ident[:]).then_inc(S["w_turned"], 1)
                pe.wait_ge(S["hmask"], 1)
                for k in range(NT):
                    last = nc.tensor.transpose(ps_d[0:E, k * P:(k + 1) * P], mask_rows[:, k, :], ident[:])
                last.then_inc(S["hm_turned"], 1)
                pe.wait_ge(S["w_copied"], 1)
                pe.wait_ge(S["spread"], 1)
                nc.tensor.matmul(ps_b[:, 0:2 * P], w_t[:], a_rep[:].rearrange("p c n -> p (c n)"),
                                 start=True, stop=True).then_inc(S["v_ready"], 1)
                pe.wait_ge(S["scaled"], NT)
                for m in range(NT):
                    bank = ps_a if m % 2 == 0 else ps_c
                    if m >= 2:
                        pe.wait_ge(S["untied_even"] if m % 2 == 0 else S["untied_odd"], m // 2)
                    for k in range(NT):
                        last = nc.tensor.transpose(bank[:, k * P:(k + 1) * P], rows[:, k, m * P:(m + 1) * P], ident[:])
                    last.then_inc(S["turned"], 1)

    pair = sb("pair", [P, NT, 2, F])
    xhh, xll = sb("xhh", [P, N], F32R), sb("xll", [P, N], F32R)
    h_t = sb("h_t", [P, N])
    h_n = sb("h_n", [P, NT, P])
    al = sb("al", [E, N])
    al_t = sb("al_t", [P, NT, E])
    al_stat = sb("al_stat", [E, 3])
    agg2, nagg2 = sb("agg2", [P, PAIRS]), sb("nagg2", [P, PAIRS])
    agg_td = sb("agg_td", [F, 2, E])
    agg_t = sb("agg_t", [P, E])
    agg_e = sb("agg_e", [E, P])
    he_e, he = sb("he_e", [F, E]), sb("he", [F, E])
    u_t = sb("u_t", [P, E])
    age = sb("age", [P, 1])
    beta = sb("beta", [P, N])
    bhl, chl = sb("bhl", [P, N], F32R), sb("chl", [P, N], F32R)
    lc = sb("lc", [P, NT, E])
    lc_stat = sb("lc_stat", [P, 3, NT])
    c_n = sb("c_n", [P, NT, 2, E])
    m1, c1 = sb("m1", [E, N]), sb("c1", [E, N])
    hlin = sb("hlin", [P, N])
    zc = [sb(f"zc{i}", [P, N]) for i in range(2)]
    r = [sb(f"r{i}", [P, N]) for i in range(4)]
    ex = [sb(f"ex{i}", [P, N]) for i in range(2)]
    u = [sb(f"u{i}", [P, N]) for i in range(2)]
    sel_b, sel_c = ([sb(f"sel_{n}{i}", [P, 2, F], F32R) for i in range(2)] for n in "bc")
    g_t = sb("g_t", [P, N])
    ind = sb("ind", [P, N])
    xw = sb("xw", [P, NT, P])
    tg, ti = zc[0], zc[1]
    mix = r[0]
    res = r[1]

    names = ("paired xt hh ll ht ht_out v hg hn hn_out v02 lean peak alex alinv alnorm al_turned al_out agg "
             "agg_td agg_out agg_back agg_e he_ex he_min he_done age ut ut_out se age_out tanh_b beta bhi blo lc mx "
             "lcs lce lcsum lcinv c_n "
             "c_turned chi m1 c1 clo lin bsum hlin g xw_out ind ind_out sg sg_out si si_out diff wt wt2 d dw "
             "res res_t added passed pe_passed")
    S = {n: sem(n) for n in names.split()}
    names = "selb selc b_in zc_done r_done ex_done t_done c_in u_done folded"
    T = {n: sem(n) for n in names.split()}
    LAG = 3

    with nc.Block() as block:
        def pairs_of(loop, step):
            ends = lambda s: lambda k: 0 <= s - k < PAIRS
            for s in range(4):
                step(s, s % 4, ends(s))
            with loop(4, PAIRS - 7, 4) as s0:
                for j in range(4):
                    step(s0 + j, j, lambda k: True)
            for s in range(PAIRS - 4, PAIRS + LAG + 1):
                step(s, s % 4, ends(s))

        def batches(loop, all_pairs, transition, early):
            for s in early:
                early[s](0)
            transition(None, 0)
            if B > 1:
                with loop(0, B - 1) as b:
                    all_pairs(b)
                    transition(b, b + 1)
            all_pairs(B - 1)
            transition(B - 1, None)

        def next_early(b, s, early):
            if isinstance(s, int) and s in early and not (isinstance(b, int) and b == B - 1):
                early[s](b + 1)

        @block.gpsimd
        def _(pool):
            def copy_pair(n):
                rows = hx[:, n * NT:(n + 1) * NT, :] if isinstance(n, int) else hx[:, bass.ds(n * NT, NT), :]
                nc.gpsimd.tensor_copy(pair[:], rows.unsqueeze(2).broadcast_to([P, NT, 2, F])).then_inc(S["paired"], 1)

            def all_pairs(b):
                def step(s, j, has):
                    if has(1):
                        pool.wait_ge(T["ex_done"], PAIRS * b + s)
                        nc.gpsimd.tensor_tensor(r[(j - 1) % 4][:], r[(j - 1) % 4][:], ex[(j - 1) % 2][:], ALU.add)\
                            .then_inc(T["t_done"], 1)

                if not isinstance(b, int) or b < B - 1:
                    pool.wait_ge(S["xt"], b + 1)
                    pool.sem_inc(S["passed"], 1)
                    copy_pair(b + 1)
                pairs_of(pool.Fori, step)

            copy_pair(0)
            batches(pool.Fori, all_pairs, lambda b, n: None, {})

        @block.tensor
        def _(pe):
            def product(out, lhs_t, parts):
                for c in halves:
                    for part in parts:
                        last = nc.tensor.matmul(out[:, c], lhs_t, part[:, c], start=(part is parts[0]),
                                                stop=(part is parts[-1]))
                return last

            def rows_of(out, weights):
                for k in range(NT):
                    c = slice(k * P, (k + 1) * P)
                    for part in (xhh, xll):
                        last = nc.tensor.matmul(out[:, c], part[:, c], weights[:], start=(part is xhh),
                                                stop=(part is xll))
                return last

            def industry(c):
                for m in range(NT):
                    last = nc.tensor.matmul(ps_b[:, c], xw[:, m, :], adj_t[:, m, c], start=(m == 0),
                                            stop=(m == NT - 1))
                return last

            def turn_x(n):
                if not isinstance(n, int):
                    pe.wait_ge(T["zc_done"], PAIRS * n)
                pe.wait_ge(S["paired"], n + 1)
                for k in range(NT):
                    last = nc.tensor.transpose(ps_a[:, k * P:(k + 1) * P],
                                               pair[:, k].rearrange("p c f -> p (c f)"), ident[:])
                last.then_inc(S["xt"], 1)

            def node_terms(n):
                pe.wait_ge(S["ll"], n + 1)
                product(ps_a, v_st[:, 0], (xhh, xll)).then_inc(S["v"], 1)

            early = {PAIRS: turn_x, PAIRS + 2: node_terms}

            def transition(b, n):
                ends, starts = b is not None, n is not None
                ended = lambda name: pe.wait_ge(S[name], b + 1)
                after = lambda name: pe.wait_ge(S[name], n + 1)
                if ends:
                    pe.wait_ge(T["u_done"], PAIRS * b + PAIRS)
                    product(ps_d, fcw[:], (ind[0:F, :],)).then_inc(S["si"], 1)
                if ends:
                    ended("g")
                    product(ps_b, fcw[:], (g_t[0:F, :],)).then_inc(S["sg"], 1)
                    ended("si_out")
                if starts:
                    rows_of(ps_d, both_st).then_inc(S["hn"], 1)
                    after("alnorm")
                    pe.sem_inc(S["pe_passed"], 1)
                    for k in range(NT):
                        last = nc.tensor.transpose(ps_a[:, k * E:(k + 1) * E], al[:, k * P:(k + 1) * P],
                                                   ident[0:E, 0:E])
                    last.then_inc(S["al_turned"], 1)
                if ends:
                    ended("sg_out")
                    for c in halves:
                        nc.tensor.matmul(ps_c[:, c], av_rep[:], tg[:, c], start=True, stop=False)
                        last = nc.tensor.matmul(ps_c[:, c], av_neg[:], ti[:, c], start=False, stop=True)
                    last.then_inc(S["diff"], 1)
                if starts:
                    product(ps_b, w_st[:], (xhh, xll)).then_inc(S["ht"], 1)
                    if ends:
                        ended("wt")
                    product(ps_c, v_st[:, 1], (xhh, xll)).then_inc(S["hg"], 1)
                    after("hn_out")
                    after("xw_out")
                    after("al_out")
                    after("ht_out")
                    for k in range(NT):
                        last = nc.tensor.matmul(ps_b[:, 0:E], h_n[:, k, :], al_t[:, k, :], start=(k == 0),
                                                stop=(k == NT - 1))
                    last.then_inc(S["agg"], 1)
                if ends:
                    ended("res")
                    pe.sem_inc(S["pe_passed"], 1)
                    for k in range(NT):
                        last = nc.tensor.transpose(ps_d[:, k * F:(k + 1) * F], res[0:F, k * P:(k + 1) * P],
                                                   ident[0:F, 0:F])
                    last.then_inc(S["res_t"], 1)
                if not starts:
                    return
                after("agg_out")
                nc.tensor.matmul(ps_a[:, 0:1], agg_td[:].rearrange("p c e -> p (c e)"), age_col[:],
                                 start=True, stop=True).then_inc(S["age"], 1)
                nc.tensor.transpose(ps_b[0:E, HALF:HALF + P], agg_t[:], ident[:]).then_inc(S["agg_back"], 1)
                after("he_done")
                nc.tensor.matmul(ps_a[:, HALF:HALF + E], fcw[:], he[:], start=True, stop=True).then_inc(S["ut"], 1)
                after("ut_out")
                after("age_out")
                nc.tensor.matmul(ps_a[:, 0:E], av_rep[:], u_t[:], start=True, stop=True).then_inc(S["se"], 1)
                after("agg_e")
                industry(halves[0])
                if ends:
                    ended("added")
                after("c_n")
                for k in range(NT):
                    last = nc.tensor.transpose(ps_d[:, k * P:(k + 1) * P],
                                               c_n[:, k].rearrange("p c e -> p (c e)"), ident[:])
                last.then_inc(S["c_turned"], 1)
                industry(halves[1]).then_inc(S["ind"], 1)
                after("m1")
                product(ps_a, ones[0:E, :], (m1,)).then_inc(S["bsum"], 1)
                after("c1")
                after("tanh_b")
                for c in halves:
                    last = nc.tensor.matmul(ps_c[:, c], agg_e[:], c1[:, c], start=True, stop=False)
                last.then_inc(S["lin"], 1)
                after("hlin")
                after("blo")
                after("clo")
                after("ind_out")

            def all_pairs(b):
                column = lambda sel, j: sel[j % 2][:].rearrange("p c f -> p (c f)")

                def step(s, j, has):
                    n = PAIRS * b + s
                    if has(3):
                        pe.wait_ge(T["selc"], n - 2)
                        if has(4):
                            pe.wait_ge(T["u_done"], n - 3)
                        product(ps_d, column(sel_c, j - 3), (chl,)).then_inc(T["c_in"], 1)
                    if has(-1):
                        pe.wait_ge(T["selb"], n + 2)
                        if has(1):
                            pe.wait_ge(T["zc_done"], n)
                        product((ps_a, ps_b)[(j + 1) % 2], column(sel_b, j + 1), (bhl,)).then_inc(T["b_in"], 1)
                    if has(4):
                        pe.wait_ge(T["u_done"], n - 3)
                        final = isinstance(s, int) and s == PAIRS + LAG
                        for c in halves:
                            last = nc.tensor.matmul(ps_c[:, c], fold2[:].rearrange("p c f -> p (c f)"),
                                                    u[(j - 4) % 2][:, c], start=False, stop=final)
                        last.then_inc(T["folded"], 1)
                    next_early(b, s, early)

                pe.wait_ge(T["selb"], PAIRS * b + 1)
                product(ps_a, column(sel_b, 0), (bhl,)).then_inc(T["b_in"], 1)
                pairs_of(pe.Fori, step)

            batches(pe.Fori, all_pairs, transition, early)

        @block.vector
        def _(dve):
            tt, ts, stt = nc.vector.tensor_tensor, nc.vector.tensor_scalar, nc.vector.scalar_tensor_tensor

            def low_x(n):
                dve.wait_ge(S["hh"], n + 1)
                tt(xll[:], ps_a[:], xhh[:].bitcast(F32), ALU.subtract).then_inc(S["ll"], 1)

            def node_scores(n):
                dve.wait_ge(S["v02"], n + 1)
                stt(out=al[:], in0=ps_a[0:E, :], scalar=1.0, in1=m1[:], op0=ALU.mult, op1=ALU.max)\
                    .then_inc(S["lean"], 1)
                dve.wait_ge(S["lean"], n + 1)
                dve.sem_inc(S["passed"], 1)
                nc.vector.tensor_tensor_reduce(out=al[:], in0=al[:], in1=mask_cols[:], scale=-1.0, scalar=3.0e38,
                                               op0=ALU.add, op1=ALU.min, accum_out=al_stat[:, 0:1])\
                    .then_inc(S["peak"], 1)

            early = {PAIRS + 1: low_x, PAIRS + 3: node_scores}

            def transition(b, n):
                ends, starts = b is not None, n is not None
                ended = lambda name: dve.wait_ge(S[name], b + 1)
                after = lambda name: dve.wait_ge(S[name], n + 1)
                if ends:
                    dve.wait_ge(T["folded"], PAIRS * b + PAIRS)
                    stt(out=g_t[:], in0=ps_c[:], scalar=-1.0, in1=hlin[:], op0=ALU.add, op1=ALU.add).then_inc(S["g"], 1)
                if starts:
                    after("alex")
                    nc.vector.reciprocal(al_stat[:, 2:3], al_stat[:, 1:2]).then_inc(S["alinv"], 1)
                    after("alinv")
                    ts(al[:], al[:], al_stat[:, 2:3], None, ALU.mult).then_inc(S["alnorm"], 1)
                if ends:
                    ended("g")
                    tt(res[:], g_t[:], ind[:], ALU.subtract).then_inc(S["d"], 1)
                if starts:
                    after("al_turned")
                    nc.vector.tensor_copy(al_t[:].rearrange("p k e -> p (k e)"), ps_a[:, 0:NT * E])\
                        .then_inc(S["al_out"], 1)
                if ends:
                    ended("wt")
                    ts(mix[:], mix[:], 0.5, 0.5, ALU.mult, ALU.add).then_inc(S["wt2"], 1)
                    ended("wt2")
                    tt(res[:], res[:], mix[:], ALU.mult).then_inc(S["dw"], 1)
                    ended("dw")
                    tt(res[:], res[:], ind[:], ALU.add).then_inc(S["res"], 1)
                if starts:
                    after("agg")
                    nc.vector.tensor_copy(agg_td[:], ps_b[0:F, 0:E].unsqueeze(1).broadcast_to([F, 2, E]))\
                        .then_inc(S["agg_td"], 1)
                    nc.vector.tensor_copy(agg_t[:], ps_b[:, 0:E]).then_inc(S["agg_out"], 1)
                    for c in range(2):
                        part = ps_b[c * F:(c + 1) * F, c * PAIRS:(c + 1) * PAIRS]
                        nc.vector.tensor_copy(agg2[c * F:(c + 1) * F, :], part)
                        ts(nagg2[c * F:(c + 1) * F, :], part, -1.0, None, ALU.mult)
                if ends:
                    ended("res_t")
                    rows = x[:, bass.ds(b * NT, NT), :]
                    tt(rows, rows, ps_d[:, 0:NT * F].rearrange("p (k f) -> p k f", f=F), ALU.add)\
                        .then_inc(S["added"], 1)
                if not starts:
                    return
                after("he_ex")
                ts(he_e[:], he_e[:], 1.0, -1.0, ALU.min, ALU.add).then_inc(S["he_min"], 1)
                after("he_min")
                stt(out=he[:], in0=agg_td[:, 0, :], scalar=0.0, in1=he_e[:], op0=ALU.max, op1=ALU.add)\
                    .then_inc(S["he_done"], 1)
                after("agg_back")
                nc.vector.tensor_copy(agg_e[:], ps_b[0:E, HALF:HALF + P]).then_inc(S["agg_e"], 1)
                after("tanh_b")
                ts(beta[:], beta[:], 0.5, 0.5, ALU.mult, ALU.add).then_inc(S["beta"], 1)
                after("bhi")
                tt(bhl[F:P, :], beta[F:P, :], bhl[F:P, :].bitcast(F32), ALU.subtract).then_inc(S["blo"], 1)
                wide = [P, NT, E]
                over_e = lambda i: lc_stat[:, i, :].unsqueeze(2).broadcast_to(wide)
                after("se")
                tt(lc[:], mask_rows[:], ps_a[:, 0:E].unsqueeze(1).broadcast_to(wide), ALU.add).then_inc(S["lc"], 1)
                after("lc")
                nc.vector.tensor_reduce(lc_stat[:, 0, :], lc[:], AX.X, ALU.max).then_inc(S["mx"], 1)
                after("mx")
                tt(lc[:], lc[:], over_e(0), ALU.subtract).then_inc(S["lcs"], 1)
                after("lce")
                nc.vector.tensor_reduce(lc_stat[:, 1, :], lc[:], AX.X, ALU.add).then_inc(S["lcsum"], 1)
                after("lcsum")
                nc.vector.reciprocal(lc_stat[:, 2, :], lc_stat[:, 1, :]).then_inc(S["lcinv"], 1)
                after("lcinv")
                for c in range(2):
                    last = tt(c_n[:, :, c, :], lc[:], over_e(2), ALU.mult)
                last.then_inc(S["c_n"], 1)
                after("c_turned")
                after("chi")
                tt(m1[:], ps_d[0:E, :], beta[0:E, :], ALU.mult).then_inc(S["m1"], 1)
                after("m1")
                tt(c1[:], ps_d[0:E, :], m1[:], ALU.subtract).then_inc(S["c1"], 1)
                tt(chl[F:P, :], ps_d[F:P, :], chl[F:P, :].bitcast(F32), ALU.subtract).then_inc(S["clo"], 1)
                after("bsum")
                tt(hlin[:], h_t[:], ps_a[:], ALU.mult).then_inc(S["hlin"], 1)

            def all_pairs(b):
                def step(s, j, has):
                    n = PAIRS * b + s
                    if has(0):
                        if has(2):
                            dve.wait_ge(T["r_done"], n - 1)
                        dve.wait_ge(T["b_in"], n + 1)
                        stt(out=zc[j % 2][:], in0=h_t[:], scalar=agg2[:, bass.ds(s, 1)], in1=(ps_a, ps_b)[j % 2][:],
                            op0=ALU.subtract, op1=ALU.mult).then_inc(T["zc_done"], 1)
                    if has(3):
                        dve.wait_ge(T["t_done"], n - 2)
                        if has(5):
                            dve.wait_ge(T["folded"], n - 4)
                        dve.wait_ge(T["c_in"], n - 2)
                        tt(u[(j - 3) % 2][:], r[(j - 3) % 4][:], ps_d[:], ALU.mult).then_inc(T["u_done"], 1)
                    next_early(b, s, early)

                pairs_of(dve.Fori, step)

            batches(dve.Fori, all_pairs, transition, early)

        @block.scalar
        def _(act):
            fn = nc.scalar.activation

            def high_x(n):
                act.wait_ge(S["xt"], n + 1)
                fn(xhh[:], ps_a[:], ACT.Copy).then_inc(S["hh"], 1)

            def node_slope(n):
                act.wait_ge(S["v"], n + 1)
                fn(m1[:], ps_a[0:E, :], ACT.Copy, scale=0.2).then_inc(S["v02"], 1)

            def node_exp(n):
                act.wait_ge(S["peak"], n + 1)
                fn(al[:], al[:], ACT.Exp, bias=al_stat[:, 0:1], scale=-1.0, accum_out=al_stat[:, 1:2])\
                    .then_inc(S["alex"], 1)

            early = {PAIRS + 1: high_x, PAIRS + 2: node_slope, PAIRS + 3: node_exp}

            def transition(b, n):
                ends, starts = b is not None, n is not None
                ended = lambda name: act.wait_ge(S[name], b + 1)
                after = lambda name: act.wait_ge(S[name], n + 1)
                if ends:
                    ended("si")
                    fn(ti[:], ps_d[:], ACT.Tanh, bias=fcb_col[:, 0:1]).then_inc(S["si_out"], 1)
                    ended("sg")
                    fn(tg[:], ps_b[:], ACT.Tanh, bias=fcb_col[:, 0:1]).then_inc(S["sg_out"], 1)
                if starts:
                    after("hn")
                    both = ps_d[:].rearrange("p (k c f) -> p k c f", c=2, f=F)
                    twice = [P, NT, 2, F]
                    fn(h_n[:].rearrange("p k (c f) -> p k c f", f=F),
                       both[:, :, 0, :].unsqueeze(2).broadcast_to(twice), ACT.Copy).then_inc(S["hn_out"], 1)
                    fn(xw[:].rearrange("p k (c f) -> p k c f", f=F),
                       both[:, :, 1, :].unsqueeze(2).broadcast_to(twice), ACT.Copy).then_inc(S["xw_out"], 1)
                if ends:
                    ended("diff")
                    fn(mix[:], ps_c[:], ACT.Tanh, scale=0.5).then_inc(S["wt"], 1)
                if not starts:
                    return
                after("ht")
                fn(h_t[:], ps_b[:], ACT.Copy).then_inc(S["ht_out"], 1)
                after("agg_td")
                fn(he_e[:], agg_td[:, 0, :], ACT.Exp).then_inc(S["he_ex"], 1)
                after("age")
                fn(age[:], ps_a[:, 0:1], ACT.Copy, scale=0.5).then_inc(S["age_out"], 1)
                after("ut")
                fn(u_t[:], ps_a[:, HALF:HALF + E], ACT.Tanh, bias=fcb_col[:, 0:1]).then_inc(S["ut_out"], 1)
                after("hg")
                after("age_out")
                fn(beta[:], ps_c[:], ACT.Tanh, bias=age[:, 0:1], scale=0.5).then_inc(S["tanh_b"], 1)
                after("beta")
                fn(bhl[:], beta[:], ACT.Copy).then_inc(S["bhi"], 1)
                after("lcs")
                fn(lc[:], lc[:], ACT.Exp).then_inc(S["lce"], 1)
                after("c_turned")
                fn(chl[:], ps_d[:], ACT.Copy).then_inc(S["chi"], 1)
                after("ind")
                fn(ind[:], ps_b[:], ACT.Copy).then_inc(S["ind_out"], 1)

            def all_pairs(b):
                def select(to, k, done):
                    src = fold[:].rearrange("p (c k) -> p c k", k=PAIRS)[:, :, bass.ds(k, 1)]
                    fn(to[:], src.broadcast_to([P, 2, F]), ACT.Copy).then_inc(done, 1)

                def step(s, j, has):
                    n = PAIRS * b + s
                    if has(2):
                        if has(4):
                            act.wait_ge(T["c_in"], n - 3)
                            act.sem_inc(S["passed"], 1)
                        select(sel_c[j % 2], s - 2, T["selc"])
                    if has(-2):
                        act.wait_ge(T["b_in"], n + 1)
                        act.sem_inc(S["passed"], 1)
                        select(sel_b[j % 2], s + 2, T["selb"])
                    if has(0):
                        if has(4):
                            act.wait_ge(T["u_done"], n - 3)
                        act.wait_ge(T["zc_done"], n + 1)
                        act.sem_inc(S["passed"], 1)
                        fn(r[j % 4][:], zc[j % 2][:], ACT.Relu, bias=nagg2[:, bass.ds(s, 1)], scale=-1.0)\
                            .then_inc(T["r_done"], 1)
                    if has(1):
                        if has(3):
                            act.wait_ge(T["t_done"], n - 2)
                        act.wait_ge(T["r_done"], n)
                        fn(ex[(j - 1) % 2][:], r[(j - 1) % 4][:], ACT.Exp, scale=-1.0).then_inc(T["ex_done"], 1)
                    next_early(b, s, early)

                for k in range(2):
                    select(sel_b[k], k, T["selb"])
                pairs_of(act.Fori, step)

            batches(act.Fori, all_pairs, transition, early)


class Attention:

    def __init__(self, nc, ctx, name):
        sb = lambda n, s, d=F32: ctx.enter_context(nc.sbuf_tensor(f"{name}_{n}", s, d))
        sem = lambda n: nc.alloc_semaphore(f"{name}_{n}")
        ps = lambda n, s: ctx.enter_context(nc.psum_tensor(f"{name}_{n}", s, F32))
        self.nc = nc
        self.pair = sb("pair", [P, NT, 2, F])
        self.paired = sem("paired")
        self.prob = [sb(f"prob{i}", [P, N]) for i in range(4)]
        self.negmax = sb("negmax", [P, 4])
        self.rowsum = sb("rowsum", [P, 4])
        self.rowinv = sb("rowinv", [P, 4])
        self.pt_hi = [sb(f"pt_hi{i}", [P, NT, HALF], F32R) for i in range(2)]
        self.pt_lo = [sb(f"pt_lo{i}", [P, NT, HALF], F32R) for i in range(2)]
        self.z = [sb(f"z{i}", [P, HALF]) for i in range(2)]
        self.ps_score = [ps(f"ps_score{i}", [P, N]) for i in range(2)]
        self.ps_turn = [ps(f"ps_turn{i}", [P, HALF]) for i in range(2)]
        self.ps_z = ps("ps_z", [P, HALF])
        self.ps_post = ps("ps_post", [P, HALF])
        self.xhh = sb("xhh", [P, N], F32R)
        self.xll = sb("xll", [P, N], F32R)
        self.xhl = sb("xhl", [P, N], F32R)
        self.xm = sb("xm", [P, NT, P], F32R)
        self.scored = sem("scored")
        self.masked = sem("masked")
        self.exped = sem("exped")
        self.dve_passed, self.pool_passed = sem("dve_passed"), sem("pool_passed")
        self.inverted = sem("inverted")
        self.normed = sem("normed")
        self.turned = sem("turned")
        self.high = sem("high")
        self.low = sem("low")
        self.summed = sem("summed")
        self.copied = sem("copied")
        self.posted = sem("posted")

    def dve_credits(self, dve):
        dve.sem_inc(self.masked, 2)
        dve.sem_inc(self.low, 2)
        dve.sem_inc(self.copied, 1)

    def pe_credits(self, pe):
        pe.sem_inc(self.turned, 8)
        pe.sem_inc(self.summed, 2)
        pe.sem_inc(self.posted, 2)

    def pe_score_free(self, pe, u, i):
        pe.wait_ge(self.masked, 8 * u + i + 1)

    def dve_mask_add(self, dve, u, i, mask):
        dve.wait_ge(self.turned, 16 * u + 2 * i + 2)
        dve.wait_ge(self.scored, 8 * u + i + 1)
        dve.sem_inc(self.dve_passed, 1)
        self.nc.vector.tensor_tensor_reduce(
            out=self.prob[i % 4][:], in0=self.ps_score[i % 2][:], in1=mask, scale=-1.0, scalar=3.0e38,
            op0=ALU.add, op1=ALU.min, accum_out=self.negmax[:, i % 4:i % 4 + 1]).then_inc(self.masked, 1)

    def act_exp(self, act, u, i):
        act.wait_ge(self.masked, 8 * u + i + 3)
        c = slice(i % 4, i % 4 + 1)
        self.nc.scalar.activation(self.prob[i % 4][:], self.prob[i % 4][:], ACT.Exp, bias=self.negmax[:, c],
                                  scale=-1.0, accum_out=self.rowsum[:, c]).then_inc(self.exped, 1)

    def dve_invert(self, dve, u, i):
        dve.wait_ge(self.exped, 8 * u + i + 1)
        c = slice(i % 4, i % 4 + 1)
        self.nc.vector.reciprocal(self.rowinv[:, c], self.rowsum[:, c]).then_inc(self.inverted, 1)

    def pool_norm(self, pool, u, i):
        pool.wait_ge(self.inverted, 8 * u + i + 1)
        pool.sem_inc(self.pool_passed, 1)
        self.nc.gpsimd.tensor_scalar(self.prob[i % 4][:], self.prob[i % 4][:], self.rowinv[:, i % 4:i % 4 + 1],
                                     1.0, ALU.mult, ALU.mult).then_inc(self.normed, 1)

    def pe_turn(self, pe, u, i, ident):
        pe.wait_ge(self.normed, 8 * u + i + 1)
        for j in range(2):
            pe.wait_ge(self.low, 16 * u + 2 * i + j + 1)
            for k in range(TPH):
                m = TPH * j + k
                last = self.nc.tensor.transpose(self.ps_turn[j][:, k * P:(k + 1) * P],
                                                self.prob[i % 4][:, m * P:(m + 1) * P], ident[:])
            last.then_inc(self.turned, 1)

    def part(self, parts, i, j):
        return parts[i // TPH][:, TPH * j:TPH * (j + 1), (i % TPH) * P:(i % TPH + 1) * P]

    def act_high(self, act, u, i, j):
        act.wait_ge(self.turned, 16 * u + 2 * i + j + 9)
        if i % TPH == 0 and j == 0:
            act.wait_ge(self.summed, 2 * u + i // TPH + 1)
        self.nc.scalar.activation(self.part(self.pt_hi, i, j),
                                  self.ps_turn[j][:].rearrange("p (k n) -> p k n", n=P),
                                  ACT.Copy).then_inc(self.high, 1)

    def dve_low(self, dve, u, i, j):
        dve.wait_ge(self.high, 16 * u + 2 * i + j + 1)
        if i % TPH == 0 and j == 0:
            dve.wait_ge(self.summed, 2 * u + i // TPH + 1)
        self.nc.vector.tensor_tensor(self.part(self.pt_lo, i, j),
                                     self.ps_turn[j][:].rearrange("p (k n) -> p k n", n=P),
                                     self.part(self.pt_hi, i, j).bitcast(F32), ALU.subtract).then_inc(self.low, 1)

    def pe_sum(self, pe, u, q, quarter, values):
        if quarter == 0:
            pe.wait_ge(self.low, 16 * u + 8 * (q + 1) + 2)
            pe.wait_ge(self.copied, 2 * u + q + 1)
        for k in range(4 * quarter, 4 * quarter + 4):
            part, m = (self.pt_hi, self.pt_lo)[k // NT], k % NT
            last = self.nc.tensor.matmul(self.ps_z[:], values[:, m, :], part[q][:, m, :],
                                         start=(k == 0), stop=(k == 2 * NT - 1))
        if quarter == 3:
            last.then_inc(self.summed, 1)

    def act_copy(self, act, u, q):
        act.wait_ge(self.summed, 2 * u + q + 3)
        act.wait_ge(self.posted, 2 * u + q + 1)
        self.nc.scalar.activation(self.z[q][:], self.ps_z[:], ACT.Copy).then_inc(self.copied, 1)

    def pool_pair(self, pool, b, hx):
        rows = hx[:, b * NT:(b + 1) * NT, :] if isinstance(b, int) else hx[:, bass.ds(b * NT, NT), :]
        self.nc.gpsimd.tensor_copy(
            self.pair[:], rows.unsqueeze(2).broadcast_to([P, NT, 2, F]))\
            .then_inc(self.paired, 1)


def layer1(nc, ctx, B, x, hx, mask, ident, fold, Wh, bh, W_out, b_out):
    sb = lambda n, s, d=F32: ctx.enter_context(nc.sbuf_tensor(n, s, d))
    sem = lambda n: nc.alloc_semaphore(n)
    UNITS = HEADS + 1
    ww = sb("ww", [P, HEADS, HID])
    g = sb("g", [P, HEADS, P], F32R)
    bcol = sb("bcol", [P, HEADS])
    wo = sb("wo", [P, HEADS, 2, F])
    bout = sb("bout", [P, F])
    at = Attention(nc, ctx, "l1")
    loaded, wt_ready, wt_done, g_ready, g_hi, g_lo = (
        sem(f"l1_{n}") for n in ("loaded", "wt_ready", "wt_done", "g_ready", "g_hi", "g_lo"))
    LOADS = 6 * 16
    wt = at.prob[0]

    with ExitStack() as norm:
        def loads(sp):
            sp.dma_start(ww[0:F], Wh.rearrange("h c d -> c h d")).then_inc(loaded, 16)
            sp.dma_start(ww[F:P], Wh.rearrange("h c d -> c h d")).then_inc(loaded, 16)
            with nc.allow_non_contiguous_dma(reason="a small transposed load"):
                sp.dma_start(bcol[:], bh.rearrange("h d -> d h")).then_inc(loaded, 16)
            for c in range(2):
                sp.dma_start(wo[:, :, c, :], W_out.rearrange("(h d) f -> d h f", d=HID)).then_inc(loaded, 16)
            sp.dma_start(bout[:], b_out.rearrange("(o f) -> o f", o=1).broadcast_to([P, F])).then_inc(loaded, 16)

        layer_norm_relu(nc, norm, B, x, hx, "ln1", loads)

    with nc.Block() as block:
        @block.tensor
        def _(pe):
            pe.wait_ge(loaded, LOADS)
            for h in range(HEADS):
                last = nc.tensor.transpose(at.ps_score[0][:, h * P:(h + 1) * P], ww[:, h, :], ident[:])
            last.then_inc(wt_ready, 1)
            pe.wait_ge(wt_done, 1)
            for h in range(HEADS):
                w = wt[:, h * P:(h + 1) * P]
                last = nc.tensor.matmul(at.ps_score[1][:, h * P:(h + 1) * P], w, w, start=True, stop=True)
            last.then_inc(g_ready, 1)

        @block.vector
        def _(dve):
            dve.wait_ge(wt_ready, 1)
            nc.vector.tensor_copy(wt[:], at.ps_score[0][:]).then_inc(wt_done, 1)
            dve.wait_ge(g_hi, 1)
            nc.vector.tensor_tensor(g[F:P], at.ps_score[1][F:P, :].rearrange("p (h c) -> p h c", c=P),
                                    g[F:P].bitcast(F32), ALU.subtract).then_inc(g_lo, 1)

        @block.scalar
        def _(act):
            act.wait_ge(g_ready, 1)
            nc.scalar.activation(g[:], at.ps_score[1][:].rearrange("p (h c) -> p h c", c=P),
                                 ACT.Copy).then_inc(g_hi, 1)

    ohh, oll, ohl = (sb(n, [P, N], F32R) for n in ("ohh", "oll", "ohl"))
    om = sb("om", [P, NT, P], F32R)
    y = [sb(f"y{i}", [P, N], F32R) for i in range(2)]
    gs = [sb(f"gs{i}", [P, P], F32R) for i in range(2)]
    ws = [sb(f"ws{i}", [P, HID]) for i in range(2)]
    wos = [sb(f"wos{i}", [P, P]) for i in range(2)]
    bs = [sb(f"bs{i}", [P, 1]) for i in range(2)]
    biased = [sb(f"biased{i}", [P, HALF]) for i in range(2)]
    cat = [sb(f"cat{i}", [P, HALF]) for i in range(2)]
    hout = sb("hout", [P, N])
    last_act = sb("last_act", [P, TPH, F])
    xt_ready, hh_ready, ll_ready, hl_ready, xm_turned, xm_ready = (
        sem(f"l1_{n}") for n in ("xt_ready", "hh_ready", "ll_ready", "hl_ready", "xm_turned", "xm_ready"))
    ohh_ready, oll_ready, ohl_ready, om_turned, om_ready = (
        sem(f"l1_{n}") for n in ("ohh_ready", "oll_ready", "ohl_ready", "om_turned", "om_ready"))
    g_staged, w_staged = sem("l1_g_staged"), sem("l1_w_staged")
    projected = sem("l1_projected")
    y_hi, y_lo = sem("l1_y_hi"), sem("l1_y_lo")
    cat_biased = sem("l1_cat_biased")
    cat_done = sem("l1_cat_done")
    mixed = sem("l1_mixed")
    hout_done = sem("l1_hout_done")
    zeroed = sem("l1_zeroed")
    out_sum = sem("l1_out_sum")
    halves = [slice(q * HALF, (q + 1) * HALF) for q in range(2)]

    OUTPUT, HEAD = "output layer", "head"
    not_first = lambda h: not (isinstance(h, int) and h == 1)

    def later_heads(loop, unit):
        unit(1, 1, HEAD, True, True)
        with loop(2, HEADS - 2, 2) as h:
            unit(h, 0, HEAD, True, True)
            unit(h + 1, 1, HEAD, True, True)
        unit(HEADS - 2, 0, HEAD, True, True)
        unit(HEADS - 1, 1, HEAD, True, False)
        unit(HEADS, 0, HEAD, False, False)

    def batches(loop, first_operands, unit_of, output_of, finish):
        first_operands(0)
        unit_of(0)(0, 0, None, True, True)
        if B > 1:
            with loop(0, B - 1) as b:
                later_heads(loop, unit_of(b))
                output_of(b, True)
                unit_of(b + 1)(0, 0, OUTPUT, True, True)
        later_heads(loop, unit_of(B - 1))
        output_of(B - 1, False)
        finish(B - 1)

    with nc.Block() as block:
        @block.tensor
        def _(pe):
            at.pe_credits(pe)
            pe.sem_inc(mixed, 2)

            def x_turn(b, q):
                if q == 0:
                    pe.wait_ge(at.paired, b + 1)
                else:
                    pe.wait_ge(ll_ready, 2 * b + 1)
                for k in range(TPH):
                    last = nc.tensor.transpose(at.ps_post[:, k * P:(k + 1) * P],
                                               at.pair[:, TPH * q + k].rearrange("p c f -> p (c f)"), ident[:])
                last.then_inc(xt_ready, 1)

            def xm_turn(b, q):
                pe.wait_ge(hl_ready, 4 * b + 4)
                if q == 1:
                    pe.wait_ge(xm_ready, 2 * b + 1)
                for k in range(TPH):
                    m = TPH * q + k
                    last = nc.tensor.transpose(at.ps_post[:, k * P:(k + 1) * P],
                                               at.xhl[:, m * P:(m + 1) * P].bitcast(F32), ident[:])
                last.then_inc(xm_turned, 1)

            def project(b, h, par, q):
                if q == 0:
                    pe.wait_ge(g_staged, HEADS * b + h + 1)
                else:
                    pe.wait_ge(y_lo, 2 * HEADS * b + 2 * h + 1)
                nc.tensor.matmul(at.ps_post[:], gs[par][:], at.xhh[:, halves[q]], start=True, stop=False)
                nc.tensor.matmul(at.ps_post[:], gs[par][:], at.xll[:, halves[q]], start=False, stop=True)\
                    .then_inc(projected, 1)

            def score(u, i, rows, columns):
                at.pe_score_free(pe, u, i)
                for c in halves:
                    for part in columns:
                        last = nc.tensor.matmul(at.ps_score[i % 2][:, c], rows[:, i * P:(i + 1) * P], part[:, c],
                                                start=(part is columns[0]), stop=(part is columns[-1]))
                last.then_inc(at.scored, 1)

            def fold_out(b, q):
                pe.wait_ge(at.copied, 2 * (b * UNITS + HEADS) + q + 2)
                for i in range(TPH):
                    last = nc.tensor.matmul(at.ps_post[:, i * F:(i + 1) * F], at.z[q][:, i * P:(i + 1) * P],
                                            fold[:], start=True, stop=True)
                last.then_inc(at.posted, 1)

            def unit_of(b):
                u0, n0 = b * UNITS, b * (2 * HEADS)

                def post(h, par, q):
                    if q == 0:
                        pe.wait_ge(w_staged, 3 * HEADS * b + 3 * h + 3)
                    pe.wait_ge(at.copied, 2 * u0 + 2 * h + q + 2)
                    nc.tensor.matmul(at.ps_post[:], ws[par][:], at.z[q][:], start=True, stop=True)\
                        .then_inc(at.posted, 1)

                def mix(h, par, q):
                    pe.wait_ge(cat_done, n0 + 2 * h + q + 1)
                    nc.tensor.matmul(at.ps_post[:], wos[par][:], cat[q][:], start=True, stop=True)\
                        .then_inc(mixed, 1)

                def unit(h, par, prev, current, following):
                    u = u0 + h
                    values = om if prev == OUTPUT else at.xm
                    if current:
                        pe.wait_ge(y_lo, n0 + 2 * h + 2)
                    if current and isinstance(h, int) and h == 0:
                        pe.wait_ge(xm_ready, 2 * b + 2)
                    for i in range(NT):
                        if current:
                            score(u, i, y[par], (at.xhh, at.xll))
                        if i == 1 and prev == HEAD and not_first(h):
                            mix(h - 2, par, 1)
                        if i == 4 and prev == HEAD:
                            mix(h - 1, 1 - par, 0)
                        if i == 5 and following:
                            if prev == HEAD:
                                pe.wait_ge(hout_done, n0 + 2 * h - 1)
                            elif prev == OUTPUT:
                                pe.wait_ge(out_sum, 6 * b + 1)
                            project(b, h + 1, 1 - par, 0)
                        if i == 6 and following:
                            project(b, h + 1, 1 - par, 1)
                        if i >= 2 and current:
                            at.pe_turn(pe, u, i - 2, ident)
                        elif i < 2 and prev:
                            at.pe_turn(pe, u - 1, i + 6, ident)
                        if prev == HEAD and i == 2:
                            if not_first(h):
                                pe.wait_ge(hout_done, n0 + 2 * h - 2)
                            else:
                                pe.wait_ge(out_sum, 6 * b + 4)
                            post(h - 1, 1 - par, 0)
                        if prev == OUTPUT and i == 2:
                            fold_out(b - 1, 0)
                        if prev and i == 7:
                            if following:
                                pe.wait_ge(y_lo, n0 + 2 * h + 4)
                            else:
                                pe.wait_ge(hout_done, n0 + 2 * h - 1)
                            if prev == HEAD:
                                post(h - 1, 1 - par, 1)
                            else:
                                fold_out(b - 1, 1)
                        if i >= 6 and current:
                            at.pe_sum(pe, u, 0, i - 6, at.xm)
                        elif i < 2 and prev:
                            at.pe_sum(pe, u - 1, 0, i + 2, values)
                        elif 2 <= i < 6 and prev:
                            at.pe_sum(pe, u - 1, 1, i - 2, values)
                    if not current:
                        mix(h - 1, 1 - par, 1)

                return unit

            def output_of(b, following):
                u = b * UNITS + HEADS

                def om_turn(q):
                    if q == 0:
                        pe.wait_ge(at.copied, 2 * u + 1)
                    else:
                        pe.wait_ge(om_ready, 2 * b + 1)
                    for k in range(TPH):
                        m = TPH * q + k
                        last = nc.tensor.transpose(at.ps_z[:, k * P:(k + 1) * P],
                                                   ohl[:, m * P:(m + 1) * P].bitcast(F32), ident[:])
                    last.then_inc(om_turned, 1)

                pe.wait_ge(ohl_ready, 4 * b + 4)
                pe.wait_ge(oll_ready, 2 * b + 2)
                for i in range(NT):
                    score(u, i, ohl, (ohh, oll))
                    if i >= 2:
                        at.pe_turn(pe, u, i - 2, ident)
                    if i == 6:
                        pe.wait_ge(om_ready, 2 * b + 2)
                    if i >= 6:
                        at.pe_sum(pe, u, 0, i - 6, om)
                    if i < 2:
                        om_turn(i)
                    if following and i < 2:
                        if i == 0:
                            pe.wait_ge(hout_done, 2 * HEADS * (b + 1))
                        x_turn(b + 1, i)
                    if following and i in (3, 4):
                        xm_turn(b + 1, i - 3)
                    if following and i in (5, 6):
                        if i == 5:
                            pe.wait_ge(xm_ready, 2 * b + 4)
                        project(b + 1, 0, 0, i - 5)

            def first_operands(b):
                for q in range(2):
                    x_turn(b, q)
                pe.wait_ge(ll_ready, 2 * b + 2)
                for q in range(2):
                    xm_turn(b, q)
                pe.wait_ge(xm_ready, 2 * b + 2)
                for q in range(2):
                    project(b, 0, 0, q)

            def finish(b):
                u = b * UNITS + HEADS
                for i in (6, 7):
                    at.pe_turn(pe, u, i, ident)
                for q in range(2):
                    for quarter in range(4):
                        if q == 1 or quarter >= 2:
                            at.pe_sum(pe, u, q, quarter, om)
                pe.wait_ge(hout_done, 2 * HEADS * (b + 1))
                fold_out(b, 0)
                pe.wait_ge(out_sum, 6 * b + 7)
                fold_out(b, 1)

            batches(pe.Fori, first_operands, unit_of, output_of, finish)

        @block.vector
        def _(dve):
            at.dve_credits(dve)
            dve.sem_inc(out_sum, 6)

            def tile(u, i, prev, current, between=lambda: None):
                if i >= 1 and current:
                    at.dve_invert(dve, u, i - 1)
                elif i < 1 and prev:
                    at.dve_invert(dve, u - 1, NT - 1)
                if current:
                    at.dve_mask_add(dve, u, i, mask[:, i, :])
                between()
                for j in range(2):
                    if i >= 2 and current:
                        at.dve_low(dve, u, i - 2, j)
                    elif i < 2 and prev:
                        at.dve_low(dve, u - 1, i + 6, j)

            def low_x(b, q):
                dve.wait_ge(hh_ready, 2 * b + q + 1)
                nc.vector.tensor_tensor(at.xll[:, halves[q]], at.ps_post[:], at.xhh[:, halves[q]].bitcast(F32),
                                        ALU.subtract).then_inc(ll_ready, 1)

            def take_xm(b, q):
                dve.wait_ge(xm_turned, 2 * b + q + 1)
                nc.vector.tensor_copy(at.xm[:, TPH * q:TPH * (q + 1), :].rearrange("p k c -> p (k c)"), at.ps_post[:])\
                    .then_inc(xm_ready, 1)

            def split_y(b, h, par, q):
                dve.wait_ge(y_hi, 2 * HEADS * b + 2 * h + q + 1)
                c = halves[q]
                nc.vector.tensor_tensor(y[par][F:P, c], at.ps_post[F:P, :], y[par][F:P, c].bitcast(F32),
                                        ALU.subtract).then_inc(y_lo, 1)

            def low_out(b, q):
                dve.wait_ge(ohh_ready, 2 * b + q + 1)
                for to, rows, done in ((ohl, slice(F, P), ohl_ready), (oll, slice(0, P), oll_ready)):
                    nc.vector.tensor_tensor(to[rows, halves[q]], hout[rows, halves[q]],
                                            ohh[rows, halves[q]].bitcast(F32), ALU.subtract).then_inc(done, 1)

            def add_out(b, q):
                n = 6 * b + 3 * q + 6
                dve.wait_ge(at.posted, 2 * (b * UNITS + HEADS) + q + 3)
                dve.wait_ge(out_sum, n)
                nc.vector.tensor_tensor(last_act[:], at.ps_post[:, 0:TPH * F].rearrange("p (i f) -> p i f", f=F),
                                        bout[:].unsqueeze(1).broadcast_to([P, TPH, F]), ALU.add).then_inc(out_sum, 1)
                dve.wait_ge(out_sum, n + 1)
                nc.vector.scalar_tensor_tensor(out=last_act[:], in0=last_act[:], scalar=0.01, in1=last_act[:],
                                               op0=ALU.mult, op1=ALU.max).then_inc(out_sum, 1)
                dve.wait_ge(out_sum, n + 2)
                rows = x[:, bass.ds(b * NT + q * TPH, TPH), :]
                nc.vector.tensor_tensor(rows, rows, last_act[:], ALU.add).then_inc(out_sum, 1)

            def unit_of(b):
                u0, n0 = b * UNITS, b * (2 * HEADS)

                def leaky(h, q):
                    dve.wait_ge(cat_biased, n0 + 2 * h + q + 1)
                    dve.wait_ge(mixed, n0 + 2 * h + q + 1)
                    nc.vector.scalar_tensor_tensor(out=cat[q][:], in0=biased[q][:], scalar=0.01, in1=biased[q][:],
                                                   op0=ALU.mult, op1=ALU.max).then_inc(cat_done, 1)

                def accumulate(h, q):
                    dve.wait_ge(mixed, n0 + 2 * h + q + 3)
                    c = halves[q]
                    nc.vector.tensor_tensor(hout[:, c], at.ps_post[:], hout[:, c], ALU.add).then_inc(hout_done, 1)

                def unit(h, par, prev, current, following):
                    u = u0 + h

                    def between(i):
                        if i == 0 and prev == HEAD and not_first(h):
                            leaky(h - 2, 1)
                        if i == 0 and prev == HEAD and not not_first(h):
                            dve.wait_ge(zeroed, b + 1)
                        if i == 1 and prev == HEAD and not_first(h):
                            accumulate(h - 2, 1)
                        if i == 3 and prev == HEAD:
                            leaky(h - 1, 0)
                        if i == 3 and prev == OUTPUT:
                            add_out(b - 1, 0)
                        if i == 4 and prev == HEAD:
                            accumulate(h - 1, 0)
                        if i in (5, 6) and following:
                            split_y(b, h + 1, 1 - par, i - 5)
                        if i == 6 and not current:
                            low_out(b, 0)

                    for i in range(NT):
                        tile(u, i, prev, current, lambda: between(i))
                    if prev == OUTPUT:
                        add_out(b - 1, 1)
                    if not current:
                        leaky(h - 1, 1)
                        accumulate(h - 1, 1)

                return unit

            def output_of(b, following):
                u = b * UNITS + HEADS
                low_out(b, 1)

                def between(i):
                    if i in (1, 2):
                        low_x(b + 1, i - 1)
                    if i in (4, 5):
                        take_xm(b + 1, i - 4)
                    if i in (6, 7):
                        split_y(b + 1, 0, 0, i - 6)

                for i in range(NT):
                    tile(u, i, None, True, lambda: following and between(i))

            def first_operands(b):
                for q in range(2):
                    low_x(b, q)
                for q in range(2):
                    take_xm(b, q)
                for q in range(2):
                    split_y(b, 0, 0, q)

            def finish(b):
                for i in range(2):
                    tile((b + 1) * UNITS, i, OUTPUT, False)
                for q in range(2):
                    add_out(b, q)

            batches(dve.Fori, first_operands, unit_of, output_of, finish)

        @block.scalar
        def _(act):
            copy = lambda out, src: nc.scalar.activation(out, src, ACT.Copy)

            def tile(u, i, prev, current):
                for j in range(2):
                    if i >= 2 and current:
                        at.act_high(act, u, i - 2, j)
                    elif i < 2 and prev:
                        at.act_high(act, u - 1, i + 6, j)
                if current:
                    at.act_exp(act, u, i)

            def high_x(b, q):
                act.wait_ge(xt_ready, 2 * b + q + 1)
                copy(at.xhh[:, halves[q]], at.ps_post[:]).then_inc(hh_ready, 1)

            def stack_x(b, q):
                act.wait_ge(ll_ready, 2 * b + q + 1)
                for rows, part in ((slice(0, F), at.xhh), (slice(F, P), at.xll)):
                    copy(at.xhl[rows, halves[q]], part[rows, halves[q]].bitcast(F32)).then_inc(hl_ready, 1)

            def high_out(b, q):
                act.wait_ge(hout_done, 2 * HEADS * (b + 1) - 1 + q)
                copy(ohh[:, halves[q]], hout[:, halves[q]]).then_inc(ohh_ready, 1)
                copy(ohl[0:F, halves[q]], hout[0:F, halves[q]]).then_inc(ohl_ready, 1)

            def high_y(b, h, par, q):
                act.wait_ge(projected, 2 * HEADS * b + 2 * h + q + 1)
                copy(y[par][:, halves[q]], at.ps_post[:]).then_inc(y_hi, 1)

            def unit_of(b):
                u0 = b * UNITS

                def bias(h, par, q):
                    act.wait_ge(at.posted, 2 * u0 + 2 * h + q + 3)
                    nc.scalar.activation(biased[q][:], at.ps_post[:], ACT.Identity, bias=bs[par][:, 0:1])\
                        .then_inc(cat_biased, 1)

                def unit(h, par, prev, current, following):
                    u = u0 + h
                    for i in range(NT):
                        if i in (5, 6) and following:
                            high_y(b, h + 1, 1 - par, i - 5)
                        if i in (2, 6) and prev:
                            at.act_copy(act, u - 1, (i - 2) // 4)
                        if i == 5 and not current:
                            high_out(b, 0)
                        tile(u, i, prev, current)
                        if i in (2, 7) and prev == HEAD:
                            bias(h - 1, 1 - par, (i - 2) // 5)

                return unit

            def output_of(b, following):
                high_out(b, 1)
                for i in range(NT):
                    if i in (1, 2):
                        act.wait_ge(om_turned, 2 * b + i)
                        copy(om[:, TPH * (i - 1):TPH * i, :].rearrange("p k c -> p (k c)"), at.ps_z[:])\
                            .then_inc(om_ready, 1)
                    if following and i in (1, 2):
                        high_x(b + 1, i - 1)
                    if following and i in (6, 7):
                        high_y(b + 1, 0, 0, i - 6)
                    tile(b * UNITS + HEADS, i, None, True)
                    if following and i in (1, 2):
                        stack_x(b + 1, i - 1)

            def first_operands(b):
                for q in range(2):
                    high_x(b, q)
                for q in range(2):
                    stack_x(b, q)
                for q in range(2):
                    high_y(b, 0, 0, q)

            def finish(b):
                u = b * UNITS + HEADS
                for i in range(2):
                    tile(u + 1, i, OUTPUT, False)
                for q in range(2):
                    at.act_copy(act, u, q)

            batches(act.Fori, first_operands, unit_of, output_of, finish)

        @block.gpsimd
        def _(pool):
            def stage_g(h, par):
                nc.gpsimd.tensor_copy(gs[par][:], g[:, bass.ds(h, 1), :].bitcast(F32).rearrange("p o c -> p (o c)"))\
                    .then_inc(g_staged, 1)

            def stage_w(h, par):
                for out, src in ((ws[par][:], ww[:, bass.ds(h, 1), :].rearrange("p o c -> p (o c)")),
                                 (wos[par][:], wo[:, bass.ds(h, 1)].rearrange("p o c f -> p (o c f)")),
                                 (bs[par][:], bcol[:, bass.ds(h, 1)])):
                    nc.gpsimd.tensor_copy(out, src).then_inc(w_staged, 1)

            def unit_of(b):
                u0, n0 = b * UNITS, b * (2 * HEADS)

                def unit(h, par, prev, current, following):
                    u = u0 + h
                    for i in range(NT):
                        if i == 0 and following:
                            pool.wait_ge(projected, n0 + 2 * h + 2)
                            pool.sem_inc(at.pool_passed, 1)
                            stage_g(h + 1, 1 - par)
                        if current:
                            at.pool_norm(pool, u, i)
                        if i == 3 and current:
                            if prev == HEAD and not_first(h):
                                pool.wait_ge(hout_done, n0 + 2 * h - 2)
                                pool.sem_inc(at.pool_passed, 1)
                            stage_w(h, par)
                    if not current and not (isinstance(b, int) and b == B - 1):
                        pool.wait_ge(xt_ready, 2 * b + 2)
                        pool.sem_inc(at.pool_passed, 1)
                        at.pool_pair(pool, b + 1, hx)

                return unit

            def output_of(b, following):
                for i in range(NT):
                    at.pool_norm(pool, b * UNITS + HEADS, i)
                    if following and i == 0:
                        stage_g(0, 0)
                if following:
                    pool.wait_ge(oll_ready, 2 * b + 2)
                    pool.wait_ge(ohl_ready, 4 * b + 4)
                    pool.sem_inc(at.pool_passed, 1)
                    nc.gpsimd.memset(hout[:], 0.0).then_inc(zeroed, 1)

            def first_operands(b):
                at.pool_pair(pool, b, hx)
                nc.gpsimd.memset(hout[:], 0.0).then_inc(zeroed, 1)
                stage_g(0, 0)

            batches(pool.Fori, first_operands, unit_of, output_of, lambda b: None)


def edge_layer(nc, ctx, B, x, hx, mask, adj, ident, name, W, a, bias):
    sb = lambda n, s, d=F32: ctx.enter_context(nc.sbuf_tensor(f"{name}_{n}", s, d))
    ps = lambda n, s: ctx.enter_context(nc.psum_tensor(f"{name}_{n}", s, F32))
    sem = lambda n: nc.alloc_semaphore(f"{name}_{n}")
    weighted = bias is not None
    SLOPE = 0.2
    pairs = sb("pairs", [P, NT, N]) if weighted else mask
    given = sb("given", [P, P])
    other = sb("other", [P, P])
    acol = sb("acol", [F, 2])
    arep = sb("arep", [F, 2, P])
    vecs = sb("vecs", [P, 2, P], F32R)
    brow = sb("brow", [P, F])
    ps_x, ps_d = ps("ps_x", [P, N]), ps("ps_d", [P, N])
    ps_turn = [ps(f"ps_turn{i}", [P, HALF]) for i in range(2)]
    ps_z, ps_post = ps("ps_z", [P, HALF]), ps("ps_post", [P, HALF])
    loaded, spread, w_turned, copied_w, mixed, split_hi, split_lo = (
        sem(n) for n in ("loaded", "spread", "w_turned", "w_copied", "mixed", "split_hi", "split_lo"))
    LOADS = 5 if weighted else 4
    adj_in, set_ones = sem("adj_in"), sem("set_ones")
    a_flat = a.rearrange("(c f) o -> f (c o)", f=F) if weighted else a.rearrange("(c f) -> f c", f=F)

    with ExitStack() as norm:
        def loads(sp):
            for c in range(2):
                to = given[c * F:(c + 1) * F, 0:F] if weighted else given[0:F, c * F:(c + 1) * F]
                sp.dma_start(to, W).then_inc(loaded, 16)
            with nc.allow_non_contiguous_dma(reason="128 numbers"):
                for c in range(2):
                    sp.dma_start(acol[:, c:c + 1], a_flat[:, c:c + 1]).then_inc(loaded, 16)
            if weighted:
                sp.dma_start(brow[:], bias.rearrange("(o f) -> o f", o=1).broadcast_to([P, F])).then_inc(loaded, 16)
                sp.dma_start(pairs[:], adj.rearrange("(k p) m -> p k m", p=P)).then_inc(adj_in, 16)

        layer_norm_relu(nc, norm, B, x, hx, f"{name}_ln", loads)

    with nc.Block() as block:
        @block.tensor
        def _(pe):
            pe.wait_ge(loaded, 16 * LOADS)
            if weighted:
                nc.tensor.transpose(ps_post[0:F, 0:P], given[:, 0:F], ident[:]).then_inc(w_turned, 1)
            else:
                nc.tensor.transpose(ps_post[:, 0:F], given[0:F, :], ident[0:F, 0:F]).then_inc(w_turned, 1)
            pe.wait_ge(copied_w, 1)
            pe.wait_ge(spread, 1)
            lhs = other[0:F, :] if weighted else given[0:F, :]
            nc.tensor.matmul(ps_z[:, 0:2 * P], lhs, arep[:].rearrange("p c n -> p (c n)"),
                             start=True, stop=True).then_inc(mixed, 1)

        @block.vector
        def _(dve):
            dve.wait_ge(loaded, 16 * LOADS)
            nc.vector.tensor_copy(arep[:], acol[:].unsqueeze(2).broadcast_to([F, 2, P])).then_inc(spread, 1)
            dve.wait_ge(w_turned, 1)
            if weighted:
                nc.vector.tensor_copy(other[0:F, :], ps_post[0:F, 0:P]).then_inc(copied_w, 1)
            else:
                nc.vector.tensor_copy(other[:, 0:F], ps_post[:, 0:F]).then_inc(copied_w, 1)
            dve.wait_ge(split_hi, 1)
            nc.vector.tensor_tensor(vecs[F:P], ps_z[F:P, 0:2 * P].rearrange("p (c n) -> p c n", n=P),
                                    vecs[F:P].bitcast(F32), ALU.subtract).then_inc(split_lo, 1)

        @block.scalar
        def _(act):
            act.wait_ge(mixed, 1)
            nc.scalar.activation(vecs[:], ps_z[:, 0:2 * P].rearrange("p (c n) -> p c n", n=P),
                                 ACT.Copy).then_inc(split_hi, 1)

    w_io = given[0:F, 0:F] if weighted else other[0:F, 0:F]
    pair = sb("pair", [P, NT, 2, F])
    xhh, xll = sb("xhh", [P, N], F32R), sb("xll", [P, N], F32R)
    xm = [sb(f"xm{i}", [P, NT, F]) for i in range(2)]
    d1, d02 = ([sb(f"{n}{i}", [P, N]) for i in range(2)] for n in ("d1_", "d02_"))
    s1, s02 = ([sb(f"{n}{i}", [P, NT, 2]) for i in range(2)] for n in ("s1_", "s02_"))
    prob = [sb(f"prob{i}", [P, N]) for i in range(4)]
    peak, negmax, rowsum, rowinv = (sb(n, [P, 4]) for n in ("peak", "negmax", "rowsum", "rowinv"))
    pt = [sb(f"pt{i}", [P, NT, HALF]) for i in range(2)]
    z = [sb(f"z{i}", [F, HALF]) for i in range(2)]
    e, new = sb("e", [P, TPH, F]), sb("new", [P, TPH, F])

    paired, xt_ready, hh_ready, ll_ready, projected, termed, xm_ready = (
        sem(n) for n in ("paired", "xt_ready", "hh_ready", "ll_ready", "projected", "termed", "xm_ready"))
    sloped = sem("sloped")
    leaned, peaked, masked = sem("leaned"), sem("peaked"), sem("masked")
    exped, inverted, normed = sem("exped"), sem("inverted"), sem("normed")
    turned = sem("turned")
    untied = sem("untied")
    summed, copied, posted = sem("summed"), sem("copied"), sem("posted")
    exped_out, floored, out_read, added = (sem(n) for n in ("exped_out", "floored", "out_read", "added"))
    pe_passed, dve_passed, act_passed, pool_passed = (sem(f"{n}_passed") for n in ("pe", "dve", "act", "pool"))

    def wait_count(eng, semaphore, count):
        if not isinstance(count, int) or count > 0:
            eng.wait_ge(semaphore, count)

    def batches(loop, unit):
        unit(0, 0, False, True, True)
        unit(1, 1, True, True, True)
        if B > 4:
            with loop(2, B - 2, 2) as b:
                unit(b, 0, True, True, True)
                unit(b + 1, 1, True, True, True)
        unit(B - 2, 0, True, True, True)
        unit(B - 1, 1, True, True, False)
        unit(B, 0, True, False, False)

    with nc.Block() as block:
        @block.tensor
        def _(pe):
            def x_turn(b):
                wait_count(pe, termed, 3 * b)
                pe.wait_ge(paired, b + 1)
                for k in range(NT):
                    last = nc.tensor.transpose(ps_x[:, k * P:(k + 1) * P], pair[:, k].rearrange("p c f -> p (c f)"),
                                               ident[:])
                last.then_inc(xt_ready, 1)

            def terms(b):
                pe.wait_ge(ll_ready, b + 1)
                for q in range(2):
                    c = slice(q * HALF, (q + 1) * HALF)
                    nc.tensor.matmul(ps_d[:, c], vecs[:, 1, :], xhh[:, c], start=True, stop=False)
                    last = nc.tensor.matmul(ps_d[:, c], vecs[:, 1, :], xll[:, c], start=False, stop=True)
                last.then_inc(projected, 1)
                for i in range(NT):
                    for part in (xhh, xll):
                        last = nc.tensor.matmul(ps_x[:, 2 * i:2 * i + 2], part[:, i * P:(i + 1) * P],
                                                vecs[:, 0, 0:2], start=(part is xhh), stop=(part is xll))
                last.then_inc(projected, 1)

            def turn(u, i):
                pe.wait_ge(normed, NT * u + i + 1)
                for j in range(2):
                    wait_count(pe, untied, 2 * NT * u + 2 * i + j - 1)
                    for k in range(TPH):
                        m = TPH * j + k
                        last = nc.tensor.transpose(ps_turn[j][:, k * P:(k + 1) * P],
                                                   prob[i % 4][:, m * P:(m + 1) * P], ident[:])
                    last.then_inc(turned, 1)

            def quarter_sum(u, par, q, quarter):
                if quarter == 0:
                    pe.wait_ge(xm_ready, u + 1)
                    pe.wait_ge(untied, 2 * NT * u + NT * (q + 1))
                    wait_count(pe, copied, 2 * u + q)
                for m in range(2 * quarter, 2 * quarter + 2):
                    last = nc.tensor.matmul(ps_z[0:F, :], xm[par][:, m, :], pt[q][:, m, :],
                                            start=(m == 0), stop=(m == NT - 1))
                if quarter == 3:
                    last.then_inc(summed, 1)

            def post(u, q):
                pe.wait_ge(copied, 2 * u + q + 1)
                wait_count(pe, out_read, 2 * u + q)
                pe.sem_inc(pe_passed, 1)
                for i in range(TPH):
                    last = nc.tensor.matmul(ps_post[:, i * F:(i + 1) * F], z[q][:, i * P:(i + 1) * P], w_io,
                                            start=True, stop=True)
                last.then_inc(posted, 1)

            def unit(u, par, prev, current, following):
                for i in range(NT):
                    if i >= 2 and current:
                        turn(u, i - 2)
                    elif i < 2 and prev:
                        turn(u - 1, i + 6)
                    if i >= 6 and current:
                        quarter_sum(u, par, 0, i - 6)
                    elif i < 2 and prev:
                        quarter_sum(u - 1, 1 - par, 0, i + 2)
                    elif 2 <= i < 6 and prev:
                        quarter_sum(u - 1, 1 - par, 1, i - 2)
                    if i in (2, 6) and prev:
                        post(u - 1, (i - 2) // 4)
                    if i == 1 and following:
                        x_turn(u + 1)
                    if i == 5 and following:
                        terms(u + 1)

            x_turn(0)
            terms(0)
            batches(pe.Fori, unit)

        @block.vector
        def _(dve):
            def low_x(b):
                dve.wait_ge(hh_ready, b + 1)
                nc.vector.tensor_tensor(xll[:], ps_x[:], xhh[:].bitcast(F32), ALU.subtract).then_inc(ll_ready, 1)

            def lean(u, par, i):
                if weighted:
                    dve.wait_ge(sloped, NT * u + i + 1)
                else:
                    if i == 0:
                        dve.wait_ge(termed, 3 * u + 3)
                    wait_count(dve, turned, 2 * NT * u + 2 * i - 6)
                p = prob[i % 4][:]
                nc.vector.scalar_tensor_tensor(out=p, in0=d1[par][:], scalar=s1[par][:, i, 0:1],
                                               in1=p if weighted else d02[par][:],
                                               op0=ALU.add, op1=ALU.max).then_inc(leaned, 1)

            def edges(u, i):
                p, c = prob[i % 4][:], slice(i % 4, i % 4 + 1)
                dve.wait_ge(leaned, NT * u + i + 1)
                dve.sem_inc(dve_passed, 1)
                if weighted:
                    nc.vector.tensor_tensor_reduce(out=p, in0=p, in1=pairs[:, i, :], scale=1.0, scalar=-3.0e38,
                                                   op0=ALU.mult, op1=ALU.max, accum_out=peak[:, c]).then_inc(peaked, 1)
                else:
                    nc.vector.tensor_tensor_reduce(out=p, in0=p, in1=pairs[:, i, :], scale=-1.0, scalar=3.0e38,
                                                   op0=ALU.add, op1=ALU.min, accum_out=negmax[:, c]).then_inc(masked, 1)

            def negate(u, i):
                c = slice(i % 4, i % 4 + 1)
                dve.wait_ge(peaked, NT * u + i + 1)
                nc.vector.tensor_scalar(negmax[:, c], peak[:, c], -1.0, None, ALU.mult).then_inc(masked, 1)

            def invert(u, i):
                c = slice(i % 4, i % 4 + 1)
                dve.wait_ge(exped, NT * u + i + 1)
                nc.vector.reciprocal(rowinv[:, c], rowsum[:, c]).then_inc(inverted, 1)

            def output(u, q):
                v = ps_post[:, 0:TPH * F].rearrange("p (i f) -> p i f", f=F)
                if weighted:
                    dve.wait_ge(posted, 2 * u + q + 1)
                    wait_count(dve, added, 2 * u + q)
                    nc.vector.tensor_tensor(new[:], v, brow[:].unsqueeze(1).broadcast_to([P, TPH, F]),
                                            ALU.add).then_inc(out_read, 1)
                else:
                    dve.wait_ge(exped_out, 2 * u + q + 1)
                    nc.vector.tensor_scalar(e[:], e[:], 1.0, -1.0, ALU.min, ALU.add).then_inc(floored, 1)
                    dve.wait_ge(floored, 2 * u + q + 1)
                    nc.vector.scalar_tensor_tensor(out=new[:].rearrange("p i f -> p (i f)"),
                                                   in0=ps_post[:, 0:TPH * F], scalar=0.0,
                                                   in1=e[:].rearrange("p i f -> p (i f)"),
                                                   op0=ALU.max, op1=ALU.add).then_inc(out_read, 1)
                dve.wait_ge(out_read, 2 * u + q + 1)
                rows = x[:, bass.ds(u * NT + q * TPH, TPH), :]
                nc.vector.tensor_tensor(rows, rows, new[:], ALU.add).then_inc(added, 1)

            def unit(u, par, prev, current, following):
                for i in range(NT):
                    if current:
                        lean(u, par, i)
                    if i >= 1 and current:
                        invert(u, i - 1)
                    elif i == 0 and prev:
                        invert(u - 1, NT - 1)
                    if current:
                        edges(u, i)
                    if i == 3 and following:
                        low_x(u + 1)
                    if i in (3, 7) and prev:
                        output(u - 1, (i - 3) // 4)
                    if current and weighted:
                        negate(u, i)

            low_x(0)
            if weighted:
                dve.wait_ge(set_ones, 1)
            batches(dve.Fori, unit)

        @block.scalar
        def _(act):
            fn = nc.scalar.activation

            def pair_up(b):
                rows = hx[:, b * NT:(b + 1) * NT, :] if isinstance(b, int) else hx[:, bass.ds(b * NT, NT), :]
                wait_count(act, xt_ready, b)
                wait_count(act, xm_ready, b)
                act.sem_inc(act_passed, 1)
                fn(pair[:], rows.unsqueeze(2).broadcast_to([P, NT, 2, F]), ACT.Copy).then_inc(paired, 1)

            def high_x(b):
                act.wait_ge(xt_ready, b + 1)
                fn(xhh[:], ps_x[:], ACT.Copy).then_inc(hh_ready, 1)

            def take_terms(b, par):
                act.wait_ge(projected, 2 * b + 2)
                src = ps_x[:, 0:2 * NT].rearrange("p (i c) -> p i c", c=2)
                fn(d1[par][:], ps_d[:], ACT.Copy).then_inc(termed, 1)
                if not weighted:
                    fn(d02[par][:], ps_d[:], ACT.Copy, scale=SLOPE).then_inc(termed, 1)
                fn(s1[par][:], src, ACT.Copy, scale=1.0 if weighted else 1.0 - SLOPE).then_inc(termed, 1)
                if weighted:
                    fn(s02[par][:], src, ACT.Copy, scale=SLOPE).then_inc(termed, 1)

            def take_rows(b, par):
                act.wait_ge(paired, b + 1)
                wait_count(act, summed, 2 * b - 2)
                fn(xm[par][:], pair[:, :, 0, :], ACT.Copy).then_inc(xm_ready, 1)

            def exp(u, i):
                act.wait_ge(masked, NT * u + i + 1)
                c = slice(i % 4, i % 4 + 1)
                fn(prob[i % 4][:], prob[i % 4][:], ACT.Exp, bias=negmax[:, c], scale=1.0 if weighted else -1.0,
                   accum_out=rowsum[:, c]).then_inc(exped, 1)

            def untie(u, i, j):
                act.wait_ge(turned, 2 * NT * u + 2 * i + j + 1)
                if i % TPH == 0 and j == 0:
                    wait_count(act, summed, 2 * u + i // TPH - 1)
                fn(pt[i // TPH][:, TPH * j:TPH * (j + 1), (i % TPH) * P:(i % TPH + 1) * P],
                   ps_turn[j][:].rearrange("p (k n) -> p k n", n=P), ACT.Copy).then_inc(untied, 1)

            def copy_z(u, q):
                act.wait_ge(summed, 2 * u + q + 1)
                wait_count(act, posted, 2 * u + q - 1)
                fn(z[q][:], ps_z[0:F, :], ACT.Copy).then_inc(copied, 1)

            def exp_out(u, q):
                act.wait_ge(posted, 2 * u + q + 1)
                wait_count(act, out_read, 2 * u + q)
                fn(e[:], ps_post[:, 0:TPH * F].rearrange("p (i f) -> p i f", f=F), ACT.Exp).then_inc(exped_out, 1)

            def unit(u, par, prev, current, following):
                for i in range(NT):
                    if i in (2, 6) and prev:
                        copy_z(u - 1, (i - 2) // 4)
                    if i in (3, 7) and prev and not weighted:
                        exp_out(u - 1, (i - 3) // 4)
                    for j in range(2):
                        if i >= 2 and current:
                            untie(u, i - 2, j)
                        elif i < 2 and prev:
                            untie(u - 1, i + 6, j)
                    if current:
                        exp(u, i)
                    if i == 0 and following:
                        pair_up(u + 1)
                    if i == 2 and following:
                        high_x(u + 1)
                    if i == 6 and following:
                        take_terms(u + 1, 1 - par)
                    if i == 7 and following:
                        take_rows(u + 1, 1 - par)

            pair_up(0)
            high_x(0)
            take_terms(0, 0)
            take_rows(0, 0)
            batches(act.Fori, unit)

        @block.gpsimd
        def _(pool):
            def slope(u, par, i):
                if i == 0:
                    pool.wait_ge(termed, 3 * u + 3)
                wait_count(pool, turned, 2 * NT * u + 2 * i - 6)
                pool.sem_inc(pool_passed, 1)
                nc.gpsimd.tensor_scalar(prob[i % 4][:], d1[par][:], SLOPE, s02[par][:, i, 0:1], ALU.mult, ALU.add)\
                    .then_inc(sloped, 1)

            def norm(u, i):
                pool.wait_ge(inverted, NT * u + i + 1)
                pool.sem_inc(pool_passed, 1)
                nc.gpsimd.tensor_scalar(prob[i % 4][:], prob[i % 4][:], rowinv[:, i % 4:i % 4 + 1], 1.0,
                                        ALU.mult, ALU.mult).then_inc(normed, 1)

            def unit(u, par, prev, current, following):
                for i in range(NT):
                    if weighted and i + 2 < NT and current:
                        slope(u, par, i + 2)
                    elif weighted and i + 2 >= NT and following:
                        slope(u + 1, 1 - par, i + 2 - NT)
                    if current:
                        norm(u, i)

            if weighted:
                pool.wait_ge(adj_in, 16)
                nc.gpsimd.affine_select(out=pairs[:], in_=pairs[:], compare_op=ALU.not_equal, fill=1.0, base=0,
                                        pattern=[[P, NT], [-1, N]], channel_multiplier=1).then_inc(set_ones, 1)
                slope(0, 0, 0)
                slope(0, 0, 1)
            batches(pool.Fori, unit)


def build(nc, B, x_in, adj, L0, L1, L2, L3, out):
    with ExitStack() as ctx:
        sb = lambda n, s, d=F32: ctx.enter_context(nc.sbuf_tensor(n, s, d))
        x = sb("x", [P, B * NT, F])
        hx = sb("hx", [P, B * NT, F])
        mask = sb("mask", [P, NT, N], BF16)
        ident = sb("ident", [P, P])
        fold = sb("fold", [P, F])
        stored = nc.alloc_semaphore("stored")
        with nc.cleanup_on_exit(), ExitStack() as own:
            layer0(nc, own, B, x_in, x, hx, mask, ident, fold, adj, *L0)
        with nc.cleanup_on_exit(), ExitStack() as own:
            layer1(nc, own, B, x, hx, mask, ident, fold, *L1)
        with nc.cleanup_on_exit(), ExitStack() as own:
            edge_layer(nc, own, B, x, hx, mask, adj, ident, "l2", *L2)
        with nc.cleanup_on_exit(), ExitStack() as own:
            edge_layer(nc, own, B, x, hx, mask, adj, ident, "l3", *L3, None)
        with nc.Block() as block:
            @block.sync
            def _(sp):
                sp.dma_start(out.rearrange("b (k p) f -> p (b k) f", p=P), x[:]).then_inc(stored, 16)
                sp.wait_ge(stored, 16)


_INS = ['x', 'adj', 'L0_gnn_H', 'L0_gnn_W', 'L0_gnn_W_ind', 'L0_gnn_a_node', 'L0_gnn_a_gn', 'L0_gnn_a_ge',
        'L0_gnn_fcW', 'L0_gnn_fcb', 'L0_gnn_av', 'L1_gnn_Wh', 'L1_gnn_bh', 'L1_gnn_W_out', 'L1_gnn_b_out',
        'L2_gnn_weight', 'L2_gnn_a', 'L2_gnn_bias', 'L3_gnn_W', 'L3_gnn_a']
_OUTS = [((8, 1024, 64), 'float32')]


def kernel(**inputs):
    import numpy as _np
    import concourse.bacc as _bacc
    from concourse import mybir as _mybir
    from concourse.bass_utils import run_bass_kernel_spmd as _run

    nc = _bacc.Bacc("TRN2", target_bir_lowering=False, num_devices=1)
    arrays, args = {}, {}
    for name in _INS:
        arrays[f"in_{name}_dram"] = _np.ascontiguousarray(inputs[name])
        args[name] = nc.dram_tensor(f"in_{name}_dram", arrays[f"in_{name}_dram"].shape,
                                    _mybir.dt.from_np(arrays[f"in_{name}_dram"].dtype), kind="ExternalInput").ap()
    shape, dtype = _OUTS[0]
    out = nc.dram_tensor("out_0_dram", shape, _mybir.dt.from_np(_np.dtype(dtype)), kind="ExternalOutput").ap()
    of_layer = [[args[n] for n in _INS if n.startswith(f"L{k}_")] for k in range(4)]
    build(nc, shape[0], args["x"], args["adj"], *of_layer, out)
    r = _run(nc, [arrays], core_ids=[0])
    return r.results[0]["out_0_dram"]
```
